# Optimizing a Trainium2 kernel written in Bass

```python
import numpy as np
import jax
import jax.numpy as jnp

def _softmax(x, axis=-1):
    return jax.nn.softmax(x, axis=axis)

def _gelu(x):
    return jax.nn.gelu(x, approximate=True)

def _silu(x):
    return jax.nn.silu(x)

def _sigmoid(x):
    return jax.nn.sigmoid(x)

def _layernorm(x, axis=-1, eps=1e-05):
    m = jnp.mean(x, axis=axis, keepdims=True)
    v = jnp.var(x, axis=axis, keepdims=True)
    return (x - m) / jnp.sqrt(v + eps)

def _scatter_add(tgt, idx, src, axis=0):
    return tgt.at[idx].add(src)

def _segment_sum(src, seg, n):
    return jax.ops.segment_sum(src, seg, n)
kernel_name = 'mk_gnn_ffn_d2_gnn_r8_46d5da'

def setup_inputs(seed: int=0):
    np.random.seed(seed)
    _w = jnp.asarray

    def _rec_inputs():
        import jax
        import jax.numpy as jnp
        _gk = jax.random.key(seed)
        x = -0.0002117 + 1 * jax.random.normal(jax.random.fold_in(_gk, 1), (12500, 256), jnp.float32)
        _s = jax.random.randint(jax.random.fold_in(_gk, 2), (100000,), 0, 12500, jnp.int32)
        _d = jax.random.randint(jax.random.fold_in(_gk, 3), (100000,), 0, 12500, jnp.int32)
        _loop = jnp.arange(12500, dtype=jnp.int32)
        src = jnp.concatenate([_s, _d, _loop])
        dst = jnp.concatenate([_d, _s, _loop])
        _o = jnp.argsort(dst, stable=True)
        src = src[_o]
        dst = dst[_o]
        edge_weight = jax.random.uniform(jax.random.fold_in(_gk, 14), (212500,), jnp.float32, 0.0, 1)
        return (x, src, dst, edge_weight)
    x, src, dst, edge_weight = _rec_inputs()

    def _L0_gnn_setup():
        import jax, jax.numpy as jnp
        import numpy as np
        N = 12500
        E = 200000
        IN_FEATS = 256
        OUT_FEATS = 256
        MAXK = 32

        def _maxk(x, k):
            _, idx = jax.lax.top_k(x, k)
            rows = jnp.arange(x.shape[0])[:, None]
            mask = jnp.zeros_like(x).at[rows, idx].set(1.0)
            return x * mask
        key = jax.random.key(seed)
        k1, k2, k3, k4, k5 = jax.random.split(key, 5)
        feat = jax.random.normal(k1, (N, IN_FEATS), dtype=jnp.float32)
        W_self = jax.random.normal(k2, (IN_FEATS, OUT_FEATS), dtype=jnp.float32) * (1.0 / np.sqrt(IN_FEATS))
        W_neigh = jax.random.normal(k3, (IN_FEATS, OUT_FEATS), dtype=jnp.float32) * (1.0 / np.sqrt(IN_FEATS))
        src = jax.random.randint(k4, (E,), 0, N, dtype=jnp.int64)
        dst = jax.random.randint(k5, (E,), 0, N, dtype=jnp.int64)
        return {'feat': feat, 'W_self': W_self, 'W_neigh': W_neigh, 'src': src, 'dst': dst}
    _L0_gnn_all = _L0_gnn_setup()
    _L0_gnn_in = {k: v for k, v in _L0_gnn_all.items() if k in ('W_self', 'W_neigh')}
    del _L0_gnn_all

    def _L0_ffn_setup():
        import jax, jax.numpy as jnp
        import numpy as np
        BN_EPS = 0.001

        def _bn(h, g, b, m, v):
            return g * (h - m) * jax.lax.rsqrt(v + BN_EPS) + b
        key = jax.random.key(seed)
        ks = jax.random.split(key, 8)
        B, F, Df = (256, 64, 256)
        E, H, D = (8, 256, 256)
        s1 = 1.0 / np.sqrt(Df)
        s2 = 1.0 / np.sqrt(H)
        return {'x': jax.random.normal(ks[0], (B, F, Df), jnp.float32), 'Wr': jax.random.normal(ks[1], (Df, E), jnp.float32) * s1, 'br': jnp.zeros((E,), jnp.float32), 'W1': jax.random.normal(ks[2], (E, Df, H), jnp.float32) * s1, 'b1': jnp.zeros((E, H), jnp.float32), 'g1': jnp.ones((E, H), jnp.float32), 'be1': jnp.zeros((E, H), jnp.float32), 'm1': jnp.zeros((E, H), jnp.float32), 'v1': jnp.ones((E, H), jnp.float32), 'W2': jax.random.normal(ks[3], (E, H, H), jnp.float32) * s2, 'b2': jnp.zeros((E, H), jnp.float32), 'g2': jnp.ones((E, H), jnp.float32), 'be2': jnp.zeros((E, H), jnp.float32), 'm2': jnp.zeros((E, H), jnp.float32), 'v2': jnp.ones((E, H), jnp.float32), 'Wo': jax.random.normal(ks[4], (E, H, D), jnp.float32) * s2, 'bo': jnp.zeros((E, D), jnp.float32)}
    _L0_ffn_all = _L0_ffn_setup()
    _L0_ffn_in = {k: v for k, v in _L0_ffn_all.items() if k in ('Wr', 'br', 'W1', 'b1', 'g1', 'be1', 'm1', 'v1', 'W2', 'b2', 'g2', 'be2', 'm2', 'v2', 'Wo', 'bo')}
    del _L0_ffn_all

    def _L1_gnn_setup():
        import jax, jax.numpy as jnp
        import numpy as np
        N, E, C = (6250, 100000, 256)
        EPS = 1e-05
        key = jax.random.key(seed)
        ks = jax.random.split(key, 6)
        s = 1.0 / np.sqrt(C)
        return {'x': jax.random.normal(ks[0], (N, C), jnp.float32), 'edge_weight': jax.random.uniform(ks[1], (E,), jnp.float32), 'W_rel': jax.random.normal(ks[2], (C, C), jnp.float32) * s, 'b_rel': jnp.zeros((C,), jnp.float32), 'W_root': jax.random.normal(ks[3], (C, C), jnp.float32) * s, 'gamma': jnp.ones((C,), jnp.float32), 'beta': jnp.zeros((C,), jnp.float32), 'edge_index': jax.random.randint(ks[4], (2, E), 0, N, jnp.int32), 'batch': jnp.zeros((N,), jnp.int32)}
    _L1_gnn_all = _L1_gnn_setup()
    _L1_gnn_in = {k: v for k, v in _L1_gnn_all.items() if k in ('W_rel', 'b_rel', 'W_root', 'gamma', 'beta')}
    del _L1_gnn_all

    def _L1_ffn_setup():
        import math
        import jax, jax.numpy as jnp
        import numpy as np
        CAPACITY_FACTOR = 1.25
        key = jax.random.key(seed)
        ks = jax.random.split(key, 5)
        B, L, D, F, E = (8, 1024, 256, 1024, 8)
        h = jax.random.normal(ks[0], (B, L, D), dtype=jnp.float32)
        gate_w = jax.random.normal(ks[1], (D, E), dtype=jnp.float32) * 0.02
        gate_b = jnp.zeros((E,), dtype=jnp.float32)
        w1 = jax.random.normal(ks[2], (E, D, F), dtype=jnp.float32) * (1.0 / math.sqrt(D))
        b1 = jnp.zeros((E, F), dtype=jnp.float32)
        w2 = jax.random.normal(ks[3], (E, F, D), dtype=jnp.float32) * (1.0 / math.sqrt(F))
        b2 = jnp.zeros((E, D), dtype=jnp.float32)
        return {'h': h, 'gate_w': gate_w, 'gate_b': gate_b, 'w1': w1, 'b1': b1, 'w2': w2, 'b2': b2}
    _L1_ffn_all = _L1_ffn_setup()
    _L1_ffn_in = {k: v for k, v in _L1_ffn_all.items() if k in ('gate_w', 'gate_b', 'w1', 'b1', 'w2', 'b2')}
    del _L1_ffn_all
    return {'x': x, 'src': src, 'dst': dst, 'edge_weight': edge_weight, 'L0_gnn_W_self': _L0_gnn_in['W_self'], 'L0_gnn_W_neigh': _L0_gnn_in['W_neigh'], 'L0_ffn_Wr': _L0_ffn_in['Wr'], 'L0_ffn_br': _L0_ffn_in['br'], 'L0_ffn_W1': _L0_ffn_in['W1'], 'L0_ffn_b1': _L0_ffn_in['b1'], 'L0_ffn_g1': _L0_ffn_in['g1'], 'L0_ffn_be1': _L0_ffn_in['be1'], 'L0_ffn_m1': _L0_ffn_in['m1'], 'L0_ffn_v1': _L0_ffn_in['v1'], 'L0_ffn_W2': _L0_ffn_in['W2'], 'L0_ffn_b2': _L0_ffn_in['b2'], 'L0_ffn_g2': _L0_ffn_in['g2'], 'L0_ffn_be2': _L0_ffn_in['be2'], 'L0_ffn_m2': _L0_ffn_in['m2'], 'L0_ffn_v2': _L0_ffn_in['v2'], 'L0_ffn_Wo': _L0_ffn_in['Wo'], 'L0_ffn_bo': _L0_ffn_in['bo'], 'L1_gnn_W_rel': _L1_gnn_in['W_rel'], 'L1_gnn_b_rel': _L1_gnn_in['b_rel'], 'L1_gnn_W_root': _L1_gnn_in['W_root'], 'L1_gnn_gamma': _L1_gnn_in['gamma'], 'L1_gnn_beta': _L1_gnn_in['beta'], 'L1_ffn_gate_w': _L1_ffn_in['gate_w'], 'L1_ffn_gate_b': _L1_ffn_in['gate_b'], 'L1_ffn_w1': _L1_ffn_in['w1'], 'L1_ffn_b1': _L1_ffn_in['b1'], 'L1_ffn_w2': _L1_ffn_in['w2'], 'L1_ffn_b2': _L1_ffn_in['b2']}

def reference(x, src, dst, edge_weight, L0_gnn_W_self, L0_gnn_W_neigh, L0_ffn_Wr, L0_ffn_br, L0_ffn_W1, L0_ffn_b1, L0_ffn_g1, L0_ffn_be1, L0_ffn_m1, L0_ffn_v1, L0_ffn_W2, L0_ffn_b2, L0_ffn_g2, L0_ffn_be2, L0_ffn_m2, L0_ffn_v2, L0_ffn_Wo, L0_ffn_bo, L1_gnn_W_rel, L1_gnn_b_rel, L1_gnn_W_root, L1_gnn_gamma, L1_gnn_beta, L1_ffn_gate_w, L1_ffn_gate_b, L1_ffn_w1, L1_ffn_b1, L1_ffn_w2, L1_ffn_b2):
    import jax
    import jax.numpy as jnp

    def _L0_gnn_ref(feat, W_self, W_neigh, src, dst):
        import jax, jax.numpy as jnp
        import numpy as np
        N = 12500
        E = 200000
        IN_FEATS = 256
        OUT_FEATS = 256
        MAXK = 32

        def _maxk(x, k):
            _, idx = jax.lax.top_k(x, k)
            rows = jnp.arange(x.shape[0])[:, None]
            mask = jnp.zeros_like(x).at[rows, idx].set(1.0)
            return x * mask
        n = feat.shape[0]
        h_self = feat @ W_self
        h_neigh = feat @ W_neigh
        h_sparse = _maxk(h_neigh, MAXK)
        msg = h_sparse[src]
        summed = jax.ops.segment_sum(msg, dst, num_segments=n)
        deg = jax.ops.segment_sum(jnp.ones((src.shape[0],), dtype=feat.dtype), dst, num_segments=n)
        neigh = summed / jnp.maximum(deg, 1.0)[:, None]
        return h_self + neigh

    def _L0_ffn_ref(x, Wr, br, W1, b1, g1, be1, m1, v1, W2, b2, g2, be2, m2, v2, Wo, bo):
        import jax, jax.numpy as jnp
        import numpy as np
        BN_EPS = 0.001

        def _bn(h, g, b, m, v):
            return g * (h - m) * jax.lax.rsqrt(v + BN_EPS) + b
        feat = jnp.mean(x, axis=0)
        w = jax.nn.softmax(feat @ Wr + br, axis=-1)
        h = jnp.einsum('bfd,edh->bfeh', x, W1) + b1
        h = jax.nn.relu(_bn(h, g1, be1, m1, v1))
        h = jnp.einsum('bfeh,ehk->bfek', h, W2) + b2
        h = jax.nn.relu(_bn(h, g2, be2, m2, v2))
        y = jnp.einsum('bfeh,ehd->bfed', h, Wo) + bo
        return jnp.einsum('bfed,fe->bfd', y, w)

    def _L1_gnn_ref(x, edge_weight, W_rel, b_rel, W_root, gamma, beta, edge_index, batch):
        import jax, jax.numpy as jnp
        import numpy as np
        N, E, C = (6250, 100000, 256)
        EPS = 1e-05
        src, dst = (edge_index[0], edge_index[1])
        msg = x[src] * edge_weight[:, None]
        agg = jax.ops.segment_sum(msg, dst, num_segments=x.shape[0])
        out = agg @ W_rel.T + b_rel + x @ W_root.T
        mean = out.mean(axis=0)
        var = out.var(axis=0)
        out = (out - mean) * jax.lax.rsqrt(var + EPS) * gamma + beta
        out = jax.nn.relu(out)
        out = jax.nn.relu(out + x)
        return out

    def _L1_ffn_ref(h, gate_w, gate_b, w1, b1, w2, b2):
        import math
        import jax, jax.numpy as jnp
        import numpy as np
        CAPACITY_FACTOR = 1.25
        B, L, D = h.shape
        E = gate_w.shape[1]
        T = B * L
        C = max(1, math.ceil(CAPACITY_FACTOR * T / E))
        x = h.reshape(T, D)
        logits = x @ gate_w + gate_b
        probs = jax.nn.softmax(logits, axis=-1)
        idx = jnp.argmax(probs, axis=-1)
        prb = jnp.take_along_axis(probs, idx[:, None], axis=1)[:, 0]
        one_hot = jax.nn.one_hot(idx, E, dtype=jnp.float32)
        pos = (jnp.cumsum(one_hot, axis=0) * one_hot).sum(-1).astype(jnp.int32) - 1
        kept = pos < C
        pos_safe = jnp.where(kept, pos, C)
        buf = jnp.zeros((E, C, D), dtype=h.dtype).at[idx, pos_safe].set(x, mode='drop')
        hmid = jax.nn.relu(jnp.einsum('ecd,edf->ecf', buf, w1) + b1[:, None, :])
        ybuf = jnp.einsum('ecf,efd->ecd', hmid, w2) + b2[:, None, :]
        pos_g = jnp.minimum(pos, C - 1)
        y_tok = ybuf[idx, pos_g] * (prb * kept)[:, None]
        y = y_tok.reshape(B, L, D)
        y = jnp.nan_to_num(y, nan=0.0, posinf=10000.0, neginf=-10000.0)
        return y
    edge_index = jnp.stack([src, dst])
    batch0 = jnp.zeros((12500,), jnp.int32)
    x = x + _L0_gnn_ref(_layernorm(x, axis=-1), L0_gnn_W_self, L0_gnn_W_neigh, src, dst)
    x = x + _L0_ffn_ref(_layernorm(x, axis=-1)[None], L0_ffn_Wr, L0_ffn_br, L0_ffn_W1, L0_ffn_b1, L0_ffn_g1, L0_ffn_be1, L0_ffn_m1, L0_ffn_v1, L0_ffn_W2, L0_ffn_b2, L0_ffn_g2, L0_ffn_be2, L0_ffn_m2, L0_ffn_v2, L0_ffn_Wo, L0_ffn_bo)[0]
    x = x + _L1_gnn_ref(_layernorm(x, axis=-1), edge_weight, L1_gnn_W_rel, L1_gnn_b_rel, L1_gnn_W_root, L1_gnn_gamma, L1_gnn_beta, edge_index, batch0)
    x = x + _L1_ffn_ref(_layernorm(x, axis=-1)[None], L1_ffn_gate_w, L1_ffn_gate_b, L1_ffn_w1, L1_ffn_b1, L1_ffn_w2, L1_ffn_b2)[0]
    return x

_drawn_inputs = setup_inputs


def setup_inputs(seed=0):
    import zlib

    import numpy as np

    out = dict(_drawn_inputs(seed))
    spreads = {'L0_ffn_br': (0.0, 0.323),
     'L0_ffn_b1': (0.0, 0.414),
     'L0_ffn_g1': (1.0, 0.2),
     'L0_ffn_be1': (0.0, 0.421),
     'L0_ffn_m1': (0.0, 0.415),
     'L0_ffn_v1': (1.0, 0.6),
     'L0_ffn_b2': (0.0, 0.307),
     'L0_ffn_g2': (1.0, 0.2),
     'L0_ffn_be2': (0.0, 0.316),
     'L0_ffn_m2': (0.0, 0.303),
     'L0_ffn_v2': (1.0, 0.6),
     'L0_ffn_bo': (0.0, 0.1),
     'L1_gnn_b_rel': (0.0, 0.8),
     'L1_gnn_gamma': (1.0, 0.2),
     'L1_gnn_beta': (0.0, 0.1),
     'L1_ffn_gate_b': (0.0, 0.1),
     'L1_ffn_b1': (0.0, 0.8),
     'L1_ffn_b2': (0.0, 0.8)}
    factors = {}
    for name, (base, spread) in spreads.items():
        noise = np.random.default_rng([zlib.crc32(name.encode()), seed]).standard_normal(out[name].shape)
        drawn = base * np.exp(spread * noise) if base else spread * noise
        out[name] = jnp.asarray(drawn.astype(out[name].dtype))
    for name, factor in factors.items():
        out[name] = (out[name] * factor).astype(out[name].dtype)
    return out
```

```python
import concourse.bass as bass
from concourse import mybir
from contextlib import ExitStack

F32 = mybir.dt.float32
I32 = mybir.dt.int32
ALU = mybir.AluOpType
ACT = mybir.ActivationFunctionType
AX = mybir.AxisListType

D = 256
KD = D // 128
SUB = 125
PER = 4
GRP = SUB * PER
CH = 8
BLK = 128 * CH
WIN = 128
TOPK = 32
E0 = 8
E1 = 8
F1 = 1024
NF = F1 // 128
META = 4
TOK = 256
LN_EPS = 1e-5
BN_EPS0 = 1e-3
BN_EPS1 = 1e-5
WEIGHT_LOADS = 10 + 3 * E0 + 5
GONE = -3.0e38
FMAX = 3.4028234663852886e38
FAR = 1.0e6


class Plan:

    def __init__(self, nodes, edges):
        self.nodes = nodes
        self.groups = nodes // GRP
        self.tiles = self.groups * PER
        assert self.groups * GRP == nodes
        self.blocks = -(-edges // BLK)
        self.chunks = self.blocks * CH
        self.cap = max(1, -(-5 * nodes // (4 * E1)))
        self.slots = -(-self.cap // TOK) * TOK


class Steps:

    def __init__(self, engine, sem, count=0):
        self.engine, self.sem, self.count = engine, sem, count

    def then(self, instruction):
        instruction.then_inc(self.sem, 1)
        self.count += 1
        self.engine.wait_ge(self.sem, self.count)


def apart(engine, sem, value, started):
    if not isinstance(value, int):
        value = engine.to_reg(value)
    engine.wait_ge(started, 1)
    engine.wait_ge(sem, value)


def tile_of(view, t):
    return view[t] if isinstance(t, int) else view[bass.ds(t, 1)].rearrange("t p d -> (t p) d")


def half(buffer, g):
    return buffer[:, g % 2] if isinstance(g, int) else buffer[:, bass.ds(g % 2, 1), :, :].rearrange("p a j d -> p (a j) d")


def slot_of(buffer, g, j):
    return buffer[:, g % 2, j, :] if isinstance(g, int) else buffer[:, bass.ds(g % 2, 1), j, :].rearrange("p a d -> p (a d)")


def zero_rows(engine, rows, zeros, done):
    flat = rows.rearrange("r c -> (r c)")
    total, width = flat.shape[0], zeros.shape[1]
    per = total // 128
    whole, rest = per // width, per % width
    body = flat[0:128 * per].rearrange("(p n) -> p n", p=128)
    n = 0
    if whole:
        engine.dma_start(body[:, 0:whole * width].rearrange("p (a w) -> p a w", w=width),
                         zeros[:, :].unsqueeze(1).to_broadcast([128, whole, width])).then_inc(done, 16)
        n += 1
    if rest:
        engine.dma_start(body[:, whole * width:per], zeros[:, 0:rest]).then_inc(done, 16)
        n += 1
    if total % 128:
        engine.dma_start(flat[128 * per:total].rearrange("(a n) -> a n", a=1), zeros[0:1, 0:total % 128]).then_inc(done, 16)
        n += 1
    return n


def build(nc, A, out, nodes, edges, stop=99):
    P = Plan(nodes, edges)
    with ExitStack() as whole:
        def sem(name):
            return whole.enter_context(nc.semaphore(name))

        def dram(name, shape, dt=F32):
            return nc.dram_tensor(name, shape, dt).ap()

        S = {"started": sem("started")}
        M = {
            "kept": dram("kept_rows", (nodes, D)),
            "xs": dram("x_plus_self", (nodes, D)),
            "sum0": dram("sum0", (nodes + WIN, D + 1)),
            "x2": dram("x2", (nodes, D)),
            "xl": dram("x2_normed", (nodes, D)),
            "rel": dram("rel_rows", (nodes, D)),
            "sum1": dram("sum1", (nodes + WIN, D)),
            "buf": dram("expert_rows", (E1 * P.slots, D + META)),
        }
        with ExitStack() as edge_life:
            def keep(name, shape, dt=F32):
                return edge_life.enter_context(nc.sbuf_tensor(name, shape, dt))

            T = {
                "src": keep("src_of_edge", [128, P.chunks], I32),
                "dst": keep("dst_of_edge", [128, P.chunks]),
                "base": keep("base_of_block", [128, P.blocks]),
                "base_i": keep("base_int", [1, P.blocks], I32),
                "windows": keep("windows_int", [1, 1], I32),
                "need": keep("blocks_before_group", [1, P.groups + 1], I32),
                "begin": keep("blocks_at_step0", [1, P.groups + 1], I32),
                "middle": keep("blocks_before_catch_up", [1, P.groups + 1], I32),
                "end": keep("blocks_after_catch_up", [1, P.groups + 1], I32),
                "offset": keep("window_offset", [128, nodes // WIN + 2]),
                "iota": keep("column_number", [128, WIN]),
                "ident": keep("identity", [128, 128]),
            }
            for name in ("begin", "middle", "end"):
                T[name + "_max"] = P.blocks
            with ExitStack() as phase:
                taken = []

                def own_sem(name):
                    taken.append(phase.enter_context(nc.semaphore(name)))
                    return taken[-1]

                first_linear(nc, A, M, T, S, P, own_sem)
                with nc.Block() as block:
                    @block.gpsimd
                    def _(pool):
                        for used in taken:
                            pool.sem_clear(used)
            if stop >= 2:
                dense_layer(nc, A, M, T, S, P, sem)
            if stop >= 3:
                second_sum(nc, A, M, T, S, P, sem)
        if stop >= 4:
            route_and_experts(nc, A, M, S, P, sem, out, stop)
        else:
            dump(nc, M, out, stop, nodes, sem)
    return nc


def dump(nc, M, out, stop, nodes, sem):
    s = sem("dump")
    src = {1: M["xs"], 1.5: M["kept"], 2: M["x2"], 2.5: M["rel"], 3: M["sum1"][0:nodes, :], 2.2: M["sum0"][0:nodes, 0:D], 2.3: M["xl"]}[stop]
    with nc.Block() as block:
        @block.sync
        def _(sp):
            sp.dma_start(out, src).then_inc(s, 16)
            sp.wait_ge(s, 16)


def first_linear(nc, A, M, T, S, P, sem):
    G, NB = P.groups, P.blocks
    with ExitStack() as life:
        def sb(name, shape, dt=F32):
            return life.enter_context(nc.sbuf_tensor(name, shape, dt))

        def pb(name, shape):
            return life.enter_context(nc.psum_tensor(name, shape, F32))

        x = sb("a_x", [SUB, 2, PER, D])
        stats = sb("a_stats", [SUB, PER, 6])
        mv = sb("a_mean_var", [SUB, PER, 2])
        dev = sb("a_dev", [SUB, PER])
        rstd = sb("a_rstd", [SUB, PER])
        xn = sb("a_xn", [SUB, PER, D])
        xT = sb("a_xT", [128, PER, KD, SUB])
        h = sb("a_h", [SUB, PER, 2 * D])
        left = sb("a_left", [SUB, PER, D])
        top = sb("a_top", [SUB, PER, 8])
        kept = sb("a_kept", [SUB, PER, D])
        xs = sb("a_xs", [SUB, PER, D])
        w = sb("a_w", [128, KD, 2 * D])
        eps = sb("a_eps", [128, 1])
        zeros = sb("a_zeros", [128, 4 * (D + META)])
        dst_i = sb("a_dst_int", [128, P.chunks], I32)
        least = sb("a_least", [128, 2 * NB])
        over = sb("a_over_partitions", [128, 2 * NB])
        span = sb("a_span", [1, NB + 1])
        span_i = sb("a_span_int", [1, 2], I32)
        order = sb("a_block_number", [1, NB])
        edge_of = sb("a_group_ends", [1, G])
        before = sb("a_before", [1, G, NB])
        need = sb("a_need", [1, G + 2])
        eights = sb("a_eights", [1, G])
        after = sb("a_after", [1, G + 1])
        begin = sb("a_begin", [1, G + 1])
        tp = [pb(f"a_tp{i}", [128, 512]) for i in range(2)]
        hp = [pb(f"a_hp{i}", [128, 512]) for i in range(2)]

        x_in = [sem(f"a_x_in{j}") for j in range(PER)]
        consts_in = sem("a_consts_in")
        edges_in = sem("a_edges_in")
        x_free = sem("a_x_free")
        stats_done = sem("a_stats_done")
        mv_done = sem("a_mv_done")
        dev_done = sem("a_dev_done")
        rstd_done = sem("a_rstd_done")
        xn_done = sem("a_xn_done")
        tp_done = sem("a_tp_done")
        xT_done = sem("a_xT_done")
        hp_done = sem("a_hp_done")
        h_done = sem("a_h_done")
        top_done = sem("a_top_done")
        left_done = sem("a_left_done")
        kept_done = sem("a_kept_done")
        kept_out = [sem(f"a_kept_out{j}") for j in range(PER)]
        xs_out = [sem(f"a_xs_out{j}") for j in range(PER)]
        set_up = sem("a_set_up")
        eps_set = sem("a_eps_set")
        plan = sem("a_plan")
        reduced = sem("a_reduced")
        zeroed = sem("a_zeroed")

        x_t = A["x"].rearrange("(t p) d -> t p d", p=SUB)
        kept_t = M["kept"].rearrange("(t p) d -> t p d", p=SUB)
        xs_t = M["xs"].rearrange("(t p) d -> t p d", p=SUB)

        with nc.Block() as block:

            @block.sync
            def _(sp):
                for j in range(PER):
                    sp.dma_start(x[:, 0, j, :], x_t[j]).then_inc(x_in[j], 16)
                sp.dma_start(w[:, :, :], A["w_first"].rearrange("(k p) n -> p k n", p=128)).then_inc(consts_in, 16)
                sp.dma_start(T["src"][:, :], A["src"]).then_inc(edges_in, 16)
                sp.dma_start(dst_i[:, :], A["dst"]).then_inc(edges_in, 16)
                sp.wait_ge(set_up, 4)
                n = zero_rows(sp, M["sum0"], zeros, zeroed)
                n += zero_rows(sp, M["buf"], zeros, zeroed)
                n += zero_rows(sp, M["sum1"][P.nodes:P.nodes + WIN, :], zeros, zeroed)

                def store_xs(t, j):
                    apart(sp, x_free, t + 2 * PER + 1, S["started"])
                    sp.dma_start(tile_of(xs_t, t), xs[:, j, :]).then_inc(xs_out[j], 16)

                if G > 1:
                    with sp.Fori(1, G) as g:
                        for j in range(PER):
                            apart(sp, x_in[j], g * 16, S["started"])
                            apart(sp, x_free, g * PER + (j + 1), S["started"])
                            sp.dma_start(slot_of(x, g, j), tile_of(x_t, g * PER + j)).then_inc(x_in[j], 16)
                        for j in range(PER):
                            store_xs(g * PER + (j - PER), j)
                for j in range(PER):
                    store_xs((G - 1) * PER + j, j)
                for j in range(PER):
                    sp.wait_ge(xs_out[j], 16 * G)
                sp.wait_ge(zeroed, 16 * n)

            @block.scalar
            def _(act):
                act.sem_inc(xT_done, 2)
                act.sem_inc(h_done, 2)
                act.wait_ge(eps_set, 1)

                def store_kept(t, j):
                    act.wait_ge(kept_done, t + PER + 1)
                    act.dma_start(tile_of(kept_t, t), kept[:, j, :]).then_inc(kept_out[j], 16)

                def group(g, first):
                    act.wait_ge(mv_done, g * PER + PER)
                    nc.scalar.activation(dev[:, :], mv[:, :, 1], ACT.Sqrt, bias=eps[0:SUB, :]).then_inc(dev_done, 1)

                    def transposed(j):
                        act.wait_ge(tp_done, g * PER + (j + 1 + PER))
                        nc.scalar.activation(xT[:, j, :, :], tp[j % 2][:, 0:KD * SUB].rearrange("p (k n) -> p k n", k=KD), ACT.Copy).then_inc(xT_done, 1)

                    transposed(0)
                    for j in range(PER):
                        if j + 1 < PER:
                            transposed(j + 1)
                        if not first:
                            store_kept(g * PER + (j - PER), j)
                            act.wait_ge(x_free, g * PER + (j + 1 + PER))
                        act.wait_ge(hp_done, g * PER + (j + 1))
                        nc.scalar.activation(h[:, j, :], hp[j % 2][0:SUB, :], ACT.Copy).then_inc(h_done, 1)

                group(0, True)
                if G > 1:
                    with act.Fori(1, G) as g:
                        group(g, False)
                for j in range(PER):
                    store_kept((G - 1) * PER + j, j)
                for j in range(PER):
                    act.wait_ge(kept_out[j], 16 * G)

            @block.tensor
            def _(pe):
                pe.sem_inc(tp_done, PER)
                pe.wait_ge(consts_in, 16)
                pe.wait_ge(set_up, 4)
                with pe.Fori(0, G) as g:

                    def transpose(j):
                        pe.wait_ge(xn_done, g * PER + j + 1)
                        pe.wait_ge(xT_done, g * PER + j + 1)
                        for k in range(KD):
                            last = nc.tensor.transpose(tp[j % 2][:, k * SUB:(k + 1) * SUB], xn[:, j, k * 128:(k + 1) * 128], T["ident"][0:SUB, 0:SUB])
                        last.then_inc(tp_done, 1)

                    transpose(0)
                    for j in range(PER):
                        if j + 1 < PER:
                            transpose(j + 1)
                        pe.wait_ge(xT_done, g * PER + j + 3)
                        pe.wait_ge(h_done, g * PER + j + 1)
                        for k in range(KD):
                            last = nc.tensor.matmul(hp[j % 2][0:SUB, :], xT[:, j, k, :], w[:, k, :], start=k == 0, stop=k == KD - 1)
                        last.then_inc(hp_done, 1)

            @block.gpsimd
            def _(pool):
                pool.sem_inc(x_free, 2 * PER)
                pool.sem_inc(S["started"], 1)
                nc.gpsimd.iota(T["iota"][:, :], pattern=[[1, WIN]], base=0, channel_multiplier=0, allow_small_or_imprecise_dtypes=True).then_inc(set_up, 1)
                nc.gpsimd.memset(T["ident"][:, :], 0.0).then_inc(set_up, 1)
                nc.gpsimd.memset(zeros[:, :], 0.0).then_inc(set_up, 1)
                pool.wait_ge(set_up, 3)
                nc.gpsimd.affine_select(out=T["ident"][:, :], in_=T["ident"][:, :], compare_op=ALU.not_equal, fill=1.0,
                                        base=0, pattern=[[-1, 128]], channel_multiplier=1).then_inc(set_up, 1)
                nc.gpsimd.iota(T["offset"][:, :], pattern=[[WIN, P.nodes // WIN + 2]], base=0, channel_multiplier=0, allow_small_or_imprecise_dtypes=True)
                nc.gpsimd.iota(order[:, :], pattern=[[1, NB]], base=1, channel_multiplier=0, allow_small_or_imprecise_dtypes=True)
                nc.gpsimd.iota(edge_of[:, :], pattern=[[GRP, G]], base=GRP - 1, channel_multiplier=0, allow_small_or_imprecise_dtypes=True).then_inc(set_up, 1)
                pool.wait_ge(plan, 3)
                nc.gpsimd.partition_all_reduce(over[:, :], least[:, :], 128, bass.bass_isa.ReduceOp.max).then_inc(reduced, 1)
                with pool.Fori(0, G) as g:
                    for j in range(PER):
                        pool.wait_ge(h_done, g * PER + j + 3)
                        pool.wait_ge(xs_out[j], g * 16)
                        nc.gpsimd.tensor_tensor(xs[:, j, :], slot_of(x, g, j), h[:, j, 0:D], ALU.add).then_inc(x_free, 1)

            @block.vector
            def _(dve):
                nc.vector.memset(eps[:, :], LN_EPS).then_inc(eps_set, 1)
                dve.sem_inc(kept_done, PER)
                dve.wait_ge(edges_in, 32)
                nc.vector.tensor_copy(T["dst"][:, :], dst_i[:, :]).then_inc(plan, 1)
                dve.wait_ge(plan, 1)
                by_chunk = T["dst"][:, :].rearrange("p (b k) -> p b k", k=CH)
                nc.vector.tensor_reduce(out=least[:, 0:NB], in_=by_chunk, axis=AX.X, op=ALU.min, negate=True).then_inc(plan, 1)
                nc.vector.tensor_reduce(out=least[:, NB:2 * NB], in_=by_chunk, axis=AX.X, op=ALU.max).then_inc(plan, 1)

                def norm(g):
                    for j in range(PER):
                        apart(dve, x_in[j], g * 16 + 16, S["started"])
                        nc.vector.bn_stats(stats[:, j, :], slot_of(x, g, j)).then_inc(stats_done, 1)
                    for j in range(PER):
                        apart(dve, stats_done, g * PER + (j + 1), S["started"])
                        nc.vector.bn_aggr(mv[:, j, :], stats[:, j, :]).then_inc(mv_done, 1)
                    dve.wait_ge(dev_done, g + 1)
                    nc.vector.reciprocal(rstd[:, :], dev[:, :]).then_inc(rstd_done, 1)
                    dve.wait_ge(rstd_done, g + 1)
                    for j in range(PER):
                        dve.wait_ge(tp_done, g * PER + (j + 1))
                        nc.vector.tensor_scalar(xn[:, j, :], slot_of(x, g, j), mv[:, j, 0:1], rstd[:, j:j + 1], ALU.subtract, ALU.mult).then_inc(xn_done, 1)

                def largest(g):
                    for pair in range(PER // 2):
                        past = (g * (PER // 2) + pair) * (TOPK // 8) * 2
                        for r in range(TOPK // 8):
                            for i in range(2):
                                j = 2 * pair + i
                                if r == 0:
                                    apart(dve, h_done, g * PER + (j + 3), S["started"])
                                else:
                                    apart(dve, left_done, past + (2 * (r - 1) + i + 1), S["started"])
                                nc.vector.max(top[:, j, :], left[:, j, :] if r else h[:, j, D:2 * D]).then_inc(top_done, 1)
                            for i in range(2):
                                j = 2 * pair + i
                                apart(dve, top_done, past + (2 * r + i + 1), S["started"])
                                nc.vector.match_replace(left[:, j, :], top[:, j, :], left[:, j, :] if r else h[:, j, D:2 * D], GONE).then_inc(left_done, 1)
                        for i in range(2):
                            j = 2 * pair + i
                            dve.wait_ge(left_done, past + (2 * (TOPK // 8 - 1) + i + 1))
                            dve.wait_ge(kept_out[j], g * 16)
                            nc.vector.scalar_tensor_tensor(out=kept[:, j, :], in0=left[:, j, :], scalar=GONE, in1=h[:, j, D:2 * D],
                                                           op0=ALU.is_equal, op1=ALU.mult).then_inc(kept_done, 1)

                norm(0)
                if G > 1:
                    with dve.Fori(1, G) as g:
                        norm(g)
                        largest(g - 1)
                largest(G - 1)

                steps = Steps(dve, plan, 3)
                dve.wait_ge(reduced, 1)
                dve.wait_ge(set_up, 5)
                steps.then(nc.vector.tensor_scalar(T["base"][:, :], over[:, 0:NB], -1.0, None, ALU.mult))
                steps.then(nc.vector.tensor_copy(T["base_i"][:, :], T["base"][0:1, :]))
                steps.then(nc.vector.tensor_tensor(span[:, 0:NB], over[0:1, 0:NB], over[0:1, NB:2 * NB], ALU.add))
                steps.then(nc.vector.tensor_reduce(out=span[:, NB:NB + 1], in_=span[:, 0:NB], axis=AX.X, op=ALU.max))
                steps.then(nc.vector.tensor_copy(span_i[:, 0:1], span[:, NB:NB + 1]))
                steps.then(nc.vector.tensor_scalar(span_i[:, 1:2], span_i[:, 0:1], 7, None, ALU.arith_shift_right))
                steps.then(nc.vector.tensor_scalar(T["windows"][:, :], span_i[:, 1:2], 1.0, None, ALU.add))
                steps.then(nc.vector.tensor_tensor(before[:, :, :], edge_of[:, :].unsqueeze(2).to_broadcast([1, G, NB]),
                                                   T["base"][0:1, :].unsqueeze(1).to_broadcast([1, G, NB]), ALU.is_ge))
                steps.then(nc.vector.tensor_tensor(before[:, :, :], before[:, :, :],
                                                   order[:, :].unsqueeze(1).to_broadcast([1, G, NB]), ALU.mult))
                steps.then(nc.vector.memset(need[:, :], float(NB)))
                steps.then(nc.vector.memset(eights[:, :], float(CH)))
                steps.then(nc.vector.tensor_reduce(out=need[:, 0:G], in_=before[:, :, :], axis=AX.X, op=ALU.max))
                steps.then(nc.vector.tensor_scalar(need[:, 0:G], need[:, 0:G], 1.0, None, ALU.max))
                steps.then(nc.vector.tensor_scalar(after[:, 0:1], need[:, 0:1], 6.0, None, ALU.add))
                steps.then(nc.vector.tensor_tensor_scan(after[:, 1:G + 1], need[:, 1:G + 1], eights[:, :], after[:, 0:1], ALU.max, ALU.add))
                for table, less in (("begin", 6.0), ("end", 8.0), ("middle", 0.0)):
                    steps.then(nc.vector.tensor_scalar(begin[:, :], after[:, :], less, float(NB), ALU.subtract, ALU.min))
                    steps.then(nc.vector.tensor_copy(T[table][:, :], begin[:, :]))
                steps.then(nc.vector.tensor_copy(T["need"][:, :], need[:, 0:G + 1]))


def windows_of(engine, T, P):
    return engine.value_load(T["windows"][0:1, 0:1], min_val=1, max_val=P.nodes // WIN + 2)


def window_counter(engine, name):
    q = engine.alloc_register(name)
    engine.reg_mov(q, 0)
    return q


def column_of(tile, n, width=1):
    return tile[:, n:n + width] if isinstance(n, int) else tile[:, bass.ds(n, width)]


def edge_plan(engine, T, g):
    return [engine.value_load(column_of(T[name], at), min_val=0, max_val=T[name + "_max"])
            for name, at in (("begin", g), ("middle", g), ("end", g + 1))]


def first_blocks(engine, T, NB, sum_block):
    need = engine.value_load(T["need"][0:1, 0:1], min_val=1, max_val=NB)
    with engine.Fori(0, need) as b:
        sum_block(b)


def edges_of_step(engine, e, begin, middle, end, NB, sum_block):
    b = begin + e if e < 6 else end + (e - 6)
    with engine.If(b < NB):
        sum_block(engine.bass.s_assert_within(b, 0, NB - 1))
    if e == 5:
        with engine.If(middle < end):
            with engine.Fori(middle, end) as c:
                sum_block(c)


def gather_and_add(pool, nc, P, T, S, index, rows, win, table, sums, index_set, rows_in, rows_used, win_out, added):
    windows = windows_of(pool, T, P)

    def gather_half(b, half, q):
        pool.wait_ge(rows_used, q * CH + (half + 1) * (CH // 2))
        at = CH // 2 * half
        nc.gpsimd.tensor_copy(index[:, at:at + CH // 2], column_of(T["src"], b * CH + at, CH // 2)).then_inc(index_set, 1)
        apart(pool, index_set, b * 2 + (half + 1), S["started"])
        for j in range(at, at + CH // 2):
            nc.gpsimd.indirect_dma_start(out=rows[:, j, 0:D], out_offset=None, in_=table,
                                         in_offset=bass.IndirectOffsetOnAxis(ap=index[:, j:j + 1], axis=0)).then_inc(rows_in[j], 16)

    def add_window(b, w, q):
        base = pool.value_load(column_of(T["base_i"], b), min_val=0, max_val=P.nodes)
        row = pool.alloc_register()
        pool.reg_alu(row, pool.to_reg(base + w * WIN), P.nodes, ALU.min)
        row = pool.snap(row, donate=True, min_val=0, max_val=P.nodes)
        pool.wait_ge(win_out, q + 1)
        pool.wait_ge(added, q * 16)
        pool.dma_start(sums[bass.ds(row, WIN), :], win, accum_op=ALU.add).then_inc(added, 16)

    def last_window(b, end):
        q = pool.alloc_register()
        pool.reg_alu(q, pool.to_reg(end - 1), 0, ALU.max)
        add_window(b, windows - 1, pool.snap(q, donate=True, min_val=0))

    def earlier_windows(b, q):
        with pool.If(windows > 1):
            with pool.Fori(0, windows - 1) as w:
                add_window(b, w, q + w)

    gather_half(0, 0, 0)
    gather_half(0, 1, 0)
    earlier_windows(0, 0)
    if P.blocks > 1:
        with pool.Fori(1, P.blocks) as b:
            q = pool.snap(windows * b)
            gather_half(b, 0, q)
            last_window(b - 1, q)
            gather_half(b, 1, q)
            earlier_windows(b, q)
    q = pool.snap(windows * P.blocks)
    last_window(P.blocks - 1, q)
    pool.wait_ge(added, q * 16)


def multiply_windows(pe, nc, b, q_reg, windows, bank, sel, rows, rows_in, rows_used, sel_done, win_out):
    with pe.Fori(0, windows):
        q = pe.snap(q_reg)
        pe.wait_ge(win_out, q)
        for j in range(CH):
            pe.wait_ge(rows_in[j], b * 16 + 16)
            if j % (CH // 2) == 0:
                pe.wait_ge(sel_done, q * 2 + (j // (CH // 2) + 1))
            nc.tensor.matmul(bank, sel[:, j, :], rows[:, j, :], start=j == 0, stop=j == CH - 1).then_inc(rows_used, 1)
        pe.reg_add(q_reg, q_reg, 1)


def move_windows(act, nc, q_reg, windows, bank, win, rows_used, win_out, added):
    with act.Fori(0, windows):
        q = act.snap(q_reg)
        act.wait_ge(rows_used, q * CH + 2 * CH)
        act.wait_ge(added, q * 16)
        nc.scalar.activation(win, bank, ACT.Copy).then_inc(win_out, 1)
        act.reg_add(q_reg, q_reg, 1)


def pick_windows(dve, nc, b, q_reg, windows, T, at_base, sel, rows_used, base_set, sel_done, weight=None):
    half = CH // 2
    with dve.Fori(0, windows) as w:
        q = dve.snap(q_reg)
        dve.wait_ge(sel_done, q * 2)
        nc.vector.tensor_scalar(at_base[:, :], T["iota"][:, :], column_of(T["base"], b), column_of(T["offset"], w), ALU.add, ALU.add).then_inc(base_set, 1)
        for h in range(2):
            if h == 0:
                dve.wait_ge(base_set, q + 1)
            dve.wait_ge(rows_used, q * CH + (h + 1) * half)
            first = b * CH + h * half
            if weight is None:
                nc.vector.tensor_tensor(sel[:, h * half:(h + 1) * half, :], at_base[:, :].unsqueeze(1).to_broadcast([128, half, WIN]),
                                        column_of(T["dst"], first, half).unsqueeze(2).to_broadcast([128, half, WIN]), ALU.is_equal).then_inc(sel_done, 1)
            else:
                for j in range(half):
                    last = nc.vector.tensor_scalar(sel[:, h * half + j, :], at_base[:, :], column_of(T["dst"], first + j), column_of(weight, first + j),
                                                   ALU.is_equal, ALU.mult)
                last.then_inc(sel_done, 1)
        dve.reg_add(q_reg, q_reg, 1)


def dense_layer(nc, A, M, T, S, P, sem):
    G, NB = P.groups, P.blocks
    with ExitStack() as life:
        def sb(name, shape, dt=F32):
            return life.enter_context(nc.sbuf_tensor(name, shape, dt))

        def pb(name, shape):
            return life.enter_context(nc.psum_tensor(name, shape, F32))

        index = sb("b_index", [128, CH], I32)
        rows = sb("b_rows", [128, CH, D + 1])
        at_base = sb("b_at_base", [128, WIN])
        sel = sb("b_sel", [128, CH, WIN])
        win = sb("b_win", [128, D + 1])
        w1 = sb("b_w1", [128, E0, KD, D])
        w2 = sb("b_w2", [128, E0, KD, D])
        wo = sb("b_wo", [128, E0, KD, D])
        wr = sb("b_wr", [128, KD, E0])
        br = sb("b_br", [SUB, E0])
        bo = sb("b_bo", [E0, D])
        w_second = sb("b_w_second", [128, KD, 2 * D])
        b_rel = sb("b_b_rel", [SUB, D])
        cols = {n: {k: sb(f"b_{k}{n}", [128, E0, KD]) for k in ("b", "g", "be", "m", "v")} for n in "12"}
        shift = {n: sb(f"b_shift{n}", [128, E0, KD]) for n in "12"}
        g_rows = sb("b_g_rows", [128, E0 * D])
        v_rows = sb("b_v_rows", [128, E0 * D])
        eps0 = sb("b_eps0", [128, 1])
        eps = sb("b_eps", [128, 1])
        sums = sb("b_sums", [SUB, PER, D + 1])
        xs = sb("b_xs", [SUB, PER, D])
        deg = sb("b_deg", [SUB, 2, PER])
        acc = sb("b_acc", [SUB, 2, PER, D])
        stats = sb("b_stats", [SUB, PER, 6])
        mv = sb("b_mv", [SUB, PER, 2])
        dev = sb("b_dev", [SUB, PER])
        rstd = sb("b_rstd", [SUB, PER])
        xn = sb("b_xn", [SUB, PER, D])
        xnT = sb("b_xnT", [128, KD, GRP])
        logit = sb("b_logit", [SUB, PER, E0])
        expo = sb("b_expo", [SUB, PER, E0])
        soft = sb("b_soft", [SUB, 2, PER])
        gate = sb("b_gate", [SUB, PER, E0])
        gateT = sb("b_gateT", [E0, PER, SUB])
        h1 = sb("b_h1", [128, KD, GRP])
        h2 = sb("b_h2", [128, KD, GRP])
        l_stats = sb("b_l_stats", [SUB, PER, 6])
        l_mv = sb("b_l_mv", [SUB, PER, 2])
        l_dev = sb("b_l_dev", [SUB, PER])
        l_rstd = sb("b_l_rstd", [SUB, PER])
        xl = sb("b_xl", [SUB, PER, D])
        xlT = sb("b_xlT", [128, KD, GRP])
        pr = sb("b_pr", [SUB, 2, 2 * D])
        sum_ps = pb("b_sum_ps", [128, 512])
        h1_ps = [pb(f"b_h1_ps{i}", [128, 512]) for i in range(KD)]
        h2_ps = [pb(f"b_h2_ps{i}", [128, 512]) for i in range(KD)]
        y_ps = [pb(f"b_y_ps{i}", [128, 512]) for i in range(2)]
        mix_ps = pb("b_mix_ps", [128, 512])

        weights_in = sem("b_weights_in")
        rows_in = [sem(f"b_rows_in{j}") for j in range(CH)]
        ones_set = sem("b_ones_set")
        index_set = sem("b_index_set")
        rows_used = sem("b_rows_used")
        base_set = sem("b_base_set")
        sel_done = sem("b_sel_done")
        win_out = sem("b_win_out")
        added = sem("b_added")
        fold_in = sem("b_fold_in")
        fold = sem("b_fold")
        fold_dev = sem("b_fold_dev")
        folded = sem("b_folded")
        sums_in = sem("b_sums_in")
        deg_done = sem("b_deg_done")
        acc_done = sem("b_acc_done")
        stats_done = sem("b_stats_done")
        mv_done = sem("b_mv_done")
        dev_done = sem("b_dev_done")
        rstd_done = sem("b_rstd_done")
        xn_done = sem("b_xn_done")
        xnT_ps_done = sem("b_xnT_ps_done")
        xnT_done = sem("b_xnT_done")
        logit_ps_done = sem("b_logit_ps_done")
        gate_step = sem("b_gate_step")
        expo_done = sem("b_expo_done")
        gateT_ps_done = sem("b_gateT_ps_done")
        gateT_done = sem("b_gateT_done")
        h1_ps_done = sem("b_h1_ps_done")
        h1_done = sem("b_h1_done")
        h2_ps_done = sem("b_h2_ps_done")
        h2_done = [sem(f"b_h2_done{k}") for k in range(KD)]
        y_ps_done = sem("b_y_ps_done")
        y_done = sem("b_y_done")
        l_stats_done = sem("b_l_stats_done")
        l_mv_done = sem("b_l_mv_done")
        l_dev_done = sem("b_l_dev_done")
        l_rstd_done = sem("b_l_rstd_done")
        xl_done = sem("b_xl_done")
        xlT_ps_done = sem("b_xlT_ps_done")
        xlT_done = sem("b_xlT_done")
        pr_ps_done = sem("b_pr_ps_done")
        pr_done = sem("b_pr_done")
        x2_out = sem("b_x2_out")
        xl_out = sem("b_xl_out")
        pr_out = [sem(f"b_pr_out{i}") for i in range(2)]
        USES = E0 + 1

        def group_rows(dram, g):
            at = g * GRP
            return dram[bass.ds(at, GRP) if not isinstance(g, int) else slice(at, at + GRP), :].rearrange("(j p) d -> p j d", p=SUB)

        with nc.Block() as block:

            @block.sync
            def _(sp):
                n = 0
                for n_, name in (("1", "w1"), ("2", "w2")):
                    for k in ("b", "g", "be", "m", "v"):
                        sp.dma_start(cols[n_][k][:, :, :], A[f"{k}{n_}_columns"]).then_inc(weights_in, 16)
                        n += 1
                for tile, name in ((w1, "L0_ffn_W1"), (w2, "L0_ffn_W2"), (wo, "L0_ffn_Wo")):
                    for e in range(E0):
                        sp.dma_start(tile[:, e, :, :], A[name][e].rearrange("(k p) n -> p k n", p=128)).then_inc(weights_in, 16)
                        n += 1
                sp.dma_start(wr[:, :, :], A["L0_ffn_Wr"].rearrange("(k p) n -> p k n", p=128)).then_inc(weights_in, 16)
                sp.dma_start(w_second[:, :, :], A["w_second"].rearrange("(k p) n -> p k n", p=128)).then_inc(weights_in, 16)
                sp.dma_start(bo[:, :], A["L0_ffn_bo"]).then_inc(weights_in, 16)
                sp.dma_start(br[:, :], A["L0_ffn_br"].unsqueeze(0).to_broadcast([SUB, E0])).then_inc(weights_in, 16)
                sp.dma_start(b_rel[:, :], A["L1_gnn_b_rel"].unsqueeze(0).to_broadcast([SUB, D])).then_inc(weights_in, 16)
                assert n + 5 == WEIGHT_LOADS
                for i, n_ in enumerate("12"):
                    if i:
                        sp.wait_ge(folded, 1)
                    sp.dma_start(g_rows[:, :], A[f"g{n_}_rows"].rearrange("e d -> (e d)").unsqueeze(0).to_broadcast([128, E0 * D])).then_inc(fold_in, 16)
                    sp.dma_start(v_rows[:, :], A[f"v{n_}_rows"].rearrange("e d -> (e d)").unsqueeze(0).to_broadcast([128, E0 * D])).then_inc(fold_in, 16)
                windows = windows_of(sp, T, P)

                def load(g):
                    need = sp.value_load(T["need"][0:1, bass.ds(g, 1)] if not isinstance(g, int) else T["need"][0:1, g:g + 1], min_val=1, max_val=NB)
                    apart(sp, added, need * windows * 16, S["started"])
                    apart(sp, acc_done, g * PER + PER, S["started"])
                    sp.dma_start(sums[:, :, :], group_rows(M["sum0"], g)).then_inc(sums_in, 16)
                    sp.dma_start(xs[:, :, :], group_rows(M["xs"], g)).then_inc(sums_in, 16)

                def store_normed(g):
                    apart(sp, y_done, g * (USES * PER) + (USES * PER + PER), S["started"])
                    sp.dma_start(group_rows(M["x2"], g), half(acc, g)).then_inc(x2_out, 16)
                    apart(sp, xl_done, g * PER + PER, S["started"])
                    sp.dma_start(group_rows(M["xl"], g), xl[:, :, :]).then_inc(xl_out, 16)

                def store_products(g, j):
                    apart(sp, pr_done, g * PER + (j + 1), S["started"])
                    at = g * GRP + j * SUB
                    to = slice(at, at + SUB) if isinstance(g, int) else bass.ds(at, SUB)
                    sp.dma_start(M["rel"][to, :], pr[:, j % 2, 0:D]).then_inc(pr_out[j % 2], 16)
                    sp.dma_start(M["sum1"][to, :], pr[:, j % 2, D:2 * D]).then_inc(pr_out[j % 2], 16)

                load(0)
                load(1)
                with sp.Fori(1, G - 1) as g:
                    store_normed(g - 1)
                    store_products(g - 1, 0)
                    store_products(g - 1, 1)
                    load(g + 1)
                    store_products(g - 1, 2)
                    store_products(g - 1, 3)
                for g in (G - 2, G - 1):
                    store_normed(g)
                    for j in range(PER):
                        store_products(g, j)
                sp.wait_ge(x2_out, 16 * G)
                sp.wait_ge(xl_out, 16 * G)
                for i in range(2):
                    sp.wait_ge(pr_out[i], 64 * G)

            @block.gpsimd
            def _(pool):
                pool.sem_inc(acc_done, PER)
                pool.sem_inc(rows_used, CH)
                nc.gpsimd.memset(rows[:, :, D:D + 1], 1.0).then_inc(ones_set, 1)
                gather_and_add(pool, nc, P, T, S, index, rows, win[:, :], M["kept"], M["sum0"], index_set, rows_in, rows_used, win_out, added)

            @block.tensor
            def _(pe):
                pe.wait_ge(ones_set, 1)
                pe.wait_ge(weights_in, 16 * WEIGHT_LOADS)
                windows = windows_of(pe, T, P)
                q = window_counter(pe, "b_pe_window")

                def sum_block(b):
                    multiply_windows(pe, nc, b, q, windows, sum_ps[:, 0:D + 1], sel, rows, rows_in, rows_used, sel_done, win_out)

                def up1(g, e):
                    n = g * E0 + e
                    if e == 0:
                        pe.wait_ge(xnT_done, g * KD + KD)
                    for m in range(KD):
                        for k in range(KD):
                            last = nc.tensor.matmul(h1_ps[m][:, 0:GRP], w1[:, e, k, m * 128:(m + 1) * 128], xnT[:, k, :], start=k == 0, stop=k == KD - 1)
                        last.then_inc(h1_ps_done, 1)

                def up2(g, e):
                    n = g * E0 + e
                    pe.wait_ge(h1_done, n * KD + KD)
                    for m in range(KD):
                        for k in range(KD):
                            last = nc.tensor.matmul(h2_ps[m][:, 0:GRP], w2[:, e, k, m * 128:(m + 1) * 128], h1[:, k, :], start=k == 0, stop=k == KD - 1)
                        last.then_inc(h2_ps_done, 1)

                def down(g, e):
                    n = g * E0 + e
                    use = g * USES + (e + 1)
                    if e < 0:
                        pe.wait_ge(gateT_done, g + 1)
                    else:
                        pe.wait_ge(h2_done[0], n + 1)
                        pe.wait_ge(h2_done[1], n + 1)
                    for j in range(PER):
                        if j % 2 == 0:
                            pe.wait_ge(y_done, use * PER + (j + 2))
                        to = y_ps[j // 2][0:SUB, (j % 2) * D:(j % 2 + 1) * D]
                        if e < 0:
                            last = nc.tensor.matmul(to, gateT[:, j, :], bo[:, :], start=True, stop=True)
                        else:
                            for k in range(KD):
                                last = nc.tensor.matmul(to, h2[:, k, j * SUB:(j + 1) * SUB], wo[:, e, k, :], start=k == 0, stop=k == KD - 1)
                        if j % 2:
                            last.then_inc(y_ps_done, 1)

                def transpose_xn(g):
                    pe.wait_ge(xn_done, g * PER + PER)
                    for k in range(KD):
                        for j in range(PER):
                            last = nc.tensor.transpose(h1_ps[k][:, j * SUB:(j + 1) * SUB], xn[:, j, k * 128:(k + 1) * 128], T["ident"][0:SUB, 0:SUB])
                        last.then_inc(xnT_ps_done, 1)

                def logits(g, first):
                    pe.wait_ge(xnT_done, g * KD + KD)
                    if not first:
                        pe.wait_ge(pr_done, g * PER - PER)
                    for j in range(PER):
                        for k in range(KD):
                            last = nc.tensor.matmul(mix_ps[0:SUB, j * E0:(j + 1) * E0], xnT[:, k, j * SUB:(j + 1) * SUB], wr[:, k, :], start=k == 0, stop=k == KD - 1)
                    last.then_inc(logit_ps_done, 1)

                def transpose_gates(g):
                    pe.wait_ge(gate_step, g * 6 + 6)
                    for j in range(PER):
                        last = nc.tensor.transpose(mix_ps[0:E0, j * SUB:(j + 1) * SUB], gate[:, j, :], T["ident"][0:SUB, 0:SUB])
                    last.then_inc(gateT_ps_done, 1)

                def transpose_xl(g, k):
                    if k == 0:
                        pe.wait_ge(xl_done, g * PER + PER)
                    else:
                        pe.wait_ge(xlT_done, g * KD + 1)
                    for j in range(PER):
                        last = nc.tensor.transpose(mix_ps[:, j * SUB:(j + 1) * SUB], xl[:, j, k * 128:(k + 1) * 128], T["ident"][0:SUB, 0:SUB])
                    last.then_inc(xlT_ps_done, 1)

                def products(g, j):
                    if j == 0:
                        pe.wait_ge(xlT_done, g * KD + KD)
                    else:
                        pe.wait_ge(pr_done, g * PER + j)
                    for k in range(KD):
                        last = nc.tensor.matmul(mix_ps[0:SUB, :], xlT[:, k, j * SUB:(j + 1) * SUB], w_second[:, k, :], start=k == 0, stop=k == KD - 1)
                    last.then_inc(pr_ps_done, 1)

                def between(g, e, first):
                    if e == 0:
                        return
                    if not first:
                        if e == 2:
                            transpose_xl(g - 1, 0)
                        elif e == 3:
                            transpose_xl(g - 1, 1)
                        elif e >= 4:
                            products(g - 1, e - 4)

                def group(g, first, final):
                    begin, middle, end = edge_plan(pe, T, g)
                    for e in range(E0):
                        up1(g, e)
                        if e == 0:
                            transpose_gates(g)
                        down(g, e - 1)
                        edges_of_step(pe, e, begin, middle, end, NB, sum_block)
                        up2(g, e)
                        between(g, e, first)
                    if not final:
                        transpose_xn(g + 1)
                    down(g, E0 - 1)
                    if not final:
                        logits(g + 1, first)

                pe.sem_inc(y_done, PER)
                first_blocks(pe, T, NB, sum_block)
                pe.wait_ge(folded, 2)
                transpose_xn(0)
                logits(0, True)
                group(0, True, False)
                with pe.Fori(1, G - 1) as g:
                    group(g, False, False)
                group(G - 1, False, True)
                transpose_xl(G - 1, 0)
                transpose_xl(G - 1, 1)
                for j in range(PER):
                    products(G - 1, j)

            @block.scalar
            def _(act):
                windows = windows_of(act, T, P)
                q = window_counter(act, "b_act_window")
                act.wait_ge(fold, 2)
                act.wait_ge(weights_in, 16 * WEIGHT_LOADS)
                for i, n_ in enumerate("12"):
                    nc.scalar.activation(cols[n_]["v"][:, :, :], cols[n_]["v"][:, :, :], ACT.Sqrt, bias=eps0[:, :]).then_inc(fold_dev, 1)
                for i, n_ in enumerate("12"):
                    act.wait_ge(fold_in, 32 * (i + 1))
                    nc.scalar.activation(v_rows[:, :], v_rows[:, :], ACT.Sqrt, bias=eps0[:, :]).then_inc(fold_dev, 1)

                def sum_block(b):
                    move_windows(act, nc, q, windows, sum_ps[:, 0:D + 1], win[:, :], rows_used, win_out, added)

                def deviation(g, tail):
                    if tail:
                        act.wait_ge(l_mv_done, g * PER + PER)
                        nc.scalar.activation(l_dev[:, :], l_mv[:, :, 1], ACT.Sqrt, bias=eps[0:SUB, :]).then_inc(l_dev_done, 1)
                    else:
                        act.wait_ge(mv_done, g * PER + PER)
                        nc.scalar.activation(dev[:, :], mv[:, :, 1], ACT.Sqrt, bias=eps[0:SUB, :]).then_inc(dev_done, 1)

                def take_xnT(g):
                    for k in range(KD):
                        act.wait_ge(xnT_ps_done, g * KD + (k + 1))
                        nc.scalar.activation(xnT[:, k, :], h1_ps[k][:, 0:GRP], ACT.Copy).then_inc(xnT_done, 1)

                def exponents(g):
                    act.wait_ge(gate_step, g * 6 + 3)
                    nc.scalar.activation(expo[:, :, :], logit[:, :, :], ACT.Exp).then_inc(expo_done, 1)

                def take_gateT(g):
                    act.wait_ge(gateT_ps_done, g + 1)
                    nc.scalar.activation(gateT[:, :, :], mix_ps[0:E0, 0:GRP].rearrange("e (j p) -> e j p", j=PER), ACT.Copy).then_inc(gateT_done, 1)

                def take_h1(g, e):
                    n = g * E0 + e
                    for m in range(KD):
                        act.wait_ge(h1_ps_done, n * KD + (m + 1))
                        nc.scalar.activation(h1[:, m, :], h1_ps[m][:, 0:GRP], ACT.Relu, bias=shift["1"][:, e, m:m + 1]).then_inc(h1_done, 1)

                def take_h2(g, e):
                    n = g * E0 + e
                    act.wait_ge(h2_ps_done, n * KD + 1)
                    nc.scalar.activation(h2[:, 0, :], h2_ps[0][:, 0:GRP], ACT.Relu, bias=shift["2"][:, e, 0:1]).then_inc(h2_done[0], 1)

                def take_xlT(g, k):
                    act.wait_ge(xlT_ps_done, g * KD + (k + 1))
                    nc.scalar.activation(xlT[:, k, :], mix_ps[:, 0:GRP], ACT.Copy).then_inc(xlT_done, 1)

                def group(g, first, final):
                    begin, middle, end = edge_plan(act, T, g)
                    for e in range(E0):
                        if not first:
                            if e == 1:
                                deviation(g - 1, True)
                            elif e in (3, 4):
                                take_xlT(g - 1, e - 3)
                        take_h1(g, e)
                        if e == 0:
                            exponents(g)
                            take_gateT(g)
                        edges_of_step(act, e, begin, middle, end, NB, sum_block)
                        if e == E0 - 1 and not final:
                            deviation(g + 1, False)
                        take_h2(g, e)
                    if not final:
                        take_xnT(g + 1)

                first_blocks(act, T, NB, sum_block)
                act.wait_ge(folded, 2)
                deviation(0, False)
                take_xnT(0)
                group(0, True, False)
                with act.Fori(1, G - 1) as g:
                    group(g, False, False)
                group(G - 1, False, True)
                deviation(G - 1, True)
                take_xlT(G - 1, 0)
                take_xlT(G - 1, 1)

            @block.vector
            def _(dve):
                nc.vector.memset(eps0[:, :], BN_EPS0).then_inc(fold, 1)
                nc.vector.memset(eps[:, :], LN_EPS).then_inc(fold, 1)
                steps = Steps(dve, fold, 2)
                for i, n_ in enumerate("12"):
                    c = cols[n_]
                    dve.wait_ge(fold_dev, i + 1)
                    steps.then(nc.vector.reciprocal(c["v"][:, :, :], c["v"][:, :, :]))
                    steps.then(nc.vector.tensor_tensor(c["g"][:, :, :], c["g"][:, :, :], c["v"][:, :, :], ALU.mult))
                    steps.then(nc.vector.tensor_tensor(c["b"][:, :, :], c["b"][:, :, :], c["m"][:, :, :], ALU.subtract))
                    steps.then(nc.vector.tensor_tensor(c["b"][:, :, :], c["b"][:, :, :], c["g"][:, :, :], ALU.mult))
                    steps.then(nc.vector.tensor_tensor(shift[n_][:, :, :], c["b"][:, :, :], c["be"][:, :, :], ALU.add))
                for i, (n_, tile) in enumerate((("1", w1), ("2", w2))):
                    dve.wait_ge(fold_dev, i + 3)
                    steps.then(nc.vector.reciprocal(v_rows[:, :], v_rows[:, :]))
                    steps.then(nc.vector.tensor_tensor(g_rows[:, :], g_rows[:, :], v_rows[:, :], ALU.mult))
                    for k in range(KD):
                        last = nc.vector.tensor_tensor(tile[:, :, k, :], tile[:, :, k, :], g_rows[:, :].rearrange("p (e d) -> p e d", e=E0), ALU.mult)
                        if k < KD - 1:
                            steps.then(last)
                    last.then_inc(folded, 1)
                    dve.wait_ge(folded, i + 1)

                windows = windows_of(dve, T, P)
                q = window_counter(dve, "b_dve_window")

                def sum_block(b):
                    pick_windows(dve, nc, b, q, windows, T, at_base, sel, rows_used, base_set, sel_done)

                def add_sums(g):
                    dve.wait_ge(sums_in, g * 32 + 32)
                    nc.vector.tensor_scalar(deg[:, 0, :], sums[:, :, D], 1.0, None, ALU.max).then_inc(deg_done, 1)
                    dve.wait_ge(deg_done, g * 2 + 1)
                    nc.vector.reciprocal(deg[:, 1, :], deg[:, 0, :]).then_inc(deg_done, 1)
                    dve.wait_ge(deg_done, g * 2 + 2)
                    if not isinstance(g, int) or g > 1:
                        dve.wait_ge(x2_out, g * 16 - 16)
                    for j in range(PER):
                        nc.vector.scalar_tensor_tensor(out=slot_of(acc, g, j), in0=sums[:, j, 0:D], scalar=deg[:, 1, j:j + 1], in1=xs[:, j, :],
                                                       op0=ALU.mult, op1=ALU.add).then_inc(acc_done, 1)

                def normed(g, stats, mv, dev, rstd, stats_done, mv_done, dev_done, rstd_done, ready, ready_at, part, to, to_done):
                    if part == 0:
                        for j in range(PER):
                            apart(dve, ready, ready_at + (j + 1), S["started"])
                            nc.vector.bn_stats(stats[:, j, :], slot_of(acc, g, j)).then_inc(stats_done, 1)
                        for j in range(PER):
                            apart(dve, stats_done, g * PER + (j + 1), S["started"])
                            nc.vector.bn_aggr(mv[:, j, :], stats[:, j, :]).then_inc(mv_done, 1)
                    else:
                        dve.wait_ge(dev_done, g + 1)
                        nc.vector.reciprocal(rstd[:, :], dev[:, :]).then_inc(rstd_done, 1)
                        dve.wait_ge(rstd_done, g + 1)
                        for j in range(PER):
                            nc.vector.tensor_scalar(to[:, j, :], slot_of(acc, g, j), mv[:, j, 0:1], rstd[:, j:j + 1], ALU.subtract, ALU.mult).then_inc(to_done, 1)

                def norm_first(g, part):
                    if part and not (isinstance(g, int) and g == 0):
                        dve.wait_ge(xnT_ps_done, g * KD)
                    normed(g, stats, mv, dev, rstd, stats_done, mv_done, dev_done, rstd_done, acc_done, g * PER + PER, part, xn, xn_done)

                def norm_last(g, part):
                    if part:
                        dve.wait_ge(xl_out, g * 16)
                        dve.wait_ge(xlT_ps_done, g * KD)
                    normed(g, l_stats, l_mv, l_dev, l_rstd, l_stats_done, l_mv_done, l_dev_done, l_rstd_done, y_done, g * (USES * PER) + USES * PER, part, xl, xl_done)

                def gates(g):
                    dve.wait_ge(logit_ps_done, g + 1)
                    nc.vector.tensor_tensor(logit[:, :, :], mix_ps[0:SUB, 0:PER * E0].rearrange("p (j e) -> p j e", j=PER),
                                            br[:, :].unsqueeze(1).to_broadcast([SUB, PER, E0]), ALU.add).then_inc(gate_step, 1)
                    dve.wait_ge(gate_step, g * 6 + 1)
                    nc.vector.tensor_reduce(out=soft[:, 0, :], in_=logit[:, :, :], axis=AX.X, op=ALU.max).then_inc(gate_step, 1)
                    dve.wait_ge(gate_step, g * 6 + 2)
                    nc.vector.tensor_tensor(logit[:, :, :], logit[:, :, :], soft[:, 0, :].unsqueeze(2).to_broadcast([SUB, PER, E0]), ALU.subtract).then_inc(gate_step, 1)
                    dve.wait_ge(expo_done, g + 1)
                    nc.vector.tensor_reduce(out=soft[:, 1, :], in_=expo[:, :, :], axis=AX.X, op=ALU.add).then_inc(gate_step, 1)
                    dve.wait_ge(gate_step, g * 6 + 4)
                    nc.vector.reciprocal(soft[:, 1, :], soft[:, 1, :]).then_inc(gate_step, 1)
                    dve.wait_ge(gate_step, g * 6 + 5)
                    nc.vector.tensor_tensor(gate[:, :, :], expo[:, :, :], soft[:, 1, :].unsqueeze(2).to_broadcast([SUB, PER, E0]), ALU.mult).then_inc(gate_step, 1)

                def add_y(g, e):
                    use = g * USES + (e + 1)
                    for j in range(PER):
                        if j % 2 == 0:
                            dve.wait_ge(y_ps_done, use * 2 + (j // 2 + 1))
                        dve.wait_ge(y_done, use * PER + (j + 1))
                        part = y_ps[j // 2][0:SUB, (j % 2) * D:(j % 2 + 1) * D]
                        if e < 0:
                            nc.vector.tensor_tensor(slot_of(acc, g, j), part, slot_of(acc, g, j), ALU.add).then_inc(y_done, 1)
                        else:
                            nc.vector.scalar_tensor_tensor(out=slot_of(acc, g, j), in0=part, scalar=gate[:, j, e:e + 1], in1=slot_of(acc, g, j),
                                                           op0=ALU.mult, op1=ALU.add).then_inc(y_done, 1)

                def take_h2(g, e):
                    dve.wait_ge(h2_ps_done, (g * E0 + e) * KD + 2)
                    nc.vector.tensor_scalar(h2[:, 1, :], h2_ps[1][:, 0:GRP], shift["2"][:, e, 1:2], 0.0, ALU.add, ALU.max).then_inc(h2_done[1], 1)

                def take_products(g, j):
                    dve.wait_ge(pr_ps_done, g * PER + (j + 1))
                    dve.wait_ge(pr_out[j % 2], g * 64 + (j // 2) * 32)
                    nc.vector.tensor_copy(pr[:, j % 2, 0:D], mix_ps[0:SUB, 0:D])
                    nc.vector.tensor_tensor(pr[:, j % 2, D:2 * D], mix_ps[0:SUB, D:2 * D], b_rel[:, :], ALU.add).then_inc(pr_done, 1)

                def group(g, first, final):
                    begin, middle, end = edge_plan(dve, T, g)
                    for e in range(E0):
                        if not first and e >= 5:
                            take_products(g - 1, e - 5)
                        if e == 0:
                            gates(g)
                        edges_of_step(dve, e, begin, middle, end, NB, sum_block)
                        add_y(g, e - 1)
                        if not first and e == 0:
                            norm_last(g - 1, 0)
                        if not first and e == 1:
                            norm_last(g - 1, 1)
                        if e == E0 - 1 and not final:
                            add_sums(g + 1)
                            norm_first(g + 1, 0)
                            norm_first(g + 1, 1)
                        take_h2(g, e)
                    if not first:
                        take_products(g - 1, 3)
                    add_y(g, E0 - 1)

                first_blocks(dve, T, NB, sum_block)
                add_sums(0)
                norm_first(0, 0)
                norm_first(0, 1)
                group(0, True, False)
                with dve.Fori(1, G - 1) as g:
                    group(g, False, False)
                group(G - 1, False, True)
                norm_last(G - 1, 0)
                norm_last(G - 1, 1)
                for j in range(PER):
                    take_products(G - 1, j)



def second_sum(nc, A, M, T, S, P, sem):
    with ExitStack() as life:
        def sb(name, shape, dt=F32):
            return life.enter_context(nc.sbuf_tensor(name, shape, dt))

        weight = sb("c_weight", [128, P.chunks])
        index = sb("c_index", [128, CH], I32)
        rows = sb("c_rows", [128, CH, D])
        at_base = sb("c_at_base", [128, WIN])
        sel = sb("c_sel", [128, CH, WIN])
        win = sb("c_win", [128, D])
        sum_ps = life.enter_context(nc.psum_tensor("c_sum_ps", [128, D], F32))
        weight_in = sem("c_weight_in")
        rows_in = [sem(f"c_rows_in{j}") for j in range(CH)]
        index_set = sem("c_index_set")
        rows_used = sem("c_rows_used")
        base_set = sem("c_base_set")
        sel_done = sem("c_sel_done")
        win_out = sem("c_win_out")
        added = sem("c_added")

        with nc.Block() as block:

            @block.sync
            def _(sp):
                sp.dma_start(weight[:, :], A["edge_weight"]).then_inc(weight_in, 16)

            @block.gpsimd
            def _(pool):
                pool.sem_inc(rows_used, CH)
                gather_and_add(pool, nc, P, T, S, index, rows, win[:, :], M["rel"], M["sum1"], index_set, rows_in, rows_used, win_out, added)

            @block.tensor
            def _(pe):
                windows = windows_of(pe, T, P)
                q = window_counter(pe, "c_pe_window")
                with pe.Fori(0, P.blocks) as b:
                    multiply_windows(pe, nc, b, q, windows, sum_ps[:, :], sel, rows, rows_in, rows_used, sel_done, win_out)

            @block.scalar
            def _(act):
                windows = windows_of(act, T, P)
                q = window_counter(act, "c_act_window")
                with act.Fori(0, P.blocks):
                    move_windows(act, nc, q, windows, sum_ps[:, :], win[:, :], rows_used, win_out, added)

            @block.vector
            def _(dve):
                windows = windows_of(dve, T, P)
                q = window_counter(dve, "c_dve_window")
                dve.wait_ge(weight_in, 16)
                with dve.Fori(0, P.blocks) as b:
                    pick_windows(dve, nc, b, q, windows, T, at_base, sel, rows_used, base_set, sel_done, weight)


def route_and_experts(nc, A, M, S, P, sem, out, stop):
    with ExitStack() as life:
        def keep(name, shape, dt=F32):
            return life.enter_context(nc.sbuf_tensor(name, shape, dt))

        T = {
            "scale": keep("norm_scale", [SUB, D]),
            "shift": keep("norm_shift", [SUB, D]),
            "ident": keep("identity2", [128, 128]),
            "turns": keep("turns_of_expert", [1, E1], I32),
        }
        column_stats(nc, A, M, T, S, P, sem)
        route(nc, A, M, T, S, P, sem, out)
        if stop > 4:
            experts(nc, A, M, T, S, P, sem, out)


def column_stats(nc, A, M, T, S, P, sem):
    G = P.groups
    with ExitStack() as life:
        def sb(name, shape, dt=F32):
            return life.enter_context(nc.sbuf_tensor(name, shape, dt))

        o = sb("d_rows", [SUB, PER, D])
        stats = sb("d_stats", [128, KD, G * 6])
        mv = sb("d_mv", [128, KD, 2])
        eps = sb("d_eps", [128, 1])
        gamma = sb("d_gamma", [128, KD])
        beta = sb("d_beta", [128, KD])
        dev = sb("d_dev", [128, KD])
        both = sb("d_both", [128, 2, KD])
        diag = sb("d_diag", [128, 2, KD, 128])
        ones = sb("d_ones", [128, 128])
        t_ps = [life.enter_context(nc.psum_tensor(f"d_t_ps{k}", [128, 512], F32)) for k in range(KD)]
        b_ps = [life.enter_context(nc.psum_tensor(f"d_b_ps{k}", [128, 512], F32)) for k in range(2)]
        o_in = [sem(f"d_rows_in{j}") for j in range(PER)]
        affine_in = sem("d_affine_in")
        set_up = sem("d_set_up")
        t_done = sem("d_t_done")
        stats_done = sem("d_stats_done")
        step = sem("d_step")
        dev_done = sem("d_dev_done")
        spread = sem("d_spread")
        spread_out = sem("d_spread_out")
        o_t = M["sum1"][0:P.nodes, :].rearrange("(t p) d -> t p d", p=SUB)

        with nc.Block() as block:

            @block.sync
            def _(sp):
                sp.dma_start(gamma[:, :], A["gamma"]).then_inc(affine_in, 16)
                sp.dma_start(beta[:, :], A["beta"]).then_inc(affine_in, 16)
                for j in range(PER):
                    sp.dma_start(o[:, j, :], o_t[j]).then_inc(o_in[j], 16)
                with sp.Fori(1, G) as g:
                    apart(sp, t_done, g * KD, S["started"])
                    for j in range(PER):
                        sp.dma_start(o[:, j, :], tile_of(o_t, g * PER + j)).then_inc(o_in[j], 16)

            @block.gpsimd
            def _(pool):
                nc.gpsimd.memset(T["ident"][:, :], 0.0).then_inc(set_up, 1)
                pool.wait_ge(set_up, 1)
                nc.gpsimd.affine_select(out=T["ident"][:, :], in_=T["ident"][:, :], compare_op=ALU.not_equal, fill=1.0,
                                        base=0, pattern=[[-1, 128]], channel_multiplier=1)
                nc.gpsimd.memset(ones[:, :], 1.0)
                nc.gpsimd.memset(eps[:, :], BN_EPS1).then_inc(set_up, 1)

            @block.tensor
            def _(pe):
                pe.wait_ge(set_up, 2)
                pe.sem_inc(stats_done, KD)
                with pe.Fori(0, G) as g:
                    for k in range(KD):
                        pe.wait_ge(stats_done, g * KD + (k + 1))
                        for j in range(PER):
                            if k == 0:
                                pe.wait_ge(o_in[j], g * 16 + 16)
                            last = nc.tensor.transpose(t_ps[k][:, j * SUB:(j + 1) * SUB], o[:, j, k * 128:(k + 1) * 128], T["ident"][0:SUB, 0:SUB])
                        last.then_inc(t_done, 1)
                pe.wait_ge(step, KD + 4 + 2 * KD)
                for i in range(2):
                    for k in range(KD):
                        last = nc.tensor.matmul(b_ps[i][0:SUB, k * 128:(k + 1) * 128], ones[:, 0:SUB], diag[:, i, k, :], start=True, stop=True)
                last.then_inc(spread, 1)

            @block.scalar
            def _(act):
                act.wait_ge(step, KD)
                act.wait_ge(set_up, 2)
                nc.scalar.activation(dev[:, :], mv[:, :, 1], ACT.Sqrt, bias=eps[:, :]).then_inc(dev_done, 1)

            @block.vector
            def _(dve):
                with dve.Fori(0, G) as g:
                    for k in range(KD):
                        apart(dve, t_done, g * KD + (k + 1), S["started"])
                        nc.vector.bn_stats(stats[:, k, bass.ds(g * 6, 6)], t_ps[k][:, 0:GRP]).then_inc(stats_done, 1)
                dve.wait_ge(stats_done, G * KD + KD)
                steps = Steps(dve, step)
                for k in range(KD):
                    steps.then(nc.vector.bn_aggr(mv[:, k, :], stats[:, k, :]))
                dve.wait_ge(dev_done, 1)
                dve.wait_ge(affine_in, 32)
                steps.then(nc.vector.reciprocal(dev[:, :], dev[:, :]))
                steps.then(nc.vector.tensor_tensor(both[:, 0, :], dev[:, :], gamma[:, :], ALU.mult))
                steps.then(nc.vector.tensor_tensor(both[:, 1, :], mv[:, :, 0], both[:, 0, :], ALU.mult))
                steps.then(nc.vector.tensor_tensor(both[:, 1, :], beta[:, :], both[:, 1, :], ALU.subtract))
                dve.wait_ge(set_up, 2)
                for i in range(2):
                    for k in range(KD):
                        nc.vector.tensor_scalar(diag[:, i, k, :], T["ident"][:, :], both[:, i, k:k + 1], None, ALU.mult).then_inc(step, 1)
                dve.wait_ge(spread, 1)
                nc.vector.tensor_copy(T["scale"][:, :], b_ps[0][0:SUB, 0:D])
                nc.vector.tensor_copy(T["shift"][:, :], b_ps[1][0:SUB, 0:D]).then_inc(spread_out, 1)


def route(nc, A, M, T, S, P, sem, out):
    G = P.groups
    W = D + META
    with ExitStack() as life:
        def sb(name, shape, dt=F32):
            return life.enter_context(nc.sbuf_tensor(name, shape, dt))

        def pb(name):
            return life.enter_context(nc.psum_tensor(name, [128, 512], F32))

        o = sb("e_sum", [SUB, 2, PER, D])
        xl = sb("e_xl", [SUB, 2, PER, D])
        x2 = sb("e_x2", [SUB, 2, PER, D])
        x3 = sb("e_x3", [SUB, 2, PER, W])
        row = sb("e_row", [SUB, PER, W])
        stats = sb("e_stats", [SUB, PER, 6])
        mv = sb("e_mv", [SUB, PER, 2])
        dev = sb("e_dev", [SUB, PER])
        rstd = sb("e_rstd", [SUB, PER])
        xn = sb("e_xn", [SUB, PER, D])
        xnT = sb("e_xnT", [128, KD, GRP])
        wg = sb("e_wg", [128, KD, E1])
        bg = sb("e_bg", [SUB, E1])
        eps = sb("e_eps", [128, 1])
        rank = sb("e_rank", [SUB, PER, E1])
        token = sb("e_token", [SUB, PER])
        below = sb("e_below", [SUB, SUB])
        ones = sb("e_ones", [SUB, SUB])
        logit = sb("e_logit", [SUB, PER, E1])
        expo = sb("e_expo", [SUB, PER, E1])
        first = sb("e_first", [SUB, PER, E1])
        chosen = sb("e_chosen", [SUB, PER, E1])
        place = sb("e_place", [SUB, PER, E1])
        most = sb("e_most", [SUB, 6, PER])
        ahead = sb("e_ahead", [SUB, PER + 1, E1])
        slot = sb("e_slot", [SUB, PER], I32)
        count = sb("e_count", [1, E1])
        count_i = sb("e_count_int", [1, E1], I32)
        t_ps = [pb(f"e_t_ps{k}") for k in range(KD)]
        l_ps = pb("e_l_ps")
        p_ps = pb("e_p_ps")

        gate_in = sem("e_gate_in")
        set_up = sem("e_set_up")
        o_in = sem("e_sum_in")
        xl_in = sem("e_xl_in")
        x2_in = sem("e_x2_in")
        scaled = sem("e_scaled")
        shifted = sem("e_shifted")
        relu_done = sem("e_relu_done")
        x3_done = sem("e_x3_done")
        stats_done = sem("e_stats_done")
        mv_done = sem("e_mv_done")
        dev_done = sem("e_dev_done")
        rstd_done = sem("e_rstd_done")
        xn_done = sem("e_xn_done")
        meta_done = sem("e_meta_done")
        t_done = sem("e_t_done")
        xnT_done = sem("e_xnT_done")
        l_done = sem("e_l_done")
        expo_done = sem("e_expo_done")
        pick = sem("e_pick")
        p_done = sem("e_p_done")
        row_done = sem("e_row_done")
        out_in = sem("e_out_stored")
        sent = [sem(f"e_sent{j}") for j in range(PER)]
        PICKS = 22

        def group_rows(dram, g):
            at = g * GRP
            return dram[slice(at, at + GRP) if isinstance(g, int) else bass.ds(at, GRP), :].rearrange("(j p) d -> p j d", p=SUB)

        with nc.Block() as block:

            @block.sync
            def _(sp):
                sp.dma_start(wg[:, :, :], A["L1_ffn_gate_w"].rearrange("(k p) n -> p k n", p=128)).then_inc(gate_in, 16)
                sp.dma_start(bg[:, :], A["L1_ffn_gate_b"].unsqueeze(0).to_broadcast([SUB, E1])).then_inc(gate_in, 16)

                def load(g):
                    sp.dma_start(half(o, g), group_rows(M["sum1"], g)).then_inc(o_in, 16)
                    sp.dma_start(half(xl, g), group_rows(M["xl"], g)).then_inc(xl_in, 16)
                    sp.dma_start(half(x2, g), group_rows(M["x2"], g)).then_inc(x2_in, 16)

                def store(g):
                    apart(sp, x3_done, g + 1, S["started"])
                    apart(sp, out_in, g * 16, S["started"])
                    sp.dma_start(group_rows(out, g), half(x3, g)[:, :, 0:D]).then_inc(out_in, 16)

                load(0)
                with sp.Fori(1, G) as g:
                    for landed in (o_in, xl_in, x2_in):
                        apart(sp, landed, g * 16, S["started"])
                    load(g)
                    store(g - 1)
                store(G - 1)
                sp.wait_ge(out_in, 16 * G)

            @block.gpsimd
            def _(pool):
                nc.gpsimd.memset(ones[:, :], 1.0).then_inc(set_up, 1)
                pool.wait_ge(set_up, 1)
                nc.gpsimd.affine_select(out=below[:, :], in_=ones[:, :], compare_op=ALU.is_gt, fill=0.0,
                                        base=0, pattern=[[1, SUB]], channel_multiplier=-1)
                nc.gpsimd.iota(rank[:, :, :], pattern=[[0, PER], [-1, E1]], base=E1, channel_multiplier=0, allow_small_or_imprecise_dtypes=True)
                nc.gpsimd.iota(token[:, :], pattern=[[SUB, PER]], base=1, channel_multiplier=1, allow_small_or_imprecise_dtypes=True)
                nc.gpsimd.memset(ahead[:, :, :], 0.0)
                nc.gpsimd.memset(eps[:, :], LN_EPS).then_inc(set_up, 1)

                def scale(g):
                    pool.wait_ge(o_in, g * 16 + 16)
                    nc.gpsimd.tensor_tensor(half(o, g), half(o, g), T["scale"][:, :].unsqueeze(1).to_broadcast([SUB, PER, D]), ALU.mult).then_inc(scaled, 1)

                def send(g):
                    for j in range(PER):
                        if j == 0:
                            apart(pool, row_done, g + 1, S["started"])
                            apart(pool, pick, g * PICKS + PICKS, S["started"])
                        nc.gpsimd.indirect_dma_start(out=M["buf"], out_offset=bass.IndirectOffsetOnAxis(ap=slot[:, j:j + 1], axis=0),
                                                     in_=row[:, j, :], in_offset=None, bounds_check=E1 * P.slots - 1, oob_is_err=False).then_inc(sent[j], 16)

                scale(0)
                with pool.Fori(1, G) as g:
                    scale(g)
                    send(g - 1)
                send(G - 1)
                for j in range(PER):
                    pool.wait_ge(sent[j], 16 * G)

            @block.tensor
            def _(pe):
                pe.wait_ge(gate_in, 32)
                pe.wait_ge(set_up, 2)
                with pe.Fori(0, G) as g:
                    pe.wait_ge(xn_done, g * PER + PER)
                    pe.wait_ge(xnT_done, g * KD)
                    for k in range(KD):
                        for j in range(PER):
                            last = nc.tensor.transpose(t_ps[k][:, j * SUB:(j + 1) * SUB], xn[:, j, k * 128:(k + 1) * 128], T["ident"][0:SUB, 0:SUB])
                        last.then_inc(t_done, 1)
                    pe.wait_ge(xnT_done, g * KD + KD)
                    for j in range(PER):
                        for k in range(KD):
                            last = nc.tensor.matmul(l_ps[0:SUB, j * E1:(j + 1) * E1], xnT[:, k, j * SUB:(j + 1) * SUB], wg[:, k, :], start=k == 0, stop=k == KD - 1)
                    last.then_inc(l_done, 1)
                    pe.wait_ge(pick, g * PICKS + 6)
                    flat = chosen[:, :, :].rearrange("p j e -> p (j e)")
                    nc.tensor.matmul(p_ps[0:SUB, 0:PER * E1], below[:, :], flat, start=True, stop=True)
                    nc.tensor.matmul(p_ps[0:SUB, PER * E1:2 * PER * E1], ones[:, :], flat, start=True, stop=True).then_inc(p_done, 1)

            @block.scalar
            def _(act):
                act.wait_ge(set_up, 2)

                def front(g):
                    act.wait_ge(mv_done, g * PER + PER)
                    nc.scalar.activation(dev[:, :], mv[:, :, 1], ACT.Sqrt, bias=eps[0:SUB, :]).then_inc(dev_done, 1)
                    for k in range(KD):
                        act.wait_ge(t_done, g * KD + (k + 1))
                        nc.scalar.activation(xnT[:, k, :], t_ps[k][:, 0:GRP], ACT.Copy).then_inc(xnT_done, 1)

                def back(g):
                    act.wait_ge(pick, g * PICKS + 3)
                    nc.scalar.activation(expo[:, :, :], logit[:, :, :], ACT.Exp).then_inc(expo_done, 1)
                    act.wait_ge(pick, g * PICKS + 10)
                    for j in range(PER):
                        act.wait_ge(sent[j], g * 16)
                    nc.scalar.activation(row[:, :, :], half(x3, g), ACT.Copy).then_inc(row_done, 1)

                front(0)
                with act.Fori(1, G) as g:
                    front(g)
                    back(g - 1)
                back(G - 1)

            @block.vector
            def _(dve):
                dve.wait_ge(set_up, 2)
                dve.wait_ge(gate_in, 32)

                def front(g):
                    dve.wait_ge(scaled, g + 1)
                    nc.vector.tensor_tensor(half(o, g), half(o, g), T["shift"][:, :].unsqueeze(1).to_broadcast([SUB, PER, D]), ALU.add).then_inc(shifted, 1)
                    dve.wait_ge(shifted, g + 1)
                    dve.wait_ge(xl_in, g * 16 + 16)
                    nc.vector.scalar_tensor_tensor(out=half(xl, g), in0=half(o, g), scalar=0.0, in1=half(xl, g), op0=ALU.max, op1=ALU.add).then_inc(relu_done, 1)
                    dve.wait_ge(relu_done, g + 1)
                    dve.wait_ge(x2_in, g * 16 + 16)
                    if not isinstance(g, int) or g > 1:
                        dve.wait_ge(out_in, g * 16 - 16)
                        dve.wait_ge(row_done, g - 1)
                    nc.vector.scalar_tensor_tensor(out=half(x3, g)[:, :, 0:D], in0=half(xl, g), scalar=0.0, in1=half(x2, g), op0=ALU.max, op1=ALU.add).then_inc(x3_done, 1)
                    for j in range(PER):
                        apart(dve, x3_done, g + 1, S["started"])
                        nc.vector.bn_stats(stats[:, j, :], slot_of(x3, g, j)[:, 0:D]).then_inc(stats_done, 1)
                    for j in range(PER):
                        apart(dve, stats_done, g * PER + (j + 1), S["started"])
                        nc.vector.bn_aggr(mv[:, j, :], stats[:, j, :]).then_inc(mv_done, 1)
                    dve.wait_ge(dev_done, g + 1)
                    nc.vector.reciprocal(rstd[:, :], dev[:, :]).then_inc(rstd_done, 1)
                    dve.wait_ge(rstd_done, g + 1)
                    dve.wait_ge(t_done, g * KD)
                    for j in range(PER):
                        nc.vector.tensor_scalar(xn[:, j, :], slot_of(x3, g, j)[:, 0:D], mv[:, j, 0:1], rstd[:, j:j + 1], ALU.subtract, ALU.mult).then_inc(xn_done, 1)
                    nc.vector.tensor_copy(half(x3, g)[:, :, D], mv[:, :, 0]).then_inc(meta_done, 1)
                    nc.vector.tensor_copy(half(x3, g)[:, :, D + 1], rstd[:, :]).then_inc(meta_done, 1)

                def back(g):
                    n = 0

                    def then(instruction):
                        nonlocal n
                        instruction.then_inc(pick, 1)
                        n += 1
                        dve.wait_ge(pick, g * PICKS + n)

                    def wide(a):
                        return a.unsqueeze(2).to_broadcast([SUB, PER, E1])

                    dve.wait_ge(l_done, g + 1)
                    then(nc.vector.tensor_tensor(logit[:, :, :], l_ps[0:SUB, 0:PER * E1].rearrange("p (j e) -> p j e", j=PER),
                                                 bg[:, :].unsqueeze(1).to_broadcast([SUB, PER, E1]), ALU.add))
                    then(nc.vector.tensor_reduce(out=most[:, 0, :], in_=logit[:, :, :], axis=AX.X, op=ALU.max))
                    then(nc.vector.tensor_tensor(logit[:, :, :], logit[:, :, :], wide(most[:, 0, :]), ALU.subtract))
                    then(nc.vector.scalar_tensor_tensor(out=first[:, :, :], in0=logit[:, :, :], scalar=0.0, in1=rank[:, :, :], op0=ALU.is_equal, op1=ALU.mult))
                    then(nc.vector.tensor_reduce(out=most[:, 1, :], in_=first[:, :, :], axis=AX.X, op=ALU.max))
                    then(nc.vector.tensor_tensor(chosen[:, :, :], first[:, :, :], wide(most[:, 1, :]), ALU.is_equal))
                    dve.wait_ge(expo_done, g + 1)
                    then(nc.vector.tensor_reduce(out=most[:, 2, :], in_=expo[:, :, :], axis=AX.X, op=ALU.add))
                    dve.wait_ge(meta_done, g * 2 + 2)
                    then(nc.vector.reciprocal(half(x3, g)[:, :, D + 2], most[:, 2, :]))
                    then(nc.vector.tensor_copy(half(x3, g)[:, :, D + 3], token[:, :]))
                    then(nc.vector.tensor_scalar(token[:, :], token[:, :], float(GRP), None, ALU.add))
                    dve.wait_ge(p_done, g + 1)
                    for j in range(PER):
                        then(nc.vector.tensor_tensor(ahead[:, j + 1, :], ahead[:, j, :], p_ps[0:SUB, (PER + j) * E1:(PER + j + 1) * E1], ALU.add))
                    then(nc.vector.tensor_tensor(place[:, :, :], ahead[:, 0:PER, :], p_ps[0:SUB, 0:PER * E1].rearrange("p (j e) -> p j e", j=PER), ALU.add))
                    then(nc.vector.tensor_tensor(place[:, :, :], place[:, :, :], chosen[:, :, :], ALU.mult))
                    then(nc.vector.tensor_copy(ahead[:, 0, :], ahead[:, PER, :]))
                    then(nc.vector.tensor_reduce(out=most[:, 3, :], in_=place[:, :, :], axis=AX.X, op=ALU.add))
                    then(nc.vector.tensor_scalar(most[:, 4, :], most[:, 1, :], -float(P.slots), float(E1 * P.slots), ALU.mult, ALU.add))
                    then(nc.vector.tensor_tensor(most[:, 4, :], most[:, 4, :], most[:, 3, :], ALU.add))
                    then(nc.vector.tensor_scalar(most[:, 5, :], most[:, 3, :], float(P.cap), FAR, ALU.is_ge, ALU.mult))
                    for j in range(PER):
                        dve.wait_ge(sent[j], g * 16)
                    nc.vector.tensor_tensor(slot[:, :], most[:, 4, :], most[:, 5, :], ALU.add).then_inc(pick, 1)
                    n += 1
                    assert n == PICKS, n

                front(0)
                with dve.Fori(1, G) as g:
                    front(g)
                    back(g - 1)
                back(G - 1)
                steps = Steps(dve, pick, G * PICKS)
                dve.wait_ge(pick, G * PICKS)
                steps.then(nc.vector.tensor_scalar(count[:, :], ahead[0:1, 0, :], float(P.cap), float(TOK - 1), ALU.min, ALU.add))
                steps.then(nc.vector.tensor_scalar(count[:, :], count[:, :], float(TOK), None, ALU.max))
                steps.then(nc.vector.tensor_copy(count_i[:, :], count[:, :]))
                steps.then(nc.vector.tensor_scalar(T["turns"][:, :], count_i[:, :], TOK.bit_length() - 1, None, ALU.arith_shift_right))


def experts(nc, A, M, T, S, P, sem, out):
    W = D + META
    ST = TOK // 128
    with ExitStack() as life:
        def sb(name, shape, dt=F32):
            return life.enter_context(nc.sbuf_tensor(name, shape, dt))

        def pb(name):
            return life.enter_context(nc.psum_tensor(name, [128, 512], F32))

        rows = sb("f_rows", [128, 2, ST, W])
        xf = sb("f_xf", [128, ST, D])
        xT = sb("f_xT", [128, KD, TOK])
        hT = sb("f_hT", [128, NF, TOK])
        w1 = [sb(f"f_w1_{i}", [128, KD, F1]) for i in range(2)]
        w2 = [sb(f"f_w2_{i}", [128, NF, D]) for i in range(2)]
        b1 = [sb(f"f_b1_{i}", [128, NF]) for i in range(2)]
        b2 = [sb(f"f_b2_{i}", [128, D]) for i in range(2)]
        y = sb("f_y", [128, ST, D])
        odd = sb("f_odd", [128, 3, ST, D], I32)
        fill = sb("f_fill", [128, 3, ST, D])
        res = sb("f_res", [128, ST, D])
        none = sb("f_none", [128, 2, ST])
        token = sb("f_token", [128, ST], I32)
        x_ps = pb("f_x_ps")
        h_ps = [pb(f"f_h_ps{i}") for i in range(NF // 2)]
        y_ps = [pb(f"f_y_ps{i}") for i in range(ST)]

        set_up = sem("f_set_up")
        w_in = [sem(f"f_w_in{i}") for i in range(2)]
        rows_in = sem("f_rows_in")
        xf_done = sem("f_xf_done")
        x_ps_done = sem("f_x_ps_done")
        xT_done = sem("f_xT_done")
        h_ps_done = sem("f_h_ps_done")
        h_done = [sem(f"f_h_done{i}") for i in range(2)]
        y_ps_done = sem("f_y_ps_done")
        y_step = sem("f_y_step")
        token_done = sem("f_token_done")
        res_done = sem("f_res_done")
        sent = [sem(f"f_sent{i}") for i in range(ST)]
        STEPS = 11

        def turns_of(engine, e):
            return engine.value_load(column_of(T["turns"], e), min_val=1, max_val=P.slots // TOK)

        def each_turn(engine, name, body, at_expert=None, after_expert=None):
            q_reg = window_counter(engine, name)
            with engine.Fori(0, E1 // 2) as pair:
                for i in range(2):
                    if at_expert:
                        at_expert(pair, i)
                    turns = turns_of(engine, pair * 2 + i)
                    with engine.Fori(0, turns) as t:
                        q = engine.snap(q_reg)
                        body(pair, i, t, q)
                        engine.reg_add(q_reg, q_reg, 1)
                    if after_expert:
                        after_expert(pair, i)
            return q_reg

        with nc.Block() as block:

            @block.sync
            def _(sp):
                def load(first_slot, q):
                    apart(sp, rows_in, q * 16, S["started"])
                    apart(sp, res_done, q + 1, S["started"])
                    sp.dma_start(half(rows, q), M["buf"][bass.ds(first_slot, TOK), :].rearrange("(s p) w -> p s w", p=128)).then_inc(rows_in, 16)

                def body(pair, i, t, q):
                    load(pair * (2 * P.slots) + (t * TOK + i * P.slots), q)

                q_reg = each_turn(sp, "f_sp_turn", body)
                load(0, sp.snap(q_reg))
                apart(sp, rows_in, sp.snap(q_reg) * 16 + 16, S["started"])

            @block.gpsimd
            def _(pool):
                pool.sem_inc(res_done, 2)
                for n, value in enumerate((1.0e4, -1.0e4, 0.0)):
                    last = nc.gpsimd.memset(fill[:, n, :, :], value)
                last.then_inc(set_up, 1)

                def load(e, i):
                    def of(a):
                        return a[e] if isinstance(e, int) else a[bass.ds(e, 1)]

                    flat = "a b c -> (a b) c" if not isinstance(e, int) else "b c -> b c"
                    pool.dma_start(w1[i][:, :, :], of(A["L1_ffn_w1"]).rearrange(flat).rearrange("(k p) n -> p k n", p=128)).then_inc(w_in[i], 16)
                    pool.dma_start(w2[i][:, :, :], of(A["L1_ffn_w2"]).rearrange(flat).rearrange("(k p) n -> p k n", p=128)).then_inc(w_in[i], 16)
                    pool.dma_start(b1[i][:, :], A["expert_b1_columns"][:, e, :] if isinstance(e, int) else A["expert_b1_columns"][:, bass.ds(e, 1), :].rearrange("p a f -> p (a f)")).then_inc(w_in[i], 16)
                    pool.dma_start(b2[i][:, :], (A["L1_ffn_b2"][e:e + 1, :] if isinstance(e, int) else A["L1_ffn_b2"][bass.ds(e, 1), :]).to_broadcast([128, D])).then_inc(w_in[i], 16)

                load(0, 0)
                load(1, 1)

                def body(pair, i, t, q):
                    apart(pool, res_done, q + 3, S["started"])
                    for s in range(ST):
                        nc.gpsimd.indirect_dma_start(out=out, out_offset=bass.IndirectOffsetOnAxis(ap=token[:, s:s + 1], axis=0),
                                                     in_=res[:, s, :], in_offset=None, bounds_check=P.nodes - 1, oob_is_err=False).then_inc(sent[s], 16)

                def after_expert(pair, i):
                    with pool.If(pair < E1 // 2 - 1):
                        load(nc.s_assert_within(pair * 2 + (i + 2), 2, E1 - 1, skip_runtime_bounds_check_because="the pair is not the last"), i)

                q_reg = each_turn(pool, "f_pool_turn", body, after_expert=after_expert)
                for s in range(ST):
                    apart(pool, sent[s], pool.snap(q_reg) * 16, S["started"])

            @block.tensor
            def _(pe):
                def transpose(q):
                    pe.wait_ge(xf_done, q * ST + ST)
                    pe.wait_ge(xT_done, q)
                    for k in range(KD):
                        for s in range(ST):
                            at = k * TOK + s * 128
                            last = nc.tensor.transpose(x_ps[:, at:at + 128], xf[:, s, k * 128:(k + 1) * 128], T["ident"][:, :])
                    last.then_inc(x_ps_done, 1)

                def at_expert(pair, i):
                    pe.wait_ge(w_in[i], pair * 64 + 64)

                def body(pair, i, t, q):
                    pe.wait_ge(xT_done, q + 1)
                    for f in range(NF):
                        for k in range(KD):
                            last = nc.tensor.matmul(h_ps[f // 2][:, (f % 2) * TOK:(f % 2 + 1) * TOK], w1[i][:, k, f * 128:(f + 1) * 128], xT[:, k, :], start=k == 0, stop=k == KD - 1)
                        if f % 2:
                            last.then_inc(h_ps_done, 1)
                    transpose(q + 1)
                    for s in range(ST):
                        if s == 0:
                            pe.wait_ge(y_step, q * STEPS + 2)
                        for f in range(NF):
                            if s == 0 and f % 2 == 0:
                                pe.wait_ge(h_done[f // 2 % 2], q * 2 + (f // 4 + 1))
                            last = nc.tensor.matmul(y_ps[s][:, 0:D], hT[:, f, s * 128:(s + 1) * 128], w2[i][:, f, :], start=f == 0, stop=f == NF - 1)
                        last.then_inc(y_ps_done, 1)

                pe.sem_inc(y_step, 2)
                transpose(0)
                each_turn(pe, "f_pe_turn", body, at_expert)

            @block.scalar
            def _(act):
                def take_x(q):
                    act.wait_ge(x_ps_done, q + 1)
                    nc.scalar.activation(xT[:, :, :], x_ps[:, 0:KD * TOK].rearrange("p (k n) -> p k n", k=KD), ACT.Copy).then_inc(xT_done, 1)

                def body(pair, i, t, q):
                    for n in (0, 2):
                        act.wait_ge(h_ps_done, q * (NF // 2) + (n + 1))
                        for f in (2 * n, 2 * n + 1):
                            last = nc.scalar.activation(hT[:, f, :], h_ps[n][:, (f % 2) * TOK:(f % 2 + 1) * TOK], ACT.Relu, bias=b1[i][:, f:f + 1])
                        last.then_inc(h_done[0], 1)
                    take_x(q + 1)

                take_x(0)
                each_turn(act, "f_act_turn", body, lambda pair, i: act.wait_ge(w_in[i], pair * 64 + 64))

            @block.vector
            def _(dve):
                dve.wait_ge(set_up, 1)

                def front(q):
                    dve.wait_ge(rows_in, q * 16 + 16)
                    dve.wait_ge(x_ps_done, q)
                    for s in range(ST):
                        r = slot_of(rows, q, s)
                        nc.vector.tensor_scalar(xf[:, s, :], r[:, 0:D], r[:, D:D + 1], r[:, D + 1:D + 2], ALU.subtract, ALU.mult).then_inc(xf_done, 1)

                def body(pair, i, t, q):
                    front(q + 1)
                    for n in (1, 3):
                        dve.wait_ge(h_ps_done, q * (NF // 2) + (n + 1))
                        for f in (2 * n, 2 * n + 1):
                            last = nc.vector.tensor_scalar(hT[:, f, :], h_ps[n][:, (f % 2) * TOK:(f % 2 + 1) * TOK], b1[i][:, f:f + 1], 0.0, ALU.add, ALU.max)
                        last.then_inc(h_done[1], 1)
                    mine = half(rows, q)
                    for s in range(ST):
                        dve.wait_ge(sent[s], q * 16)
                    nc.vector.tensor_scalar(none[:, 0, :], mine[:, :, D + 3], 0.0, FAR, ALU.is_equal, ALU.mult).then_inc(token_done, 1)
                    dve.wait_ge(token_done, q * 2 + 1)
                    nc.vector.scalar_tensor_tensor(out=token[:, :], in0=mine[:, :, D + 3], scalar=-1.0, in1=none[:, 0, :], op0=ALU.add, op1=ALU.add).then_inc(token_done, 1)
                    for s in range(ST):
                        dve.wait_ge(y_ps_done, q * ST + (s + 1))
                        nc.vector.tensor_tensor(y[:, s, :], y_ps[s][:, 0:D], b2[i][:, :], ALU.add).then_inc(y_step, 1)
                    for s in range(ST):
                        dve.wait_ge(y_step, q * STEPS + (s + 3))
                        nc.vector.tensor_scalar(y[:, s, :], y[:, s, :], slot_of(rows, q, s)[:, D + 2:D + 3], None, ALU.mult).then_inc(y_step, 1)
                    dve.wait_ge(y_step, q * STEPS + 6)
                    nc.vector.tensor_scalar(odd[:, 0, :, :], y[:, :, :], FMAX, None, ALU.is_gt).then_inc(y_step, 1)
                    nc.vector.tensor_scalar(odd[:, 1, :, :], y[:, :, :], -FMAX, None, ALU.is_lt).then_inc(y_step, 1)
                    nc.vector.tensor_tensor(odd[:, 2, :, :], y[:, :, :], y[:, :, :], ALU.not_equal).then_inc(y_step, 1)
                    for n in range(3):
                        apart(dve, y_step, q * STEPS + (9 + n), S["started"])
                        nc.vector.copy_predicated(y[:, :, :], odd[:, n, :, :], fill[:, n, :, :]).then_inc(y_step, 1)
                    dve.wait_ge(y_step, q * STEPS + 12)
                    for s in range(ST):
                        last = nc.vector.tensor_tensor(res[:, s, :], y[:, s, :], slot_of(rows, q, s)[:, 0:D], ALU.add)
                        if s == 0:
                            last.then_inc(y_step, 1)
                    last.then_inc(res_done, 1)

                front(0)
                each_turn(dve, "f_dve_turn", body, lambda pair, i: dve.wait_ge(w_in[i], pair * 64 + 64))


def lay_out(inputs):
    import numpy as np

    edges, nodes = len(inputs["src"]), len(inputs["x"])
    blocks = -(-edges // BLK)

    def by_partition(a, fill):
        padded = np.full(blocks * BLK, fill, a.dtype)
        padded[0:edges] = a
        return np.ascontiguousarray(padded.reshape(blocks * CH, 128).T)

    def columns(a):
        return np.ascontiguousarray(a.reshape(a.shape[0], -1, 128).transpose(2, 0, 1))

    a = {
        "x": inputs["x"],
        "src": by_partition(inputs["src"], 0),
        "dst": by_partition(inputs["dst"], nodes),
        "edge_weight": by_partition(inputs["edge_weight"], 0.0),
        "w_first": np.concatenate([inputs["L0_gnn_W_self"], inputs["L0_gnn_W_neigh"]], axis=1),
        "w_second": np.concatenate([inputs["L1_gnn_W_rel"].T, inputs["L1_gnn_W_root"].T], axis=1),
        "gamma": columns(inputs["L1_gnn_gamma"][None])[:, 0],
        "beta": columns(inputs["L1_gnn_beta"][None])[:, 0],
        "expert_b1_columns": columns(inputs["L1_ffn_b1"]),
    }
    for name in ("L0_ffn_Wr", "L0_ffn_br", "L0_ffn_W1", "L0_ffn_W2", "L0_ffn_Wo", "L0_ffn_bo", "L1_gnn_b_rel",
                 "L1_ffn_gate_w", "L1_ffn_gate_b", "L1_ffn_w1", "L1_ffn_w2", "L1_ffn_b2"):
        a[name] = inputs[name]
    for n in "12":
        for name in ("g", "v"):
            a[f"{name}{n}_rows"] = inputs[f"L0_ffn_{name}{n}"]
        for name in ("b", "g", "be", "m", "v"):
            a[f"{name}{n}_columns"] = columns(inputs[f"L0_ffn_{name}{n}"])
    return a


def kernel(**inputs):
    import numpy as np
    import concourse.bacc as bacc
    from concourse.bass_utils import run_bass_kernel_spmd

    inputs = {k: np.asarray(v) for k, v in inputs.items()}
    nodes, edges = inputs["x"].shape[0], inputs["src"].shape[0]
    nc = bacc.Bacc("TRN2", target_bir_lowering=False, num_devices=1)
    arrays, args = {}, {}
    for name, a in lay_out(inputs).items():
        a = np.ascontiguousarray(a)
        arrays[f"in_{name}"] = a
        args[name] = nc.dram_tensor(f"in_{name}", a.shape, mybir.dt.from_np(a.dtype), kind="ExternalInput").ap()
    out = nc.dram_tensor("out", (nodes, D), F32, kind="ExternalOutput").ap()
    build(nc, args, out, nodes, edges)
    return run_bass_kernel_spmd(nc, [arrays], core_ids=[0]).results[0]["out"]
```

```python
import concourse.bass as bass
from concourse import mybir
from contextlib import ExitStack

F32 = mybir.dt.float32
F32R = mybir.dt.float32r
I32 = mybir.dt.int32
ALU = mybir.AluOpType
ACT = mybir.ActivationFunctionType
AX = mybir.AxisListType

D = 256
KD = D // 128
SUB = 125
PER = 4
GRP = SUB * PER
CH = 8
BLK = 128 * CH
WIN = 128
TOPK = 32
BEFORE = 5
E0 = 8
E1 = 8
F1 = 1024
NF = F1 // 128
META = 4
TOK = 256
LN_EPS = 1e-5
BN_EPS0 = 1e-3
BN_EPS1 = 1e-5
WEIGHT_LOADS = 10 + 5
GONE = -3.0e38
FMAX = 3.4028234663852886e38
FAR = 1.0e6


class Plan:

    def __init__(self, nodes, edges):
        self.nodes = nodes
        self.groups = nodes // GRP
        self.tiles = self.groups * PER
        assert self.groups * GRP == nodes
        self.blocks = -(-edges // BLK)
        self.chunks = self.blocks * CH
        self.cap = max(1, -(-5 * nodes // (4 * E1)))
        self.slots = -(-self.cap // TOK) * TOK


class Steps:

    def __init__(self, engine, sem, count=0):
        self.engine, self.sem, self.count = engine, sem, count

    def then(self, instruction):
        instruction.then_inc(self.sem, 1)
        self.count += 1
        self.engine.wait_ge(self.sem, self.count)


def apart(engine, sem, value, started):
    if not isinstance(value, int):
        value = engine.to_reg(value)
    engine.wait_ge(started, 1)
    engine.wait_ge(sem, value)


def tile_of(view, t):
    return view[t] if isinstance(t, int) else view[bass.ds(t, 1)].rearrange("t p d -> (t p) d")


def half(buffer, g):
    n = g % buffer.shape[1]
    return buffer[:, n] if isinstance(g, int) else buffer[:, bass.ds(n, 1), :, :].rearrange("p a j d -> p (a j) d")


def slot_of(buffer, g, j):
    n = g % buffer.shape[1]
    return buffer[:, n, j, :] if isinstance(g, int) else buffer[:, bass.ds(n, 1), j, :].rearrange("p a d -> p (a d)")


def zero_rows(engine, rows, zeros, done):
    flat = rows.rearrange("r c -> (r c)")
    total, width = flat.shape[0], zeros.shape[1]
    per = total // 128
    whole, rest = per // width, per % width
    body = flat[0:128 * per].rearrange("(p n) -> p n", p=128)
    n = 0
    if whole:
        engine.dma_start(body[:, 0:whole * width].rearrange("p (a w) -> p a w", w=width),
                         zeros[:, :].unsqueeze(1).to_broadcast([128, whole, width])).then_inc(done, 16)
        n += 1
    if rest:
        engine.dma_start(body[:, whole * width:per], zeros[:, 0:rest]).then_inc(done, 16)
        n += 1
    if total % 128:
        engine.dma_start(flat[128 * per:total].rearrange("(a n) -> a n", a=1), zeros[0:1, 0:total % 128]).then_inc(done, 16)
        n += 1
    return n


def build(nc, A, out, nodes, edges, stop=99):
    P = Plan(nodes, edges)
    with ExitStack() as whole:
        def sem(name):
            return whole.enter_context(nc.semaphore(name))

        def dram(name, shape, dt=F32):
            return nc.dram_tensor(name, shape, dt).ap()

        S = {"started": sem("started")}
        M = {
            "kept": dram("kept_rows", (nodes, D)),
            "xs": dram("x_plus_self", (nodes, D)),
            "sum0": dram("sum0", (nodes + WIN, D + 1)),
            "x2": dram("x2", (nodes, D)),
            "xl": dram("x2_normed", (nodes, D)),
            "rel": dram("rel_rows", (nodes, D)),
            "sum1": dram("sum1", (nodes + WIN, D)),
            "buf": dram("expert_rows", (E1 * P.slots, D + META)),
        }
        with ExitStack() as edge_life:
            def keep(name, shape, dt=F32):
                return edge_life.enter_context(nc.sbuf_tensor(name, shape, dt))

            T = {
                "src": keep("src_of_edge", [128, P.chunks], I32),
                "dst": keep("dst_of_edge", [128, P.chunks]),
                "base": keep("base_of_block", [128, P.blocks]),
                "base_i": keep("base_int", [1, P.blocks], I32),
                "windows": keep("windows_int", [1, 1], I32),
                "need": keep("blocks_before_group", [1, P.groups + 1], I32),
                "begin": keep("blocks_at_step0", [1, P.groups + 1], I32),
                "middle": keep("blocks_before_catch_up", [1, P.groups + 1], I32),
                "end": keep("blocks_after_catch_up", [1, P.groups + 1], I32),
                "offset": keep("window_offset", [128, nodes // WIN + 2]),
                "iota": keep("column_number", [128, WIN]),
                "ident": keep("identity", [128, 128]),
            }
            for name in ("begin", "middle", "end"):
                T[name + "_max"] = P.blocks
            W = {name: tuple(keep(f"{part}_of_{name}", [128, E0, KD, D], F32R) for part in ("first", "rest")) for name in ("W1", "W2", "Wo")}
            raw_life = ExitStack()

            def raw_matrices(name):
                return raw_life.enter_context(nc.sbuf_tensor(f"raw_{name}", [128, E0, KD, D], F32))

            raw = {"W1": raw_matrices("W1")}
            S["experts_in"] = {name: sem(f"{name}_in") for name in W}
            with ExitStack() as phase:
                taken = []

                def own_sem(name):
                    taken.append(phase.enter_context(nc.semaphore(name)))
                    return taken[-1]

                first_linear(nc, A, M, T, S, P, own_sem, raw)
                with nc.Block() as block:
                    @block.gpsimd
                    def _(pool):
                        for used in taken:
                            pool.sem_clear(used)
            for name in ("W2", "Wo"):
                raw[name] = raw_matrices(name)
            split_weights(nc, A, S, sem, W, raw)
            raw_life.close()
            if stop >= 2:
                dense_layer(nc, A, M, T, S, P, sem, W)
            if stop >= 3:
                second_sum(nc, A, M, T, S, P, sem)
        if stop >= 4:
            route_and_experts(nc, A, M, S, P, sem, out, stop)
        else:
            dump(nc, M, out, stop, nodes, sem)
    return nc


def dump(nc, M, out, stop, nodes, sem):
    s = sem("dump")
    src = {1: M["xs"], 1.5: M["kept"], 2: M["x2"], 2.5: M["rel"], 3: M["sum1"][0:nodes, :], 2.2: M["sum0"][0:nodes, 0:D], 2.3: M["xl"]}[stop]
    with nc.Block() as block:
        @block.sync
        def _(sp):
            sp.dma_start(out, src).then_inc(s, 16)
            sp.wait_ge(s, 16)


def first_linear(nc, A, M, T, S, P, sem, raw):
    G, NB = P.groups, P.blocks
    with ExitStack() as life:
        def sb(name, shape, dt=F32):
            return life.enter_context(nc.sbuf_tensor(name, shape, dt))

        def pb(name, shape):
            return life.enter_context(nc.psum_tensor(name, shape, F32))

        x = sb("a_x", [SUB, 2, PER, D])
        stats = sb("a_stats", [SUB, PER, 6])
        mv = sb("a_mean_var", [SUB, PER, 2])
        dev = sb("a_dev", [SUB, PER])
        rstd = sb("a_rstd", [SUB, PER])
        xn = sb("a_xn", [SUB, PER, D])
        xT = sb("a_xT", [128, PER, KD, SUB])
        h = sb("a_h", [SUB, PER, 2 * D])
        left = sb("a_left", [SUB, PER, D])
        top = sb("a_top", [SUB, PER, 8])
        kept = sb("a_kept", [SUB, PER, D])
        xs = sb("a_xs", [SUB, PER, D])
        w = sb("a_w", [128, KD, 2 * D])
        eps = sb("a_eps", [128, 1])
        zeros = sb("a_zeros", [128, 4 * (D + META)])
        dst_i = sb("a_dst_int", [128, P.chunks], I32)
        least = sb("a_least", [128, 2 * NB])
        over = sb("a_over_partitions", [128, 2 * NB])
        span = sb("a_span", [1, NB + 1])
        span_i = sb("a_span_int", [1, 2], I32)
        order = sb("a_block_number", [1, NB])
        edge_of = sb("a_group_ends", [1, G])
        before = sb("a_before", [1, G, NB])
        need = sb("a_need", [1, G + 2])
        eights = sb("a_eights", [1, G])
        after = sb("a_after", [1, G + 1])
        begin = sb("a_begin", [1, G + 1])
        tp = [pb(f"a_tp{i}", [128, 512]) for i in range(2)]
        hp = [pb(f"a_hp{i}", [128, 512]) for i in range(2)]

        x_in = [sem(f"a_x_in{j}") for j in range(PER)]
        consts_in = sem("a_consts_in")
        edges_in = sem("a_edges_in")
        x_free = sem("a_x_free")
        stats_done = sem("a_stats_done")
        mv_done = sem("a_mv_done")
        dev_done = sem("a_dev_done")
        rstd_done = sem("a_rstd_done")
        xn_done = sem("a_xn_done")
        tp_done = sem("a_tp_done")
        xT_done = sem("a_xT_done")
        hp_done = sem("a_hp_done")
        h_done = sem("a_h_done")
        top_done = sem("a_top_done")
        left_done = sem("a_left_done")
        kept_done = sem("a_kept_done")
        kept_out = [sem(f"a_kept_out{j}") for j in range(PER)]
        xs_out = [sem(f"a_xs_out{j}") for j in range(PER)]
        set_up = sem("a_set_up")
        eps_set = sem("a_eps_set")
        plan = sem("a_plan")
        reduced = sem("a_reduced")
        zeroed = sem("a_zeroed")

        x_t = A["x"].rearrange("(t p) d -> t p d", p=SUB)
        kept_t = M["kept"].rearrange("(t p) d -> t p d", p=SUB)
        xs_t = M["xs"].rearrange("(t p) d -> t p d", p=SUB)

        with nc.Block() as block:

            @block.sync
            def _(sp):
                for j in range(PER):
                    sp.dma_start(x[:, 0, j, :], x_t[j]).then_inc(x_in[j], 16)
                sp.dma_start(w[:, :, :], A["w_first"].rearrange("(k p) n -> p k n", p=128)).then_inc(consts_in, 16)
                sp.dma_start(T["src"][:, :], A["src"]).then_inc(edges_in, 16)
                sp.dma_start(dst_i[:, :], A["dst"]).then_inc(edges_in, 16)
                sp.wait_ge(set_up, 4)
                n = zero_rows(sp, M["sum0"], zeros, zeroed)
                n += zero_rows(sp, M["buf"], zeros, zeroed)
                n += zero_rows(sp, M["sum1"][P.nodes:P.nodes + WIN, :], zeros, zeroed)

                def store_xs(t, j):
                    apart(sp, x_free, t + 2 * PER + 1, S["started"])
                    sp.dma_start(tile_of(xs_t, t), xs[:, j, :]).then_inc(xs_out[j], 16)

                def load_and_store(first, end):
                    with sp.Fori(first, end) as g:
                        for j in range(PER):
                            apart(sp, x_in[j], g * 16, S["started"])
                            apart(sp, x_free, g * PER + (j + 1), S["started"])
                            sp.dma_start(slot_of(x, g, j), tile_of(x_t, g * PER + j)).then_inc(x_in[j], 16)
                        for j in range(PER):
                            store_xs(g * PER + (j - PER), j)

                load_and_store(1, 3)
                load_matrices(sp, A, S, "W1", raw)
                if G > 3:
                    load_and_store(3, G)
                for j in range(PER):
                    store_xs((G - 1) * PER + j, j)
                for j in range(PER):
                    sp.wait_ge(xs_out[j], 16 * G)
                sp.wait_ge(zeroed, 16 * n)

            @block.scalar
            def _(act):
                act.sem_inc(xT_done, 2)
                act.sem_inc(h_done, 2)
                act.wait_ge(eps_set, 1)

                def store_kept(t, j):
                    act.wait_ge(kept_done, t + PER + 1)
                    act.dma_start(tile_of(kept_t, t), kept[:, j, :]).then_inc(kept_out[j], 16)

                def group(g, first):
                    act.wait_ge(mv_done, g * PER + PER)
                    nc.scalar.activation(dev[:, :], mv[:, :, 1], ACT.Sqrt, bias=eps[0:SUB, :]).then_inc(dev_done, 1)

                    def transposed(j):
                        act.wait_ge(tp_done, g * PER + (j + 1 + PER))
                        nc.scalar.activation(xT[:, j, :, :], tp[j % 2][:, 0:KD * SUB].rearrange("p (k n) -> p k n", k=KD), ACT.Copy).then_inc(xT_done, 1)

                    transposed(0)
                    for j in range(PER):
                        if j + 1 < PER:
                            transposed(j + 1)
                        if not first:
                            store_kept(g * PER + (j - PER), j)
                            act.wait_ge(x_free, g * PER + (j + 1 + PER))
                        act.wait_ge(hp_done, g * PER + (j + 1))
                        nc.scalar.activation(h[:, j, :], hp[j % 2][0:SUB, :], ACT.Copy).then_inc(h_done, 1)

                group(0, True)
                if G > 1:
                    with act.Fori(1, G) as g:
                        group(g, False)
                for j in range(PER):
                    store_kept((G - 1) * PER + j, j)
                for j in range(PER):
                    act.wait_ge(kept_out[j], 16 * G)

            @block.tensor
            def _(pe):
                pe.sem_inc(tp_done, PER)
                pe.wait_ge(consts_in, 16)
                pe.wait_ge(set_up, 4)
                with pe.Fori(0, G) as g:

                    def transpose(j):
                        pe.wait_ge(xn_done, g * PER + j + 1)
                        pe.wait_ge(xT_done, g * PER + j + 1)
                        for k in range(KD):
                            last = nc.tensor.transpose(tp[j % 2][:, k * SUB:(k + 1) * SUB], xn[:, j, k * 128:(k + 1) * 128], T["ident"][0:SUB, 0:SUB])
                        last.then_inc(tp_done, 1)

                    transpose(0)
                    for j in range(PER):
                        if j + 1 < PER:
                            transpose(j + 1)
                        pe.wait_ge(xT_done, g * PER + j + 3)
                        pe.wait_ge(h_done, g * PER + j + 1)
                        for k in range(KD):
                            last = nc.tensor.matmul(hp[j % 2][0:SUB, :], xT[:, j, k, :], w[:, k, :], start=k == 0, stop=k == KD - 1)
                        last.then_inc(hp_done, 1)

            @block.gpsimd
            def _(pool):
                pool.sem_inc(x_free, 2 * PER)
                pool.sem_inc(S["started"], 1)
                nc.gpsimd.iota(T["iota"][:, :], pattern=[[1, WIN]], base=0, channel_multiplier=0, allow_small_or_imprecise_dtypes=True).then_inc(set_up, 1)
                nc.gpsimd.memset(T["ident"][:, :], 0.0).then_inc(set_up, 1)
                nc.gpsimd.memset(zeros[:, :], 0.0).then_inc(set_up, 1)
                pool.wait_ge(set_up, 3)
                nc.gpsimd.affine_select(out=T["ident"][:, :], in_=T["ident"][:, :], compare_op=ALU.not_equal, fill=1.0,
                                        base=0, pattern=[[-1, 128]], channel_multiplier=1).then_inc(set_up, 1)
                nc.gpsimd.iota(T["offset"][:, :], pattern=[[WIN, P.nodes // WIN + 2]], base=0, channel_multiplier=0, allow_small_or_imprecise_dtypes=True)
                nc.gpsimd.iota(order[:, :], pattern=[[1, NB]], base=1, channel_multiplier=0, allow_small_or_imprecise_dtypes=True)
                nc.gpsimd.iota(edge_of[:, :], pattern=[[GRP, G]], base=GRP - 1, channel_multiplier=0, allow_small_or_imprecise_dtypes=True).then_inc(set_up, 1)
                pool.wait_ge(plan, 3)
                nc.gpsimd.partition_all_reduce(over[:, :], least[:, :], 128, bass.bass_isa.ReduceOp.max).then_inc(reduced, 1)
                with pool.Fori(0, G) as g:
                    for j in range(PER):
                        pool.wait_ge(h_done, g * PER + j + 3)
                        pool.wait_ge(xs_out[j], g * 16)
                        nc.gpsimd.tensor_tensor(xs[:, j, :], slot_of(x, g, j), h[:, j, 0:D], ALU.add).then_inc(x_free, 1)

            @block.vector
            def _(dve):
                nc.vector.memset(eps[:, :], LN_EPS).then_inc(eps_set, 1)
                dve.sem_inc(kept_done, PER)
                dve.wait_ge(edges_in, 32)
                nc.vector.tensor_copy(T["dst"][:, :], dst_i[:, :]).then_inc(plan, 1)
                dve.wait_ge(plan, 1)
                by_chunk = T["dst"][:, :].rearrange("p (b k) -> p b k", k=CH)
                nc.vector.tensor_reduce(out=least[:, 0:NB], in_=by_chunk, axis=AX.X, op=ALU.min, negate=True).then_inc(plan, 1)
                nc.vector.tensor_reduce(out=least[:, NB:2 * NB], in_=by_chunk, axis=AX.X, op=ALU.max).then_inc(plan, 1)

                def norm(g):
                    for j in range(PER):
                        apart(dve, x_in[j], g * 16 + 16, S["started"])
                        nc.vector.bn_stats(stats[:, j, :], slot_of(x, g, j)).then_inc(stats_done, 1)
                    for j in range(PER):
                        apart(dve, stats_done, g * PER + (j + 1), S["started"])
                        nc.vector.bn_aggr(mv[:, j, :], stats[:, j, :]).then_inc(mv_done, 1)
                    dve.wait_ge(dev_done, g + 1)
                    nc.vector.reciprocal(rstd[:, :], dev[:, :]).then_inc(rstd_done, 1)
                    dve.wait_ge(rstd_done, g + 1)
                    for j in range(PER):
                        dve.wait_ge(tp_done, g * PER + (j + 1))
                        nc.vector.tensor_scalar(xn[:, j, :], slot_of(x, g, j), mv[:, j, 0:1], rstd[:, j:j + 1], ALU.subtract, ALU.mult).then_inc(xn_done, 1)

                def largest(g):
                    for pair in range(PER // 2):
                        past = (g * (PER // 2) + pair) * (TOPK // 8) * 2
                        for r in range(TOPK // 8):
                            for i in range(2):
                                j = 2 * pair + i
                                if r == 0:
                                    apart(dve, h_done, g * PER + (j + 3), S["started"])
                                else:
                                    apart(dve, left_done, past + (2 * (r - 1) + i + 1), S["started"])
                                nc.vector.max(top[:, j, :], left[:, j, :] if r else h[:, j, D:2 * D]).then_inc(top_done, 1)
                            for i in range(2):
                                j = 2 * pair + i
                                apart(dve, top_done, past + (2 * r + i + 1), S["started"])
                                nc.vector.match_replace(left[:, j, :], top[:, j, :], left[:, j, :] if r else h[:, j, D:2 * D], GONE).then_inc(left_done, 1)
                        for i in range(2):
                            j = 2 * pair + i
                            dve.wait_ge(left_done, past + (2 * (TOPK // 8 - 1) + i + 1))
                            dve.wait_ge(kept_out[j], g * 16)
                            nc.vector.scalar_tensor_tensor(out=kept[:, j, :], in0=left[:, j, :], scalar=GONE, in1=h[:, j, D:2 * D],
                                                           op0=ALU.is_equal, op1=ALU.mult).then_inc(kept_done, 1)

                norm(0)
                if G > 1:
                    with dve.Fori(1, G) as g:
                        norm(g)
                        largest(g - 1)
                largest(G - 1)

                steps = Steps(dve, plan, 3)
                dve.wait_ge(reduced, 1)
                dve.wait_ge(set_up, 5)
                steps.then(nc.vector.tensor_scalar(T["base"][:, :], over[:, 0:NB], -1.0, None, ALU.mult))
                steps.then(nc.vector.tensor_copy(T["base_i"][:, :], T["base"][0:1, :]))
                steps.then(nc.vector.tensor_tensor(span[:, 0:NB], over[0:1, 0:NB], over[0:1, NB:2 * NB], ALU.add))
                steps.then(nc.vector.tensor_reduce(out=span[:, NB:NB + 1], in_=span[:, 0:NB], axis=AX.X, op=ALU.max))
                steps.then(nc.vector.tensor_copy(span_i[:, 0:1], span[:, NB:NB + 1]))
                steps.then(nc.vector.tensor_scalar(span_i[:, 1:2], span_i[:, 0:1], 7, None, ALU.arith_shift_right))
                steps.then(nc.vector.tensor_scalar(T["windows"][:, :], span_i[:, 1:2], 1.0, None, ALU.add))
                steps.then(nc.vector.tensor_tensor(before[:, :, :], edge_of[:, :].unsqueeze(2).to_broadcast([1, G, NB]),
                                                   T["base"][0:1, :].unsqueeze(1).to_broadcast([1, G, NB]), ALU.is_ge))
                steps.then(nc.vector.tensor_tensor(before[:, :, :], before[:, :, :],
                                                   order[:, :].unsqueeze(1).to_broadcast([1, G, NB]), ALU.mult))
                steps.then(nc.vector.memset(need[:, :], float(NB)))
                steps.then(nc.vector.memset(eights[:, :], float(CH)))
                steps.then(nc.vector.tensor_reduce(out=need[:, 0:G], in_=before[:, :, :], axis=AX.X, op=ALU.max))
                steps.then(nc.vector.tensor_scalar(need[:, 0:G], need[:, 0:G], 1.0, None, ALU.max))
                steps.then(nc.vector.tensor_scalar(after[:, 0:1], need[:, 0:1], float(BEFORE), None, ALU.add))
                steps.then(nc.vector.tensor_tensor_scan(after[:, 1:G + 1], need[:, 1:G + 1], eights[:, :], after[:, 0:1], ALU.max, ALU.add))
                for table, less in (("begin", float(BEFORE)), ("end", float(CH)), ("middle", 0.0)):
                    steps.then(nc.vector.tensor_scalar(begin[:, :], after[:, :], less, float(NB), ALU.subtract, ALU.min))
                    steps.then(nc.vector.tensor_copy(T[table][:, :], begin[:, :]))
                steps.then(nc.vector.tensor_copy(T["need"][:, :], need[:, 0:G + 1]))


def windows_of(engine, T, P):
    return engine.value_load(T["windows"][0:1, 0:1], min_val=1, max_val=P.nodes // WIN + 2)


def window_counter(engine, name):
    q = engine.alloc_register(name)
    engine.reg_mov(q, 0)
    return q


def column_of(tile, n, width=1):
    return tile[:, n:n + width] if isinstance(n, int) else tile[:, bass.ds(n, width)]


def edge_plan(engine, T, g):
    return [engine.value_load(column_of(T[name], at), min_val=0, max_val=T[name + "_max"])
            for name, at in (("begin", g), ("middle", g), ("end", g + 1))]


def first_blocks(engine, T, NB, sum_block):
    need = engine.value_load(T["need"][0:1, 0:1], min_val=1, max_val=NB)
    with engine.Fori(0, need) as b:
        sum_block(b)


def edges_of_step(engine, e, begin, middle, end, NB, sum_block):
    b = begin + e if e < BEFORE else end + (e - BEFORE)
    with engine.If(b < NB):
        sum_block(engine.bass.s_assert_within(b, 0, NB - 1))
    if e == BEFORE - 1:
        with engine.If(middle < end):
            with engine.Fori(middle, end) as c:
                sum_block(c)


def gather_and_add(pool, nc, P, T, S, index, rows, win, table, sums, index_set, rows_in, rows_used, win_out, added):
    windows = windows_of(pool, T, P)

    def gather_half(b, parity, half, q):
        if half == 0:
            apart(pool, index_set, b + 1, S["started"])
        apart(pool, rows_used, q * CH + (half + 1) * (CH // 2), S["started"])
        for j in range(CH // 2 * half, CH // 2 * (half + 1)):
            nc.gpsimd.indirect_dma_start(out=rows[:, j, 0:D], out_offset=None, in_=table,
                                         in_offset=bass.IndirectOffsetOnAxis(ap=index[:, parity, j:j + 1], axis=0)).then_inc(rows_in[j], 16)

    def add_window(b, w, q):
        base = pool.value_load(column_of(T["base_i"], b), min_val=0, max_val=P.nodes)
        row = pool.alloc_register()
        pool.reg_alu(row, pool.to_reg(base + w * WIN), P.nodes, ALU.min)
        row = pool.snap(row, donate=True, min_val=0, max_val=P.nodes)
        pool.wait_ge(win_out, q + 1)
        pool.wait_ge(added, q * 16)
        pool.dma_start(sums[bass.ds(row, WIN), :], win, accum_op=ALU.add).then_inc(added, 16)

    def last_window(b, end):
        q = pool.alloc_register()
        pool.reg_alu(q, pool.to_reg(end - 1), 0, ALU.max)
        add_window(b, windows - 1, pool.snap(q, donate=True, min_val=0))

    def earlier_windows(b, q):
        with pool.If(windows > 1):
            with pool.Fori(0, windows - 1) as w:
                add_window(b, w, q + w)

    def block_after_first(b, parity):
        q = pool.snap(windows * b)
        gather_half(b, parity, 0, q)
        last_window(b - 1, q)
        gather_half(b, parity, 1, q)
        earlier_windows(b, q)

    gather_half(0, 0, 0, 0)
    gather_half(0, 0, 1, 0)
    earlier_windows(0, 0)
    if P.blocks > 2:
        with pool.Fori(0, (P.blocks - 1) // 2) as pair:
            block_after_first(pair * 2 + 1, 1)
            block_after_first(pair * 2 + 2, 0)
    if P.blocks % 2 == 0:
        block_after_first(P.blocks - 1, 1)
    q = pool.snap(windows * P.blocks)
    last_window(P.blocks - 1, q)
    pool.wait_ge(added, q * 16)


def multiply_windows(pe, nc, b, q_reg, windows, bank, sel, rows, rows_in, rows_used, sel_done, win_out):
    with pe.Fori(0, windows):
        q = pe.snap(q_reg)
        pe.wait_ge(win_out, q)
        for j in range(CH):
            pe.wait_ge(rows_in[j], b * 16 + 16)
            if j % (CH // 2) == 0:
                pe.wait_ge(sel_done, q * 2 + (j // (CH // 2) + 1))
            nc.tensor.matmul(bank, sel[:, j, :], rows[:, j, :], start=j == 0, stop=j == CH - 1).then_inc(rows_used, 1)
        pe.reg_add(q_reg, q_reg, 1)


def move_windows(act, nc, q_reg, windows, bank, win, rows_used, win_out, added):
    with act.Fori(0, windows):
        q = act.snap(q_reg)
        act.wait_ge(rows_used, q * CH + 2 * CH)
        act.wait_ge(added, q * 16)
        nc.scalar.activation(win, bank, ACT.Copy).then_inc(win_out, 1)
        act.reg_add(q_reg, q_reg, 1)


def first_index(nc, T, index, index_set):
    nc.vector.tensor_copy(index[:, 0, :], T["src"][:, 0:CH]).then_inc(index_set, 1)


def pick_windows(dve, nc, b, q_reg, windows, T, index, index_set, at_base, sel, rows_used, base_set, sel_done, weight=None):
    half = CH // 2
    following = dve.alloc_register()
    dve.reg_alu(following, dve.to_reg(b + 1), T["src"].shape[1] // CH - 1, ALU.min)
    following = dve.snap(following, donate=True, min_val=0, max_val=T["src"].shape[1] // CH - 1)
    dve.wait_ge(rows_used, dve.snap(q_reg) * CH + CH)
    nc.vector.tensor_copy(index[:, bass.ds((b + 1) % 2, 1), :].rearrange("p a j -> p (a j)"), column_of(T["src"], following * CH, CH)).then_inc(index_set, 1)
    with dve.Fori(0, windows) as w:
        q = dve.snap(q_reg)
        dve.wait_ge(sel_done, q * 2)
        nc.vector.tensor_scalar(at_base[:, :], T["iota"][:, :], column_of(T["base"], b), column_of(T["offset"], w), ALU.add, ALU.add).then_inc(base_set, 1)
        for h in range(2):
            if h == 0:
                dve.wait_ge(base_set, q + 1)
            dve.wait_ge(rows_used, q * CH + (h + 1) * half)
            first = b * CH + h * half
            if weight is None:
                nc.vector.tensor_tensor(sel[:, h * half:(h + 1) * half, :], at_base[:, :].unsqueeze(1).to_broadcast([128, half, WIN]),
                                        column_of(T["dst"], first, half).unsqueeze(2).to_broadcast([128, half, WIN]), ALU.is_equal).then_inc(sel_done, 1)
            else:
                for j in range(half):
                    last = nc.vector.tensor_scalar(sel[:, h * half + j, :], at_base[:, :], column_of(T["dst"], first + j), column_of(weight, first + j),
                                                   ALU.is_equal, ALU.mult)
                last.then_inc(sel_done, 1)
        dve.reg_add(q_reg, q_reg, 1)


def load_matrices(engine, A, S, name, raw):
    engine.dma_start(raw[name][:, :, :, :].rearrange("p e k n -> p (e k) n"),
                     A[f"L0_ffn_{name}"].rearrange("e (k p) n -> p (e k) n", p=128)).then_inc(S["experts_in"][name], 16)


def split_weights(nc, A, S, sem, W, raw):
    first_done = sem("w_first_done")
    rest_done = sem("w_rest_done")
    with nc.Block() as block:

        @block.sync
        def _(sp):
            for name in ("W2", "Wo"):
                load_matrices(sp, A, S, name, raw)

        @block.scalar
        def _(act):
            for name, whole in raw.items():
                act.wait_ge(S["experts_in"][name], 16)
                nc.scalar.activation(W[name][0][:, :, :, :], whole[:, :, :, :], ACT.Copy).then_inc(first_done, 1)

        @block.vector
        def _(dve):
            for n, (name, whole) in enumerate(raw.items()):
                dve.wait_ge(first_done, n + 1)
                last = nc.vector.tensor_tensor(W[name][1][:, :, :, :], whole[:, :, :, :], W[name][0][:, :, :, :], ALU.subtract)
            last.then_inc(rest_done, 1)


def dense_layer(nc, A, M, T, S, P, sem, W):
    G, NB = P.groups, P.blocks
    with ExitStack() as life:
        def sb(name, shape, dt=F32):
            return life.enter_context(nc.sbuf_tensor(name, shape, dt))

        def pb(name, shape):
            return life.enter_context(nc.psum_tensor(name, shape, F32))

        index = sb("b_index", [128, 2, CH], I32)
        rows = sb("b_rows", [128, CH, D + 1])
        at_base = sb("b_at_base", [128, WIN])
        sel = sb("b_sel", [128, CH, WIN])
        win = sb("b_win", [128, D + 1])
        w1, w2, wo = W["W1"], W["W2"], W["Wo"]
        wr = sb("b_wr", [128, KD, E0])
        br = sb("b_br", [SUB, E0])
        bo = sb("b_bo", [E0, D])
        w_second = sb("b_w_second", [128, KD, 2 * D])
        b_rel = sb("b_b_rel", [SUB, D])
        cols = {n: {k: sb(f"b_{k}{n}", [128, E0, KD]) for k in ("b", "g", "be", "m", "v")} for n in "12"}
        shift = {n: sb(f"b_shift{n}", [128, E0, KD]) for n in "12"}
        eps0 = sb("b_eps0", [128, 1])
        eps = sb("b_eps", [128, 1])
        sums = sb("b_sums", [SUB, PER, D + 1])
        xs = sb("b_xs", [SUB, PER, D])
        deg = sb("b_deg", [SUB, 2, PER])
        acc = sb("b_acc", [SUB, 2, PER, D])
        stats = sb("b_stats", [SUB, PER, 6])
        mv = sb("b_mv", [SUB, PER, 2])
        dev = sb("b_dev", [SUB, PER])
        rstd = sb("b_rstd", [SUB, PER])
        xn = sb("b_xn", [SUB, PER, D])
        xnT = sb("b_xnT", [128, KD, GRP])
        logit = sb("b_logit", [SUB, PER, E0])
        expo = sb("b_expo", [SUB, PER, E0])
        soft = sb("b_soft", [SUB, 2, PER])
        gate = sb("b_gate", [SUB, PER, E0])
        gateT = sb("b_gateT", [E0, PER, SUB])
        x_parts = [sb(f"b_x_part{i}", [128, KD, GRP], F32R) for i in range(2)]
        h_full = [sb(f"b_h{i + 1}_full", [128, KD, GRP]) for i in range(2)]
        h1 = [sb(f"b_h1_part{i}", [128, KD, GRP], F32R) for i in range(2)]
        h2 = [sb(f"b_h2_part{i}", [128, KD, GRP + 128 - SUB + 1], F32R) for i in range(2)]
        behind = sb("b_zeros_behind", [128, KD, 128 - SUB + 1])
        l_stats = sb("b_l_stats", [SUB, PER, 6])
        l_mv = sb("b_l_mv", [SUB, PER, 2])
        l_dev = sb("b_l_dev", [SUB, PER])
        l_rstd = sb("b_l_rstd", [SUB, PER])
        xl = sb("b_xl", [SUB, PER, D])
        xlT = sb("b_xlT", [128, KD, GRP])
        pr = sb("b_pr", [SUB, 2, 2 * D])
        sum_ps = pb("b_sum_ps", [128, 512])
        h1_ps = [pb(f"b_h1_ps{i}", [128, 512]) for i in range(KD)]
        h2_ps = [pb(f"b_h2_ps{i}", [128, 512]) for i in range(KD)]
        y_ps = [pb(f"b_y_ps{i}", [128, 512]) for i in range(2)]
        mix_ps = pb("b_mix_ps", [128, 512])

        weights_in = sem("b_weights_in")
        rows_in = [sem(f"b_rows_in{j}") for j in range(CH)]
        ones_set = sem("b_ones_set")
        index_set = sem("b_index_set")
        rows_used = sem("b_rows_used")
        base_set = sem("b_base_set")
        sel_done = sem("b_sel_done")
        win_out = sem("b_win_out")
        added = sem("b_added")
        fold = sem("b_fold")
        fold_dev = sem("b_fold_dev")
        behind_set = sem("b_behind_set")
        x_rest_done = sem("b_x_rest_done")
        sums_in = sem("b_sums_in")
        deg_done = sem("b_deg_done")
        acc_done = sem("b_acc_done")
        stats_done = sem("b_stats_done")
        mv_done = sem("b_mv_done")
        dev_done = sem("b_dev_done")
        rstd_done = sem("b_rstd_done")
        xn_done = sem("b_xn_done")
        xnT_ps_done = sem("b_xnT_ps_done")
        xnT_done = sem("b_xnT_done")
        logit_ps_done = sem("b_logit_ps_done")
        gate_step = sem("b_gate_step")
        expo_done = sem("b_expo_done")
        gateT_ps_done = sem("b_gateT_ps_done")
        gateT_done = sem("b_gateT_done")
        h1_ps_done = sem("b_h1_ps_done")
        h_done = sem("b_h_done")
        rest_done = sem("b_rest_done")
        h2_ps_done = sem("b_h2_ps_done")
        y_ps_done = sem("b_y_ps_done")
        y_done = sem("b_y_done")
        l_stats_done = sem("b_l_stats_done")
        l_mv_done = sem("b_l_mv_done")
        l_dev_done = sem("b_l_dev_done")
        l_rstd_done = sem("b_l_rstd_done")
        xl_done = sem("b_xl_done")
        xlT_ps_done = sem("b_xlT_ps_done")
        xlT_done = sem("b_xlT_done")
        pr_ps_done = sem("b_pr_ps_done")
        pr_done = sem("b_pr_done")
        x2_out = sem("b_x2_out")
        xl_out = sem("b_xl_out")
        pr_out = [sem(f"b_pr_out{i}") for i in range(2)]
        USES = E0 + 1

        def group_rows(dram, g):
            at = g * GRP
            return dram[bass.ds(at, GRP) if not isinstance(g, int) else slice(at, at + GRP), :].rearrange("(j p) d -> p j d", p=SUB)

        with nc.Block() as block:

            @block.sync
            def _(sp):
                n = 0
                for n_, name in (("1", "w1"), ("2", "w2")):
                    for k in ("b", "g", "be", "m", "v"):
                        sp.dma_start(cols[n_][k][:, :, :], A[f"{k}{n_}_columns"]).then_inc(weights_in, 16)
                        n += 1
                sp.dma_start(wr[:, :, :], A["L0_ffn_Wr"].rearrange("(k p) n -> p k n", p=128)).then_inc(weights_in, 16)
                sp.dma_start(w_second[:, :, :], A["w_second"].rearrange("(k p) n -> p k n", p=128)).then_inc(weights_in, 16)
                sp.dma_start(bo[:, :], A["L0_ffn_bo"]).then_inc(weights_in, 16)
                sp.dma_start(br[:, :], A["L0_ffn_br"].unsqueeze(0).to_broadcast([SUB, E0])).then_inc(weights_in, 16)
                sp.dma_start(b_rel[:, :], A["L1_gnn_b_rel"].unsqueeze(0).to_broadcast([SUB, D])).then_inc(weights_in, 16)
                assert n + 5 == WEIGHT_LOADS
                windows = windows_of(sp, T, P)

                def load(g):
                    need = sp.value_load(T["need"][0:1, bass.ds(g, 1)] if not isinstance(g, int) else T["need"][0:1, g:g + 1], min_val=1, max_val=NB)
                    apart(sp, added, need * windows * 16, S["started"])
                    apart(sp, acc_done, g * PER + PER, S["started"])
                    sp.dma_start(sums[:, :, :], group_rows(M["sum0"], g)).then_inc(sums_in, 16)
                    sp.dma_start(xs[:, :, :], group_rows(M["xs"], g)).then_inc(sums_in, 16)

                def store_normed(g):
                    apart(sp, y_done, g * (USES * PER) + (USES * PER + PER), S["started"])
                    sp.dma_start(group_rows(M["x2"], g), half(acc, g)).then_inc(x2_out, 16)
                    apart(sp, xl_done, g * PER + PER, S["started"])
                    sp.dma_start(group_rows(M["xl"], g), xl[:, :, :]).then_inc(xl_out, 16)

                def store_products(g, j):
                    apart(sp, pr_done, g * PER + (j + 1), S["started"])
                    at = g * GRP + j * SUB
                    to = slice(at, at + SUB) if isinstance(g, int) else bass.ds(at, SUB)
                    sp.dma_start(M["rel"][to, :], pr[:, j % 2, 0:D]).then_inc(pr_out[j % 2], 16)
                    sp.dma_start(M["sum1"][to, :], pr[:, j % 2, D:2 * D]).then_inc(pr_out[j % 2], 16)

                load(0)
                load(1)
                with sp.Fori(1, G - 1) as g:
                    store_normed(g - 1)
                    load(g + 1)
                    for j in range(PER):
                        store_products(g - 1, j)
                for g in (G - 2, G - 1):
                    store_normed(g)
                    for j in range(PER):
                        store_products(g, j)
                sp.wait_ge(x2_out, 16 * G)
                sp.wait_ge(xl_out, 16 * G)
                for i in range(2):
                    sp.wait_ge(pr_out[i], 64 * G)

            @block.gpsimd
            def _(pool):
                pool.sem_inc(acc_done, PER)
                pool.sem_inc(rows_used, CH)
                nc.gpsimd.memset(rows[:, :, D:D + 1], 1.0).then_inc(ones_set, 1)
                gather_and_add(pool, nc, P, T, S, index, rows, win[:, :], M["kept"], M["sum0"], index_set, rows_in, rows_used, win_out, added)

            @block.tensor
            def _(pe):
                pe.wait_ge(ones_set, 1)
                windows = windows_of(pe, T, P)
                q = window_counter(pe, "b_pe_window")

                def sum_block(b):
                    multiply_windows(pe, nc, b, q, windows, sum_ps[:, 0:D + 1], sel, rows, rows_in, rows_used, sel_done, win_out)

                def up(banks, e, weight, parts, rest_ready, done):
                    for m in range(KD):
                        for k in range(KD):
                            for w in weight:
                                nc.tensor.matmul(banks[m][:, 0:GRP], w[:, e, k, m * 128:(m + 1) * 128], parts[0][:, k, :], start=k == 0 and w is weight[0], stop=False)
                    rest_ready()
                    for m in range(KD):
                        for k in range(KD):
                            last = nc.tensor.matmul(banks[m][:, 0:GRP], weight[0][:, e, k, m * 128:(m + 1) * 128], parts[1][:, k, :], start=False, stop=k == KD - 1)
                        last.then_inc(done, 1)

                def up1(g, e):
                    if e == 0:
                        pe.wait_ge(xnT_done, g * KD + KD)
                    up(h1_ps, e, w1, x_parts, lambda: pe.wait_ge(x_rest_done, g * KD + KD) if e == 0 else None, h1_ps_done)

                def up2(g, e):
                    n = g * (2 * KD * E0) + 2 * KD * e
                    pe.wait_ge(h_done, n * 2 + (2 * KD - 1))
                    up(h2_ps, e, w2, h1, lambda: pe.wait_ge(rest_done, n + 3 * KD), h2_ps_done)

                def down(g, e):
                    use = g * USES + (e + 1)
                    if e < 0:
                        pe.wait_ge(gateT_done, g + 1)
                    else:
                        pe.wait_ge(rest_done, g * (2 * KD * E0) + (2 * KD * (e + 2)))
                    for j in range(PER):
                        if j % 2 == 0:
                            pe.wait_ge(y_done, use * PER + (j + 2))
                        to = y_ps[j // 2][:, (j % 2) * D:(j % 2 + 1) * D]
                        if e < 0:
                            last = nc.tensor.matmul(to[0:SUB, :], gateT[:, j, :], bo[:, :], start=True, stop=True)
                        else:
                            for k in range(KD):
                                for n, (h, w) in enumerate(((0, 0), (0, 1), (1, 0))):
                                    last = nc.tensor.matmul(to, h2[h][:, k, j * SUB:j * SUB + 128], wo[w][:, e, k, :], start=k == 0 and n == 0, stop=k == KD - 1 and n == 2)
                        if j % 2:
                            last.then_inc(y_ps_done, 1)

                def transpose_xn(g):
                    pe.wait_ge(xn_done, g * PER + PER)
                    for k in range(KD):
                        for j in range(PER):
                            last = nc.tensor.transpose(h1_ps[k][:, j * SUB:(j + 1) * SUB], xn[:, j, k * 128:(k + 1) * 128], T["ident"][0:SUB, 0:SUB])
                        last.then_inc(xnT_ps_done, 1)

                def logits(g, first):
                    pe.wait_ge(xnT_done, g * KD + KD)
                    if not first:
                        pe.wait_ge(pr_done, g * PER - PER)
                    for j in range(PER):
                        for k in range(KD):
                            last = nc.tensor.matmul(mix_ps[0:SUB, j * E0:(j + 1) * E0], xnT[:, k, j * SUB:(j + 1) * SUB], wr[:, k, :], start=k == 0, stop=k == KD - 1)
                    last.then_inc(logit_ps_done, 1)

                def transpose_gates(g):
                    pe.wait_ge(gate_step, g * 6 + 6)
                    for j in range(PER):
                        last = nc.tensor.transpose(mix_ps[0:E0, j * SUB:(j + 1) * SUB], gate[:, j, :], T["ident"][0:SUB, 0:SUB])
                    last.then_inc(gateT_ps_done, 1)

                def transpose_xl(g, k):
                    if k == 0:
                        pe.wait_ge(xl_done, g * PER + PER)
                    else:
                        pe.wait_ge(xlT_done, g * KD + 1)
                    for j in range(PER):
                        last = nc.tensor.transpose(mix_ps[:, j * SUB:(j + 1) * SUB], xl[:, j, k * 128:(k + 1) * 128], T["ident"][0:SUB, 0:SUB])
                    last.then_inc(xlT_ps_done, 1)

                def products(g, j):
                    if j == 0:
                        pe.wait_ge(xlT_done, g * KD + KD)
                    else:
                        pe.wait_ge(pr_done, g * PER + j)
                    for k in range(KD):
                        last = nc.tensor.matmul(mix_ps[0:SUB, :], xlT[:, k, j * SUB:(j + 1) * SUB], w_second[:, k, :], start=k == 0, stop=k == KD - 1)
                    last.then_inc(pr_ps_done, 1)

                def between(g, e, first):
                    if e == 0:
                        return
                    if not first:
                        if e == 2:
                            transpose_xl(g - 1, 0)
                        elif e == 3:
                            transpose_xl(g - 1, 1)
                        elif e >= 4:
                            products(g - 1, e - 4)

                def group(g, first, final):
                    begin, middle, end = edge_plan(pe, T, g)
                    for e in range(E0):
                        up1(g, e)
                        if e == 0:
                            logits(g, first)
                        edges_of_step(pe, e, begin, middle, end, NB, sum_block)
                        if e > 0:
                            down(g, e - 1)
                        up2(g, e)
                        if e == 0:
                            transpose_gates(g)
                            down(g, -1)
                        between(g, e, first)
                    if not final:
                        transpose_xn(g + 1)
                    down(g, E0 - 1)

                pe.sem_inc(y_done, PER)
                first_blocks(pe, T, NB, sum_block)
                pe.wait_ge(weights_in, 16 * WEIGHT_LOADS)
                pe.wait_ge(behind_set, 3)
                transpose_xn(0)
                group(0, True, False)
                with pe.Fori(1, G - 1) as g:
                    group(g, False, False)
                group(G - 1, False, True)
                transpose_xl(G - 1, 0)
                transpose_xl(G - 1, 1)
                for j in range(PER):
                    products(G - 1, j)

            @block.scalar
            def _(act):
                windows = windows_of(act, T, P)
                q = window_counter(act, "b_act_window")
                act.sem_inc(rest_done, 2 * KD)
                act.wait_ge(fold, 2)
                act.wait_ge(weights_in, 16 * WEIGHT_LOADS)
                for i, n_ in enumerate("12"):
                    nc.scalar.activation(cols[n_]["v"][:, :, :], cols[n_]["v"][:, :, :], ACT.Sqrt, bias=eps0[:, :]).then_inc(fold_dev, 1)

                def sum_block(b):
                    move_windows(act, nc, q, windows, sum_ps[:, 0:D + 1], win[:, :], rows_used, win_out, added)

                def deviation(g, tail):
                    if tail:
                        act.wait_ge(l_mv_done, g * PER + PER)
                        nc.scalar.activation(l_dev[:, :], l_mv[:, :, 1], ACT.Sqrt, bias=eps[0:SUB, :]).then_inc(l_dev_done, 1)
                    else:
                        act.wait_ge(mv_done, g * PER + PER)
                        nc.scalar.activation(dev[:, :], mv[:, :, 1], ACT.Sqrt, bias=eps[0:SUB, :]).then_inc(dev_done, 1)

                def take_xnT(g):
                    for k in range(KD):
                        act.wait_ge(xnT_ps_done, g * KD + (k + 1))
                        nc.scalar.activation(x_parts[0][:, k, :], h1_ps[k][:, 0:GRP], ACT.Copy)
                        nc.scalar.activation(xnT[:, k, :], h1_ps[k][:, 0:GRP], ACT.Copy).then_inc(xnT_done, 1)

                def exponents(g):
                    act.wait_ge(gate_step, g * 6 + 3)
                    nc.scalar.activation(expo[:, :, :], logit[:, :, :], ACT.Exp).then_inc(expo_done, 1)

                def take_gateT(g):
                    act.wait_ge(gateT_ps_done, g + 1)
                    nc.scalar.activation(gateT[:, :, :], mix_ps[0:E0, 0:GRP].rearrange("e (j p) -> e j p", j=PER), ACT.Copy).then_inc(gateT_done, 1)

                def take_h(g, e, layer):
                    ps, ps_done, parts = ((h1_ps, h1_ps_done, h1), (h2_ps, h2_ps_done, h2))[layer]
                    for m in range(KD):
                        n = g * (2 * KD * E0) + (2 * KD * e + KD * layer + m)
                        act.wait_ge(ps_done, g * (E0 * KD) + (e * KD + m + 1))
                        name = "12"[layer]
                        for to in (parts[0], h_full[layer]):
                            if to is h_full[layer]:
                                act.wait_ge(rest_done, n + 1)
                            nc.scalar.activation(to[:, m, 0:GRP], ps[m][:, 0:GRP], ACT.Relu, bias=shift[name][:, e, m:m + 1],
                                                 scale=cols[name]["g"][:, e, m:m + 1]).then_inc(h_done, 1)

                def take_xlT(g, k):
                    act.wait_ge(xlT_ps_done, g * KD + (k + 1))
                    nc.scalar.activation(xlT[:, k, :], mix_ps[:, 0:GRP], ACT.Copy).then_inc(xlT_done, 1)

                def group(g, first, final):
                    begin, middle, end = edge_plan(act, T, g)
                    for e in range(E0):
                        if not first:
                            if e == 1:
                                deviation(g - 1, True)
                            elif e in (3, 4):
                                take_xlT(g - 1, e - 3)
                        take_h(g, e, 0)
                        edges_of_step(act, e, begin, middle, end, NB, sum_block)
                        if e == 0:
                            exponents(g)
                        if e == E0 - 1 and not final:
                            deviation(g + 1, False)
                        take_h(g, e, 1)
                        if e == 0:
                            take_gateT(g)
                    if not final:
                        take_xnT(g + 1)

                first_blocks(act, T, NB, sum_block)
                act.wait_ge(fold, 2 + 2 * 5)
                deviation(0, False)
                take_xnT(0)
                group(0, True, False)
                with act.Fori(1, G - 1) as g:
                    group(g, False, False)
                group(G - 1, False, True)
                deviation(G - 1, True)
                take_xlT(G - 1, 0)
                take_xlT(G - 1, 1)

            @block.vector
            def _(dve):
                first_index(nc, T, index, index_set)
                nc.vector.memset(eps0[:, :], BN_EPS0).then_inc(fold, 1)
                nc.vector.memset(eps[:, :], LN_EPS).then_inc(fold, 1)
                nc.vector.memset(behind[:, :, :], 0.0).then_inc(behind_set, 1)
                dve.wait_ge(behind_set, 1)
                for part in h2:
                    nc.vector.tensor_copy(part[:, :, GRP:], behind[:, :, :]).then_inc(behind_set, 1)
                steps = Steps(dve, fold, 2)
                for i, n_ in enumerate("12"):
                    c = cols[n_]
                    dve.wait_ge(fold_dev, i + 1)
                    steps.then(nc.vector.reciprocal(c["v"][:, :, :], c["v"][:, :, :]))
                    steps.then(nc.vector.tensor_tensor(c["g"][:, :, :], c["g"][:, :, :], c["v"][:, :, :], ALU.mult))
                    steps.then(nc.vector.tensor_tensor(c["b"][:, :, :], c["b"][:, :, :], c["m"][:, :, :], ALU.subtract))
                    steps.then(nc.vector.tensor_tensor(c["b"][:, :, :], c["b"][:, :, :], c["g"][:, :, :], ALU.mult))
                    steps.then(nc.vector.tensor_tensor(shift[n_][:, :, :], c["b"][:, :, :], c["be"][:, :, :], ALU.add))

                windows = windows_of(dve, T, P)
                q = window_counter(dve, "b_dve_window")

                def sum_block(b):
                    pick_windows(dve, nc, b, q, windows, T, index, index_set, at_base, sel, rows_used, base_set, sel_done)

                def add_sums(g):
                    dve.wait_ge(sums_in, g * 32 + 32)
                    nc.vector.tensor_scalar(deg[:, 0, :], sums[:, :, D], 1.0, None, ALU.max).then_inc(deg_done, 1)
                    dve.wait_ge(deg_done, g * 2 + 1)
                    nc.vector.reciprocal(deg[:, 1, :], deg[:, 0, :]).then_inc(deg_done, 1)
                    dve.wait_ge(deg_done, g * 2 + 2)
                    if not isinstance(g, int) or g > 1:
                        dve.wait_ge(x2_out, g * 16 - 16)
                    for j in range(PER):
                        nc.vector.scalar_tensor_tensor(out=slot_of(acc, g, j), in0=sums[:, j, 0:D], scalar=deg[:, 1, j:j + 1], in1=xs[:, j, :],
                                                       op0=ALU.mult, op1=ALU.add).then_inc(acc_done, 1)

                def normed(g, stats, mv, dev, rstd, stats_done, mv_done, dev_done, rstd_done, ready, ready_at, part, to, to_done):
                    if part == 0:
                        for j in range(PER):
                            apart(dve, ready, ready_at + (j + 1), S["started"])
                            nc.vector.bn_stats(stats[:, j, :], slot_of(acc, g, j)).then_inc(stats_done, 1)
                        for j in range(PER):
                            apart(dve, stats_done, g * PER + (j + 1), S["started"])
                            nc.vector.bn_aggr(mv[:, j, :], stats[:, j, :]).then_inc(mv_done, 1)
                    else:
                        dve.wait_ge(dev_done, g + 1)
                        nc.vector.reciprocal(rstd[:, :], dev[:, :]).then_inc(rstd_done, 1)
                        dve.wait_ge(rstd_done, g + 1)
                        for j in range(PER):
                            nc.vector.tensor_scalar(to[:, j, :], slot_of(acc, g, j), mv[:, j, 0:1], rstd[:, j:j + 1], ALU.subtract, ALU.mult).then_inc(to_done, 1)

                def norm_first(g, part):
                    if part and not (isinstance(g, int) and g == 0):
                        dve.wait_ge(xnT_ps_done, g * KD)
                    normed(g, stats, mv, dev, rstd, stats_done, mv_done, dev_done, rstd_done, acc_done, g * PER + PER, part, xn, xn_done)

                def norm_last(g, part):
                    if part:
                        dve.wait_ge(xl_out, g * 16)
                        dve.wait_ge(xlT_ps_done, g * KD)
                    normed(g, l_stats, l_mv, l_dev, l_rstd, l_stats_done, l_mv_done, l_dev_done, l_rstd_done, y_done, g * (USES * PER) + USES * PER, part, xl, xl_done)

                def gates(g):
                    dve.wait_ge(logit_ps_done, g + 1)
                    nc.vector.tensor_tensor(logit[:, :, :], mix_ps[0:SUB, 0:PER * E0].rearrange("p (j e) -> p j e", j=PER),
                                            br[:, :].unsqueeze(1).to_broadcast([SUB, PER, E0]), ALU.add).then_inc(gate_step, 1)
                    dve.wait_ge(gate_step, g * 6 + 1)
                    nc.vector.tensor_reduce(out=soft[:, 0, :], in_=logit[:, :, :], axis=AX.X, op=ALU.max).then_inc(gate_step, 1)
                    dve.wait_ge(gate_step, g * 6 + 2)
                    nc.vector.tensor_tensor(logit[:, :, :], logit[:, :, :], soft[:, 0, :].unsqueeze(2).to_broadcast([SUB, PER, E0]), ALU.subtract).then_inc(gate_step, 1)
                    dve.wait_ge(expo_done, g + 1)
                    nc.vector.tensor_reduce(out=soft[:, 1, :], in_=expo[:, :, :], axis=AX.X, op=ALU.add).then_inc(gate_step, 1)
                    dve.wait_ge(gate_step, g * 6 + 4)
                    nc.vector.reciprocal(soft[:, 1, :], soft[:, 1, :]).then_inc(gate_step, 1)
                    dve.wait_ge(gate_step, g * 6 + 5)
                    nc.vector.tensor_tensor(gate[:, :, :], expo[:, :, :], soft[:, 1, :].unsqueeze(2).to_broadcast([SUB, PER, E0]), ALU.mult).then_inc(gate_step, 1)

                def add_y(g, e):
                    use = g * USES + (e + 1)
                    for j in range(PER):
                        if j % 2 == 0:
                            dve.wait_ge(y_ps_done, use * 2 + (j // 2 + 1))
                        dve.wait_ge(y_done, use * PER + (j + 1))
                        part = y_ps[j // 2][0:SUB, (j % 2) * D:(j % 2 + 1) * D]
                        if e < 0:
                            nc.vector.tensor_tensor(slot_of(acc, g, j), part, slot_of(acc, g, j), ALU.add).then_inc(y_done, 1)
                        else:
                            nc.vector.scalar_tensor_tensor(out=slot_of(acc, g, j), in0=part, scalar=gate[:, j, e:e + 1], in1=slot_of(acc, g, j),
                                                           op0=ALU.mult, op1=ALU.add).then_inc(y_done, 1)

                def rest_of_h(g, e, layer):
                    for m in range(KD):
                        n = g * (2 * KD * E0) + (2 * KD * e + KD * layer + m)
                        dve.wait_ge(h_done, n * 2 + 2)
                        first, rest = (h1, h2)[layer]
                        nc.vector.tensor_tensor(rest[:, m, 0:GRP], h_full[layer][:, m, :], first[:, m, 0:GRP], ALU.subtract).then_inc(rest_done, 1)

                def rest_of_x(g):
                    for k in range(KD):
                        dve.wait_ge(xnT_done, g * KD + (k + 1))
                        nc.vector.tensor_tensor(x_parts[1][:, k, :], xnT[:, k, :], x_parts[0][:, k, :], ALU.subtract).then_inc(x_rest_done, 1)

                def take_products(g, j):
                    dve.wait_ge(pr_ps_done, g * PER + (j + 1))
                    dve.wait_ge(pr_out[j % 2], g * 64 + (j // 2) * 32)
                    nc.vector.tensor_copy(pr[:, j % 2, 0:D], mix_ps[0:SUB, 0:D])
                    nc.vector.tensor_tensor(pr[:, j % 2, D:2 * D], mix_ps[0:SUB, D:2 * D], b_rel[:, :], ALU.add).then_inc(pr_done, 1)

                def group(g, first, final):
                    begin, middle, end = edge_plan(dve, T, g)
                    for e in range(E0):
                        if e == 0:
                            edges_of_step(dve, e, begin, middle, end, NB, sum_block)
                        if not first and e >= 5:
                            take_products(g - 1, e - 5)
                        rest_of_h(g, e, 0)
                        if e == 0:
                            gates(g)
                        else:
                            add_y(g, e - 1)
                        if not first and e == 0:
                            norm_last(g - 1, 0)
                        if not first and e == 1:
                            norm_last(g - 1, 1)
                        if e == E0 - 1 and not final:
                            norm_first(g + 1, 1)
                        if e + 1 < E0:
                            edges_of_step(dve, e + 1, begin, middle, end, NB, sum_block)
                        rest_of_h(g, e, 1)
                        if e == 0:
                            add_y(g, -1)
                        if e == E0 - 2 and not final:
                            add_sums(g + 1)
                            norm_first(g + 1, 0)
                    if not first:
                        take_products(g - 1, 3)
                    if not final:
                        rest_of_x(g + 1)
                    add_y(g, E0 - 1)

                first_blocks(dve, T, NB, sum_block)
                add_sums(0)
                norm_first(0, 0)
                norm_first(0, 1)
                rest_of_x(0)
                group(0, True, False)
                with dve.Fori(1, G - 1) as g:
                    group(g, False, False)
                group(G - 1, False, True)
                norm_last(G - 1, 0)
                norm_last(G - 1, 1)
                for j in range(PER):
                    take_products(G - 1, j)



def second_sum(nc, A, M, T, S, P, sem):
    with ExitStack() as life:
        def sb(name, shape, dt=F32):
            return life.enter_context(nc.sbuf_tensor(name, shape, dt))

        weight = sb("c_weight", [128, P.chunks])
        index = sb("c_index", [128, 2, CH], I32)
        rows = sb("c_rows", [128, CH, D])
        at_base = sb("c_at_base", [128, WIN])
        sel = sb("c_sel", [128, CH, WIN])
        win = sb("c_win", [128, D])
        sum_ps = life.enter_context(nc.psum_tensor("c_sum_ps", [128, D], F32))
        weight_in = sem("c_weight_in")
        rows_in = [sem(f"c_rows_in{j}") for j in range(CH)]
        index_set = sem("c_index_set")
        rows_used = sem("c_rows_used")
        base_set = sem("c_base_set")
        sel_done = sem("c_sel_done")
        win_out = sem("c_win_out")
        added = sem("c_added")

        with nc.Block() as block:

            @block.sync
            def _(sp):
                sp.dma_start(weight[:, :], A["edge_weight"]).then_inc(weight_in, 16)

            @block.gpsimd
            def _(pool):
                pool.sem_inc(rows_used, CH)
                gather_and_add(pool, nc, P, T, S, index, rows, win[:, :], M["rel"], M["sum1"], index_set, rows_in, rows_used, win_out, added)

            @block.tensor
            def _(pe):
                windows = windows_of(pe, T, P)
                q = window_counter(pe, "c_pe_window")
                with pe.Fori(0, P.blocks) as b:
                    multiply_windows(pe, nc, b, q, windows, sum_ps[:, :], sel, rows, rows_in, rows_used, sel_done, win_out)

            @block.scalar
            def _(act):
                windows = windows_of(act, T, P)
                q = window_counter(act, "c_act_window")
                with act.Fori(0, P.blocks):
                    move_windows(act, nc, q, windows, sum_ps[:, :], win[:, :], rows_used, win_out, added)

            @block.vector
            def _(dve):
                windows = windows_of(dve, T, P)
                q = window_counter(dve, "c_dve_window")
                first_index(nc, T, index, index_set)
                dve.wait_ge(weight_in, 16)
                with dve.Fori(0, P.blocks) as b:
                    pick_windows(dve, nc, b, q, windows, T, index, index_set, at_base, sel, rows_used, base_set, sel_done, weight)


def route_and_experts(nc, A, M, S, P, sem, out, stop):
    with ExitStack() as life:
        def keep(name, shape, dt=F32):
            return life.enter_context(nc.sbuf_tensor(name, shape, dt))

        T = {
            "scale": keep("norm_scale", [SUB, D]),
            "shift": keep("norm_shift", [SUB, D]),
            "ident": keep("identity2", [128, 128]),
            "turns": keep("turns_of_expert", [1, E1], I32),
        }
        column_stats(nc, A, M, T, S, P, sem)
        route(nc, A, M, T, S, P, sem, out)
        if stop > 4:
            experts(nc, A, M, T, S, P, sem, out)


def column_stats(nc, A, M, T, S, P, sem):
    G = P.groups
    with ExitStack() as life:
        def sb(name, shape, dt=F32):
            return life.enter_context(nc.sbuf_tensor(name, shape, dt))

        o = sb("d_rows", [SUB, PER, D])
        stats = sb("d_stats", [128, KD, G * 6])
        mv = sb("d_mv", [128, KD, 2])
        eps = sb("d_eps", [128, 1])
        gamma = sb("d_gamma", [128, KD])
        beta = sb("d_beta", [128, KD])
        dev = sb("d_dev", [128, KD])
        both = sb("d_both", [128, 2, KD])
        diag = sb("d_diag", [128, 2, KD, 128])
        ones = sb("d_ones", [128, 128])
        t_ps = [life.enter_context(nc.psum_tensor(f"d_t_ps{k}", [128, 512], F32)) for k in range(KD)]
        b_ps = [life.enter_context(nc.psum_tensor(f"d_b_ps{k}", [128, 512], F32)) for k in range(2)]
        o_in = [sem(f"d_rows_in{j}") for j in range(PER)]
        affine_in = sem("d_affine_in")
        set_up = sem("d_set_up")
        t_done = sem("d_t_done")
        stats_done = sem("d_stats_done")
        step = sem("d_step")
        dev_done = sem("d_dev_done")
        spread = sem("d_spread")
        spread_out = sem("d_spread_out")
        o_t = M["sum1"][0:P.nodes, :].rearrange("(t p) d -> t p d", p=SUB)

        with nc.Block() as block:

            @block.sync
            def _(sp):
                sp.dma_start(gamma[:, :], A["gamma"]).then_inc(affine_in, 16)
                sp.dma_start(beta[:, :], A["beta"]).then_inc(affine_in, 16)
                for j in range(PER):
                    sp.dma_start(o[:, j, :], o_t[j]).then_inc(o_in[j], 16)
                with sp.Fori(1, G) as g:
                    apart(sp, t_done, g * KD, S["started"])
                    for j in range(PER):
                        sp.dma_start(o[:, j, :], tile_of(o_t, g * PER + j)).then_inc(o_in[j], 16)

            @block.gpsimd
            def _(pool):
                nc.gpsimd.memset(T["ident"][:, :], 0.0).then_inc(set_up, 1)
                pool.wait_ge(set_up, 1)
                nc.gpsimd.affine_select(out=T["ident"][:, :], in_=T["ident"][:, :], compare_op=ALU.not_equal, fill=1.0,
                                        base=0, pattern=[[-1, 128]], channel_multiplier=1)
                nc.gpsimd.memset(ones[:, :], 1.0)
                nc.gpsimd.memset(eps[:, :], BN_EPS1).then_inc(set_up, 1)

            @block.tensor
            def _(pe):
                pe.wait_ge(set_up, 2)
                pe.sem_inc(stats_done, KD)
                with pe.Fori(0, G) as g:
                    for k in range(KD):
                        pe.wait_ge(stats_done, g * KD + (k + 1))
                        for j in range(PER):
                            if k == 0:
                                pe.wait_ge(o_in[j], g * 16 + 16)
                            last = nc.tensor.transpose(t_ps[k][:, j * SUB:(j + 1) * SUB], o[:, j, k * 128:(k + 1) * 128], T["ident"][0:SUB, 0:SUB])
                        last.then_inc(t_done, 1)
                pe.wait_ge(step, KD + 4 + 2 * KD)
                for i in range(2):
                    for k in range(KD):
                        last = nc.tensor.matmul(b_ps[i][0:SUB, k * 128:(k + 1) * 128], ones[:, 0:SUB], diag[:, i, k, :], start=True, stop=True)
                last.then_inc(spread, 1)

            @block.scalar
            def _(act):
                act.wait_ge(step, KD)
                act.wait_ge(set_up, 2)
                nc.scalar.activation(dev[:, :], mv[:, :, 1], ACT.Sqrt, bias=eps[:, :]).then_inc(dev_done, 1)

            @block.vector
            def _(dve):
                with dve.Fori(0, G) as g:
                    for k in range(KD):
                        apart(dve, t_done, g * KD + (k + 1), S["started"])
                        nc.vector.bn_stats(stats[:, k, bass.ds(g * 6, 6)], t_ps[k][:, 0:GRP]).then_inc(stats_done, 1)
                dve.wait_ge(stats_done, G * KD + KD)
                steps = Steps(dve, step)
                for k in range(KD):
                    steps.then(nc.vector.bn_aggr(mv[:, k, :], stats[:, k, :]))
                dve.wait_ge(dev_done, 1)
                dve.wait_ge(affine_in, 32)
                steps.then(nc.vector.reciprocal(dev[:, :], dev[:, :]))
                steps.then(nc.vector.tensor_tensor(both[:, 0, :], dev[:, :], gamma[:, :], ALU.mult))
                steps.then(nc.vector.tensor_tensor(both[:, 1, :], mv[:, :, 0], both[:, 0, :], ALU.mult))
                steps.then(nc.vector.tensor_tensor(both[:, 1, :], beta[:, :], both[:, 1, :], ALU.subtract))
                dve.wait_ge(set_up, 2)
                for i in range(2):
                    for k in range(KD):
                        nc.vector.tensor_scalar(diag[:, i, k, :], T["ident"][:, :], both[:, i, k:k + 1], None, ALU.mult).then_inc(step, 1)
                dve.wait_ge(spread, 1)
                nc.vector.tensor_copy(T["scale"][:, :], b_ps[0][0:SUB, 0:D])
                nc.vector.tensor_copy(T["shift"][:, :], b_ps[1][0:SUB, 0:D]).then_inc(spread_out, 1)


def route(nc, A, M, T, S, P, sem, out):
    G = P.groups
    W = D + META
    with ExitStack() as life:
        def sb(name, shape, dt=F32):
            return life.enter_context(nc.sbuf_tensor(name, shape, dt))

        def pb(name):
            return life.enter_context(nc.psum_tensor(name, [128, 512], F32))

        o = sb("e_sum", [SUB, 2, PER, D])
        xl = sb("e_xl", [SUB, 2, PER, D])
        x2 = sb("e_x2", [SUB, 2, PER, D])
        x3 = sb("e_x3", [SUB, 2, PER, W])
        row = sb("e_row", [SUB, PER, W])
        stats = sb("e_stats", [SUB, PER, 6])
        mv = sb("e_mv", [SUB, PER, 2])
        dev = sb("e_dev", [SUB, PER])
        rstd = sb("e_rstd", [SUB, PER])
        xn = sb("e_xn", [SUB, PER, D])
        xnT = sb("e_xnT", [128, KD, GRP])
        wg = sb("e_wg", [128, KD, E1])
        bg = sb("e_bg", [SUB, E1])
        eps = sb("e_eps", [128, 1])
        rank = sb("e_rank", [SUB, PER, E1])
        token = sb("e_token", [SUB, PER])
        below = sb("e_below", [SUB, SUB])
        ones = sb("e_ones", [SUB, SUB])
        logit = sb("e_logit", [SUB, PER, E1])
        expo = sb("e_expo", [SUB, PER, E1])
        first = sb("e_first", [SUB, PER, E1])
        chosen = sb("e_chosen", [SUB, PER, E1])
        place = sb("e_place", [SUB, PER, E1])
        most = sb("e_most", [SUB, 6, PER])
        ahead = sb("e_ahead", [SUB, PER + 1, E1])
        slot = sb("e_slot", [SUB, PER], I32)
        count = sb("e_count", [1, E1])
        count_i = sb("e_count_int", [1, E1], I32)
        t_ps = [pb(f"e_t_ps{k}") for k in range(KD)]
        l_ps = pb("e_l_ps")
        p_ps = pb("e_p_ps")

        gate_in = sem("e_gate_in")
        set_up = sem("e_set_up")
        o_in = sem("e_sum_in")
        xl_in = sem("e_xl_in")
        x2_in = sem("e_x2_in")
        scaled = sem("e_scaled")
        shifted = sem("e_shifted")
        relu_done = sem("e_relu_done")
        x3_done = sem("e_x3_done")
        stats_done = sem("e_stats_done")
        mv_done = sem("e_mv_done")
        dev_done = sem("e_dev_done")
        rstd_done = sem("e_rstd_done")
        xn_done = sem("e_xn_done")
        meta_done = sem("e_meta_done")
        t_done = sem("e_t_done")
        xnT_done = sem("e_xnT_done")
        l_done = sem("e_l_done")
        expo_done = sem("e_expo_done")
        pick = sem("e_pick")
        p_done = sem("e_p_done")
        row_done = sem("e_row_done")
        out_in = sem("e_out_stored")
        sent = [sem(f"e_sent{j}") for j in range(PER)]
        PICKS = 22

        def group_rows(dram, g):
            at = g * GRP
            return dram[slice(at, at + GRP) if isinstance(g, int) else bass.ds(at, GRP), :].rearrange("(j p) d -> p j d", p=SUB)

        with nc.Block() as block:

            @block.sync
            def _(sp):
                sp.dma_start(wg[:, :, :], A["L1_ffn_gate_w"].rearrange("(k p) n -> p k n", p=128)).then_inc(gate_in, 16)
                sp.dma_start(bg[:, :], A["L1_ffn_gate_b"].unsqueeze(0).to_broadcast([SUB, E1])).then_inc(gate_in, 16)

                def load(g):
                    sp.dma_start(half(o, g), group_rows(M["sum1"], g)).then_inc(o_in, 16)
                    sp.dma_start(half(xl, g), group_rows(M["xl"], g)).then_inc(xl_in, 16)
                    sp.dma_start(half(x2, g), group_rows(M["x2"], g)).then_inc(x2_in, 16)

                def store(g):
                    apart(sp, x3_done, g + 1, S["started"])
                    apart(sp, out_in, g * 16, S["started"])
                    sp.dma_start(group_rows(out, g), half(x3, g)[:, :, 0:D]).then_inc(out_in, 16)

                def load_next(g):
                    for landed in (o_in, xl_in, x2_in):
                        apart(sp, landed, g * 16, S["started"])
                    load(g)

                load(0)
                load_next(1)
                with sp.Fori(2, G) as g:
                    store(g - 2)
                    load_next(g)
                store(G - 2)
                store(G - 1)
                sp.wait_ge(out_in, 16 * G)

            @block.gpsimd
            def _(pool):
                nc.gpsimd.memset(ones[:, :], 1.0).then_inc(set_up, 1)
                pool.wait_ge(set_up, 1)
                nc.gpsimd.affine_select(out=below[:, :], in_=ones[:, :], compare_op=ALU.is_gt, fill=0.0,
                                        base=0, pattern=[[1, SUB]], channel_multiplier=-1)
                nc.gpsimd.iota(rank[:, :, :], pattern=[[0, PER], [-1, E1]], base=E1, channel_multiplier=0, allow_small_or_imprecise_dtypes=True)
                nc.gpsimd.iota(token[:, :], pattern=[[SUB, PER]], base=1, channel_multiplier=1, allow_small_or_imprecise_dtypes=True)
                nc.gpsimd.memset(ahead[:, :, :], 0.0)
                nc.gpsimd.memset(eps[:, :], LN_EPS).then_inc(set_up, 1)

                def scale(g):
                    pool.wait_ge(o_in, g * 16 + 16)
                    nc.gpsimd.tensor_tensor(half(o, g), half(o, g), T["scale"][:, :].unsqueeze(1).to_broadcast([SUB, PER, D]), ALU.mult).then_inc(scaled, 1)
                    apart(pool, scaled, g + 1, S["started"])
                    nc.gpsimd.tensor_tensor(half(o, g), half(o, g), T["shift"][:, :].unsqueeze(1).to_broadcast([SUB, PER, D]), ALU.add).then_inc(shifted, 1)

                def send(g):
                    for j in range(PER):
                        if j == 0:
                            apart(pool, row_done, g + 1, S["started"])
                            apart(pool, pick, g * PICKS + PICKS, S["started"])
                        nc.gpsimd.indirect_dma_start(out=M["buf"], out_offset=bass.IndirectOffsetOnAxis(ap=slot[:, j:j + 1], axis=0),
                                                     in_=row[:, j, :], in_offset=None, bounds_check=E1 * P.slots - 1, oob_is_err=False).then_inc(sent[j], 16)

                scale(0)
                scale(1)
                with pool.Fori(2, G) as g:
                    scale(g)
                    send(g - 2)
                send(G - 2)
                send(G - 1)
                for j in range(PER):
                    pool.wait_ge(sent[j], 16 * G)

            @block.tensor
            def _(pe):
                pe.wait_ge(gate_in, 32)
                pe.wait_ge(set_up, 2)
                with pe.Fori(0, G) as g:
                    pe.wait_ge(xn_done, g * PER + PER)
                    pe.wait_ge(xnT_done, g * KD)
                    for k in range(KD):
                        for j in range(PER):
                            last = nc.tensor.transpose(t_ps[k][:, j * SUB:(j + 1) * SUB], xn[:, j, k * 128:(k + 1) * 128], T["ident"][0:SUB, 0:SUB])
                        last.then_inc(t_done, 1)
                    pe.wait_ge(xnT_done, g * KD + KD)
                    for j in range(PER):
                        for k in range(KD):
                            last = nc.tensor.matmul(l_ps[0:SUB, j * E1:(j + 1) * E1], xnT[:, k, j * SUB:(j + 1) * SUB], wg[:, k, :], start=k == 0, stop=k == KD - 1)
                    last.then_inc(l_done, 1)
                    pe.wait_ge(pick, g * PICKS + 6)
                    flat = chosen[:, :, :].rearrange("p j e -> p (j e)")
                    nc.tensor.matmul(p_ps[0:SUB, 0:PER * E1], below[:, :], flat, start=True, stop=True)
                    nc.tensor.matmul(p_ps[0:SUB, PER * E1:2 * PER * E1], ones[:, :], flat, start=True, stop=True).then_inc(p_done, 1)

            @block.scalar
            def _(act):
                act.wait_ge(set_up, 2)

                def deviation(g):
                    act.wait_ge(mv_done, g * PER + PER)
                    nc.scalar.activation(dev[:, :], mv[:, :, 1], ACT.Sqrt, bias=eps[0:SUB, :]).then_inc(dev_done, 1)

                def exponents(g):
                    act.wait_ge(pick, g * PICKS + 3)
                    nc.scalar.activation(expo[:, :, :], logit[:, :, :], ACT.Exp).then_inc(expo_done, 1)

                def take_xnT(g):
                    for k in range(KD):
                        act.wait_ge(t_done, g * KD + (k + 1))
                        nc.scalar.activation(xnT[:, k, :], t_ps[k][:, 0:GRP], ACT.Copy).then_inc(xnT_done, 1)

                def copy_row(g):
                    act.wait_ge(pick, g * PICKS + 10)
                    for j in range(PER):
                        act.wait_ge(sent[j], g * 16)
                    nc.scalar.activation(row[:, :, :], half(x3, g), ACT.Copy).then_inc(row_done, 1)

                deviation(0)
                take_xnT(0)
                with act.Fori(1, G) as g:
                    deviation(g)
                    exponents(g - 1)
                    take_xnT(g)
                    copy_row(g - 1)
                exponents(G - 1)
                copy_row(G - 1)

            @block.vector
            def _(dve):
                dve.wait_ge(set_up, 2)
                dve.wait_ge(gate_in, 32)

                def front(g):
                    dve.wait_ge(shifted, g + 1)
                    dve.wait_ge(xl_in, g * 16 + 16)
                    nc.vector.scalar_tensor_tensor(out=half(xl, g), in0=half(o, g), scalar=0.0, in1=half(xl, g), op0=ALU.max, op1=ALU.add).then_inc(relu_done, 1)
                    dve.wait_ge(relu_done, g + 1)
                    dve.wait_ge(x2_in, g * 16 + 16)
                    if not isinstance(g, int) or g > 1:
                        dve.wait_ge(out_in, g * 16 - 16)
                        dve.wait_ge(row_done, g - 1)
                    nc.vector.scalar_tensor_tensor(out=half(x3, g)[:, :, 0:D], in0=half(xl, g), scalar=0.0, in1=half(x2, g), op0=ALU.max, op1=ALU.add).then_inc(x3_done, 1)
                    for j in range(PER):
                        apart(dve, x3_done, g + 1, S["started"])
                        nc.vector.bn_stats(stats[:, j, :], slot_of(x3, g, j)[:, 0:D]).then_inc(stats_done, 1)
                    for j in range(PER):
                        apart(dve, stats_done, g * PER + (j + 1), S["started"])
                        nc.vector.bn_aggr(mv[:, j, :], stats[:, j, :]).then_inc(mv_done, 1)
                    dve.wait_ge(dev_done, g + 1)
                    nc.vector.reciprocal(rstd[:, :], dev[:, :]).then_inc(rstd_done, 1)
                    dve.wait_ge(rstd_done, g + 1)
                    dve.wait_ge(t_done, g * KD)
                    for j in range(PER):
                        nc.vector.tensor_scalar(xn[:, j, :], slot_of(x3, g, j)[:, 0:D], mv[:, j, 0:1], rstd[:, j:j + 1], ALU.subtract, ALU.mult).then_inc(xn_done, 1)
                    nc.vector.tensor_copy(half(x3, g)[:, :, D], mv[:, :, 0]).then_inc(meta_done, 1)
                    nc.vector.tensor_copy(half(x3, g)[:, :, D + 1], rstd[:, :]).then_inc(meta_done, 1)

                def back(g):
                    n = 0

                    def then(instruction):
                        nonlocal n
                        instruction.then_inc(pick, 1)
                        n += 1
                        dve.wait_ge(pick, g * PICKS + n)

                    def wide(a):
                        return a.unsqueeze(2).to_broadcast([SUB, PER, E1])

                    dve.wait_ge(l_done, g + 1)
                    then(nc.vector.tensor_tensor(logit[:, :, :], l_ps[0:SUB, 0:PER * E1].rearrange("p (j e) -> p j e", j=PER),
                                                 bg[:, :].unsqueeze(1).to_broadcast([SUB, PER, E1]), ALU.add))
                    then(nc.vector.tensor_reduce(out=most[:, 0, :], in_=logit[:, :, :], axis=AX.X, op=ALU.max))
                    then(nc.vector.tensor_tensor(logit[:, :, :], logit[:, :, :], wide(most[:, 0, :]), ALU.subtract))
                    then(nc.vector.scalar_tensor_tensor(out=first[:, :, :], in0=logit[:, :, :], scalar=0.0, in1=rank[:, :, :], op0=ALU.is_equal, op1=ALU.mult))
                    then(nc.vector.tensor_reduce(out=most[:, 1, :], in_=first[:, :, :], axis=AX.X, op=ALU.max))
                    then(nc.vector.tensor_tensor(chosen[:, :, :], first[:, :, :], wide(most[:, 1, :]), ALU.is_equal))
                    dve.wait_ge(expo_done, g + 1)
                    then(nc.vector.tensor_reduce(out=most[:, 2, :], in_=expo[:, :, :], axis=AX.X, op=ALU.add))
                    dve.wait_ge(meta_done, g * 2 + 2)
                    then(nc.vector.reciprocal(half(x3, g)[:, :, D + 2], most[:, 2, :]))
                    then(nc.vector.tensor_copy(half(x3, g)[:, :, D + 3], token[:, :]))
                    then(nc.vector.tensor_scalar(token[:, :], token[:, :], float(GRP), None, ALU.add))
                    dve.wait_ge(p_done, g + 1)
                    for j in range(PER):
                        then(nc.vector.tensor_tensor(ahead[:, j + 1, :], ahead[:, j, :], p_ps[0:SUB, (PER + j) * E1:(PER + j + 1) * E1], ALU.add))
                    then(nc.vector.tensor_tensor(place[:, :, :], ahead[:, 0:PER, :], p_ps[0:SUB, 0:PER * E1].rearrange("p (j e) -> p j e", j=PER), ALU.add))
                    then(nc.vector.tensor_tensor(place[:, :, :], place[:, :, :], chosen[:, :, :], ALU.mult))
                    then(nc.vector.tensor_copy(ahead[:, 0, :], ahead[:, PER, :]))
                    then(nc.vector.tensor_reduce(out=most[:, 3, :], in_=place[:, :, :], axis=AX.X, op=ALU.add))
                    then(nc.vector.tensor_scalar(most[:, 4, :], most[:, 1, :], -float(P.slots), float(E1 * P.slots), ALU.mult, ALU.add))
                    then(nc.vector.tensor_tensor(most[:, 4, :], most[:, 4, :], most[:, 3, :], ALU.add))
                    then(nc.vector.tensor_scalar(most[:, 5, :], most[:, 3, :], float(P.cap), FAR, ALU.is_ge, ALU.mult))
                    for j in range(PER):
                        dve.wait_ge(sent[j], g * 16)
                    nc.vector.tensor_tensor(slot[:, :], most[:, 4, :], most[:, 5, :], ALU.add).then_inc(pick, 1)
                    n += 1
                    assert n == PICKS, n

                front(0)
                with dve.Fori(1, G) as g:
                    front(g)
                    back(g - 1)
                back(G - 1)
                steps = Steps(dve, pick, G * PICKS)
                dve.wait_ge(pick, G * PICKS)
                steps.then(nc.vector.tensor_scalar(count[:, :], ahead[0:1, 0, :], float(P.cap), float(TOK - 1), ALU.min, ALU.add))
                steps.then(nc.vector.tensor_scalar(count[:, :], count[:, :], float(TOK), None, ALU.max))
                steps.then(nc.vector.tensor_copy(count_i[:, :], count[:, :]))
                steps.then(nc.vector.tensor_scalar(T["turns"][:, :], count_i[:, :], TOK.bit_length() - 1, None, ALU.arith_shift_right))


def experts(nc, A, M, T, S, P, sem, out):
    W = D + META
    ST = TOK // 128
    RING = 4
    with ExitStack() as life:
        def sb(name, shape, dt=F32):
            return life.enter_context(nc.sbuf_tensor(name, shape, dt))

        def pb(name):
            return life.enter_context(nc.psum_tensor(name, [128, 512], F32))

        rows = sb("f_rows", [128, RING, ST, W])
        xf = sb("f_xf", [128, ST, D])
        x_parts = [sb(f"f_x_part{i}", [128, KD, TOK], F32R) for i in range(2)]
        h_full = sb("f_h_full", [128, NF, TOK])
        h_parts = [sb(f"f_h_part{i}", [128, NF, TOK], F32R) for i in range(2)]
        w1 = [sb(f"f_w1_{i}", [128, KD, F1]) for i in range(2)]
        w2 = [sb(f"f_w2_{i}", [128, NF, D]) for i in range(2)]
        w1_parts = [[sb(f"f_w1_{i}_part{n}", [128, KD, F1], F32R) for n in range(2)] for i in range(2)]
        w2_parts = [[sb(f"f_w2_{i}_part{n}", [128, NF, D], F32R) for n in range(2)] for i in range(2)]
        b1 = [sb(f"f_b1_{i}", [128, NF]) for i in range(2)]
        b2 = [sb(f"f_b2_{i}", [128, D]) for i in range(2)]
        y = sb("f_y", [128, ST, D])
        odd = sb("f_odd", [128, 3, ST, D], I32)
        fill = sb("f_fill", [128, 3, ST, D])
        res = sb("f_res", [128, ST, D])
        none = sb("f_none", [128, 2, ST])
        token = sb("f_token", [128, ST], I32)
        x_ps = pb("f_x_ps")
        h_ps = [pb(f"f_h_ps{i}") for i in range(NF // 2)]
        y_ps = [pb(f"f_y_ps{i}") for i in range(ST)]

        set_up = sem("f_set_up")
        w_in = [sem(f"f_w_in{i}") for i in range(2)]
        biases_in = [sem(f"f_biases_in{i}") for i in range(2)]
        rows_in = sem("f_rows_in")
        xf_done = sem("f_xf_done")
        x_ps_done = sem("f_x_ps_done")
        xT_done = sem("f_xT_done")
        h_ps_done = sem("f_h_ps_done")
        h_done = sem("f_h_done")
        h_rest_done = sem("f_h_rest_done")
        x_rest_done = sem("f_x_rest_done")
        w_first_done = sem("f_w_first_done")
        w_rest_done = sem("f_w_rest_done")
        y_ps_done = sem("f_y_ps_done")
        y_step = sem("f_y_step")
        token_done = sem("f_token_done")
        res_done = sem("f_res_done")
        sent = [sem(f"f_sent{i}") for i in range(ST)]
        STEPS = 2 * ST + 6

        def turns_of(engine, e):
            return engine.value_load(column_of(T["turns"], e), min_val=1, max_val=P.slots // TOK)

        def split_ahead(engine, split, pair, i, q):
            if i == 0:
                split(pair, 1, q)
            else:
                with engine.If(pair < E1 // 2 - 1):
                    split(pair + 1, 0, q)

        def each_turn(engine, name, body, at_expert=None, after_expert=None):
            q_reg = window_counter(engine, name)
            with engine.Fori(0, E1 // 2) as pair:
                for i in range(2):
                    if at_expert:
                        at_expert(pair, i, engine.snap(q_reg))
                    turns = turns_of(engine, pair * 2 + i)
                    with engine.Fori(0, turns) as t:
                        q = engine.snap(q_reg)
                        body(pair, i, t, q)
                        engine.reg_add(q_reg, q_reg, 1)
                    if after_expert:
                        after_expert(pair, i)
            return q_reg

        with nc.Block() as block:

            @block.sync
            def _(sp):
                def load(first_slot, q):
                    apart(sp, rows_in, q * 16, S["started"])
                    apart(sp, res_done, q + 1, S["started"])
                    sp.dma_start(half(rows, q), M["buf"][bass.ds(first_slot, TOK), :].rearrange("(s p) w -> p s w", p=128)).then_inc(rows_in, 16)

                def body(pair, i, t, q):
                    load(pair * (2 * P.slots) + (t * TOK + i * P.slots), q)

                q_reg = each_turn(sp, "f_sp_turn", body)
                load(0, sp.snap(q_reg))
                apart(sp, rows_in, sp.snap(q_reg) * 16 + 16, S["started"])

            @block.gpsimd
            def _(pool):
                pool.sem_inc(res_done, RING)
                for n, value in enumerate((1.0e4, -1.0e4, 0.0)):
                    last = nc.gpsimd.memset(fill[:, n, :, :], value)
                last.then_inc(set_up, 1)

                def load_matrices(e, i):
                    def of(a):
                        return a[e] if isinstance(e, int) else a[bass.ds(e, 1)].rearrange("a b c -> (a b) c")

                    pool.dma_start(w1[i][:, :, :], of(A["L1_ffn_w1"]).rearrange("(k p) n -> p k n", p=128)).then_inc(w_in[i], 16)
                    pool.dma_start(w2[i][:, :, :], of(A["L1_ffn_w2"]).rearrange("(k p) n -> p k n", p=128)).then_inc(w_in[i], 16)

                def load_biases(e, i):
                    pool.dma_start(b1[i][:, :], A["expert_b1_columns"][:, e, :] if isinstance(e, int) else A["expert_b1_columns"][:, bass.ds(e, 1), :].rearrange("p a f -> p (a f)")).then_inc(biases_in[i], 16)
                    pool.dma_start(b2[i][:, :], (A["L1_ffn_b2"][e:e + 1, :] if isinstance(e, int) else A["L1_ffn_b2"][bass.ds(e, 1), :]).to_broadcast([128, D])).then_inc(biases_in[i], 16)

                for e in range(2):
                    load_matrices(e, e)
                    load_biases(e, e)

                def body(pair, i, t, q):
                    apart(pool, y_step, q * STEPS + 2 * STEPS, S["started"])
                    for s in range(ST):
                        apart(pool, sent[s], q * 16, S["started"])
                    for s in range(ST):
                        last = nc.gpsimd.tensor_tensor(res[:, s, :], y[:, s, :], slot_of(rows, q, s)[:, 0:D], ALU.add)
                    last.then_inc(res_done, 1)
                    apart(pool, res_done, q + RING + 1, S["started"])
                    for s in range(ST):
                        nc.gpsimd.indirect_dma_start(out=out, out_offset=bass.IndirectOffsetOnAxis(ap=token[:, s:s + 1], axis=0),
                                                     in_=res[:, s, :], in_offset=None, bounds_check=P.nodes - 1, oob_is_err=False).then_inc(sent[s], 16)

                def later(pair, i):
                    return nc.s_assert_within(pair * 2 + (i + 2), 2, E1 - 1, skip_runtime_bounds_check_because="the pair is not the last")

                def at_expert(pair, i, q):
                    apart(pool, w_rest_done, pair * 4 + (2 * i + 2), S["started"])
                    with pool.If(pair < E1 // 2 - 1):
                        load_matrices(later(pair, i), i)

                def after_expert(pair, i):
                    with pool.If(pair < E1 // 2 - 1):
                        load_biases(later(pair, i), i)

                q_reg = each_turn(pool, "f_pool_turn", body, at_expert, after_expert)
                for s in range(ST):
                    apart(pool, sent[s], pool.snap(q_reg) * 16, S["started"])

            @block.tensor
            def _(pe):
                def transpose(q):
                    pe.wait_ge(xf_done, q * ST + ST)
                    pe.wait_ge(x_rest_done, q)
                    for k in range(KD):
                        for s in range(ST):
                            at = k * TOK + s * 128
                            last = nc.tensor.transpose(x_ps[:, at:at + 128], xf[:, s, k * 128:(k + 1) * 128], T["ident"][:, :])
                    last.then_inc(x_ps_done, 1)

                def at_expert(pair, i, q):
                    pe.wait_ge(w_rest_done, pair * 4 + (2 * i + 2))

                def body(pair, i, t, q):
                    three = ((0, 0), (1, 0), (0, 1))
                    pe.wait_ge(xT_done, q + 1)
                    pe.wait_ge(x_rest_done, q + 1)
                    for f in range(NF):
                        for k in range(KD):
                            for n, (w, x) in enumerate(three):
                                last = nc.tensor.matmul(h_ps[f // 2][:, (f % 2) * TOK:(f % 2 + 1) * TOK], w1_parts[i][w][:, k, f * 128:(f + 1) * 128], x_parts[x][:, k, :],
                                                        start=k == 0 and n == 0, stop=k == KD - 1 and n == 2)
                        if f % 2:
                            last.then_inc(h_ps_done, 1)
                    pe.wait_ge(y_step, q * STEPS + ST)
                    for f in range(NF):
                        if f == NF // 2:
                            transpose(q + 1)
                        if f % 2 == 0:
                            pe.wait_ge(h_rest_done, q * (NF // 2) + (f // 2 + 1))
                        for s in range(ST):
                            for n, (w, h) in enumerate(three):
                                last = nc.tensor.matmul(y_ps[s][:, 0:D], h_parts[h][:, f, s * 128:(s + 1) * 128], w2_parts[i][w][:, f, :],
                                                        start=f == 0 and n == 0, stop=f == NF - 1 and n == 2)
                            if f == NF - 1:
                                last.then_inc(y_ps_done, 1)

                pe.sem_inc(y_step, STEPS)
                transpose(0)
                each_turn(pe, "f_pe_turn", body, at_expert)

            @block.scalar
            def _(act):
                def take_x(q):
                    act.wait_ge(x_ps_done, q + 1)
                    nc.scalar.activation(x_parts[0][:, :, :], x_ps[:, 0:KD * TOK].rearrange("p (k n) -> p k n", k=KD), ACT.Copy).then_inc(xT_done, 1)

                def split(pair, i, done):
                    act.wait_ge(w_in[i], pair * 32 + 32)
                    act.wait_ge(y_ps_done, done * ST)
                    for parts, whole in ((w1_parts, w1), (w2_parts, w2)):
                        nc.scalar.activation(parts[i][0][:, :, :], whole[i][:, :, :], ACT.Copy).then_inc(w_first_done, 1)

                def at_expert(pair, i, q):
                    apart(act, biases_in[i], pair * 32 + 32, S["started"])
                    split_ahead(act, split, pair, i, q)

                def body(pair, i, t, q):
                    for n in range(NF // 2):
                        act.wait_ge(h_ps_done, q * (NF // 2) + (n + 1))
                        for f in (2 * n, 2 * n + 1):
                            for to in (h_full, h_parts[0]):
                                last = nc.scalar.activation(to[:, f, :], h_ps[n][:, (f % 2) * TOK:(f % 2 + 1) * TOK], ACT.Relu, bias=b1[i][:, f:f + 1])
                        last.then_inc(h_done, 1)
                    take_x(q + 1)

                take_x(0)
                split(0, 0, 0)
                each_turn(act, "f_act_turn", body, at_expert)

            @block.vector
            def _(dve):
                dve.wait_ge(set_up, 1)

                def front(q):
                    dve.wait_ge(rows_in, q * 16 + 16)
                    dve.wait_ge(x_ps_done, q)
                    for s in range(ST):
                        r = slot_of(rows, q, s)
                        nc.vector.tensor_scalar(xf[:, s, :], r[:, 0:D], r[:, D:D + 1], r[:, D + 1:D + 2], ALU.subtract, ALU.mult).then_inc(xf_done, 1)

                def body(pair, i, t, q):
                    for n in range(NF // 2):
                        if n == NF // 4:
                            front(q + 1)
                        dve.wait_ge(h_done, q * (NF // 2) + (n + 1))
                        bank = slice(2 * n, 2 * n + 2)
                        nc.vector.tensor_tensor(h_parts[1][:, bank, :], h_full[:, bank, :], h_parts[0][:, bank, :], ALU.subtract).then_inc(h_rest_done, 1)
                    rest_of_x(q + 1)
                    mine = half(rows, q)
                    for s in range(ST):
                        dve.wait_ge(sent[s], q * 16)
                    nc.vector.tensor_scalar(none[:, 0, :], mine[:, :, D + 3], 0.0, FAR, ALU.is_equal, ALU.mult).then_inc(token_done, 1)
                    dve.wait_ge(token_done, q * 2 + 1)
                    nc.vector.scalar_tensor_tensor(out=token[:, :], in0=mine[:, :, D + 3], scalar=-1.0, in1=none[:, 0, :], op0=ALU.add, op1=ALU.add).then_inc(token_done, 1)
                    dve.wait_ge(res_done, q + RING)
                    for s in range(ST):
                        dve.wait_ge(y_ps_done, q * ST + (s + 1))
                        nc.vector.tensor_tensor(y[:, s, :], y_ps[s][:, 0:D], b2[i][:, :], ALU.add).then_inc(y_step, 1)
                    for s in range(ST):
                        dve.wait_ge(y_step, q * STEPS + (STEPS + s + 1))
                        nc.vector.tensor_scalar(y[:, s, :], y[:, s, :], slot_of(rows, q, s)[:, D + 2:D + 3], None, ALU.mult).then_inc(y_step, 1)
                    dve.wait_ge(y_step, q * STEPS + (STEPS + 2 * ST))
                    nc.vector.tensor_scalar(odd[:, 0, :, :], y[:, :, :], FMAX, None, ALU.is_gt).then_inc(y_step, 1)
                    nc.vector.tensor_scalar(odd[:, 1, :, :], y[:, :, :], -FMAX, None, ALU.is_lt).then_inc(y_step, 1)
                    nc.vector.tensor_tensor(odd[:, 2, :, :], y[:, :, :], y[:, :, :], ALU.not_equal).then_inc(y_step, 1)
                    for n in range(3):
                        apart(dve, y_step, q * STEPS + (STEPS + 2 * ST + 3 + n), S["started"])
                        nc.vector.copy_predicated(y[:, :, :], odd[:, n, :, :], fill[:, n, :, :]).then_inc(y_step, 1)

                def rest_of_x(q):
                    dve.wait_ge(xT_done, q + 1)
                    nc.vector.tensor_tensor(x_parts[1][:, :, :], x_ps[:, 0:KD * TOK].rearrange("p (k n) -> p k n", k=KD), x_parts[0][:, :, :], ALU.subtract).then_inc(x_rest_done, 1)

                def split(pair, i, done):
                    for n, (parts, whole) in enumerate(((w1_parts, w1), (w2_parts, w2))):
                        dve.wait_ge(w_first_done, pair * 4 + (2 * i + n + 1))
                        nc.vector.tensor_tensor(parts[i][1][:, :, :], whole[i][:, :, :], parts[i][0][:, :, :], ALU.subtract).then_inc(w_rest_done, 1)

                front(0)
                rest_of_x(0)
                split(0, 0, 0)

                def at_expert(pair, i, q):
                    apart(dve, biases_in[i], pair * 32 + 32, S["started"])
                    split_ahead(dve, split, pair, i, q)

                each_turn(dve, "f_dve_turn", body, at_expert)


def lay_out(inputs):
    import numpy as np

    edges, nodes = len(inputs["src"]), len(inputs["x"])
    blocks = -(-edges // BLK)

    def by_partition(a, fill):
        padded = np.full(blocks * BLK, fill, a.dtype)
        padded[0:edges] = a
        return np.ascontiguousarray(padded.reshape(blocks * CH, 128).T)

    def columns(a):
        return np.ascontiguousarray(a.reshape(a.shape[0], -1, 128).transpose(2, 0, 1))

    a = {
        "x": inputs["x"],
        "src": by_partition(inputs["src"], 0),
        "dst": by_partition(inputs["dst"], nodes),
        "edge_weight": by_partition(inputs["edge_weight"], 0.0),
        "w_first": np.concatenate([inputs["L0_gnn_W_self"], inputs["L0_gnn_W_neigh"]], axis=1),
        "w_second": np.concatenate([inputs["L1_gnn_W_rel"].T, inputs["L1_gnn_W_root"].T], axis=1),
        "gamma": columns(inputs["L1_gnn_gamma"][None])[:, 0],
        "beta": columns(inputs["L1_gnn_beta"][None])[:, 0],
        "expert_b1_columns": columns(inputs["L1_ffn_b1"]),
    }
    for name in ("L0_ffn_Wr", "L0_ffn_br", "L0_ffn_W1", "L0_ffn_W2", "L0_ffn_Wo", "L0_ffn_bo", "L1_gnn_b_rel",
                 "L1_ffn_gate_w", "L1_ffn_gate_b", "L1_ffn_w1", "L1_ffn_w2", "L1_ffn_b2"):
        a[name] = inputs[name]
    for n in "12":
        for name in ("g", "v"):
            a[f"{name}{n}_rows"] = inputs[f"L0_ffn_{name}{n}"]
        for name in ("b", "g", "be", "m", "v"):
            a[f"{name}{n}_columns"] = columns(inputs[f"L0_ffn_{name}{n}"])
    return a


def kernel(**inputs):
    import numpy as np
    import concourse.bacc as bacc
    from concourse.bass_utils import run_bass_kernel_spmd

    inputs = {k: np.asarray(v) for k, v in inputs.items()}
    nodes, edges = inputs["x"].shape[0], inputs["src"].shape[0]
    nc = bacc.Bacc("TRN2", target_bir_lowering=False, num_devices=1)
    arrays, args = {}, {}
    for name, a in lay_out(inputs).items():
        a = np.ascontiguousarray(a)
        arrays[f"in_{name}"] = a
        args[name] = nc.dram_tensor(f"in_{name}", a.shape, mybir.dt.from_np(a.dtype), kind="ExternalInput").ap()
    out = nc.dram_tensor("out", (nodes, D), F32, kind="ExternalOutput").ap()
    build(nc, args, out, nodes, edges)
    return run_bass_kernel_spmd(nc, [arrays], core_ids=[0]).results[0]["out"]
```
